# Optimizing a Trainium2 kernel written in Bass

```python
import numpy as np
import jax
import jax.numpy as jnp

def _softmax(x, axis=-1):
    return jax.nn.softmax(x, axis=axis)

def _gelu(x):
    return jax.nn.gelu(x, approximate=True)

def _silu(x):
    return jax.nn.silu(x)

def _sigmoid(x):
    return jax.nn.sigmoid(x)

def _layernorm(x, axis=-1, eps=1e-05):
    m = jnp.mean(x, axis=axis, keepdims=True)
    v = jnp.var(x, axis=axis, keepdims=True)
    return (x - m) / jnp.sqrt(v + eps)

def _scatter_add(tgt, idx, src, axis=0):
    return tgt.at[idx].add(src)

def _segment_sum(src, seg, n):
    return jax.ops.segment_sum(src, seg, n)
kernel_name = 'mk_gnn_preln_d4_gnn_r64_40427c'

def setup_inputs(seed: int=0):
    np.random.seed(seed)
    _w = jnp.asarray

    def _rec_inputs():
        import jax
        import jax.numpy as jnp
        _gk = jax.random.key(seed)
        x = -0.0003713 + 1 * jax.random.normal(jax.random.fold_in(_gk, 1), (50000, 128), jnp.float32)
        src = jax.random.randint(jax.random.fold_in(_gk, 2), (12500,), 0, 50000, jnp.int32)
        dst = jax.random.randint(jax.random.fold_in(_gk, 3), (12500,), 0, 50000, jnp.int32)
        _o = jnp.argsort(dst, stable=True)
        src = src[_o]
        dst = dst[_o]
        edge_type_4 = jax.random.randint(jax.random.fold_in(_gk, 13), (12500,), 0, 4, jnp.int32)
        return (x, src, dst, edge_type_4)
    x, src, dst, edge_type_4 = _rec_inputs()

    def _L0_gnn_setup():
        import jax, jax.numpy as jnp
        import numpy as np
        N_NODES = 100000
        N_EDGES = 10000
        D_IN = 128
        D_OUT = 128

        def _edge_norm(edge_index, n_nodes, dtype):
            src, dst = (edge_index[0], edge_index[1])
            w = (src != dst).astype(dtype)
            deg = jax.ops.segment_sum(w, src, num_segments=n_nodes)
            dis = jnp.where(deg > 0, jax.lax.rsqrt(jnp.maximum(deg, 1.0)), 0.0)
            return (src, dst, dis[src] * dis[dst] * w)

        def _cheb_conv(x, src, dst, norm, W0, W1, b):
            msg = norm[:, None] * x[src]
            Tx1 = -jax.ops.segment_sum(msg, dst, num_segments=x.shape[0])
            return x @ W0 + Tx1 @ W1 + b
        key = jax.random.key(seed)
        ks = jax.random.split(key, 8)
        s_in = 1.0 / np.sqrt(D_IN)
        s_out = 1.0 / np.sqrt(D_OUT)
        return {'x': jax.random.normal(ks[0], (N_NODES, D_IN), jnp.float32), 'edge_index': jax.random.randint(ks[1], (2, N_EDGES), 0, N_NODES, jnp.int64), 'W1_0': jax.random.normal(ks[2], (D_IN, D_OUT), jnp.float32) * s_in, 'W1_1': jax.random.normal(ks[3], (D_IN, D_OUT), jnp.float32) * s_in, 'b1': jnp.zeros((D_OUT,), jnp.float32), 'W2_0': jax.random.normal(ks[4], (D_OUT, D_OUT), jnp.float32) * s_out, 'W2_1': jax.random.normal(ks[5], (D_OUT, D_OUT), jnp.float32) * s_out, 'b2': jnp.zeros((D_OUT,), jnp.float32)}
    _L0_gnn_all = _L0_gnn_setup()
    _L0_gnn_in = {k: v for k, v in _L0_gnn_all.items() if k in ('W1_0', 'W1_1', 'b1', 'W2_0', 'W2_1', 'b2')}
    del _L0_gnn_all

    def _L1_gnn_setup():
        import jax, jax.numpy as jnp
        import numpy as np
        N_NODES = 50000
        N_EDGES = 9375
        DIM_H = 128
        LN_EPS = 1e-05

        def _layer_norm(x, gamma, beta):
            mu = jnp.mean(x, axis=-1, keepdims=True)
            var = jnp.mean(jnp.square(x - mu), axis=-1, keepdims=True)
            return gamma * (x - mu) * jax.lax.rsqrt(var + LN_EPS) + beta
        key = jax.random.key(seed)
        ks = jax.random.split(key, 8)
        s = 1.0 / np.sqrt(DIM_H)
        return {'nodes': jax.random.normal(ks[0], (N_NODES, DIM_H), jnp.float32), 'W_msg': jax.random.normal(ks[1], (DIM_H, DIM_H), jnp.float32) * s, 'b_msg': jnp.zeros((DIM_H,), jnp.float32), 'w_ih': jax.random.normal(ks[2], (3 * DIM_H, DIM_H), jnp.float32) * s, 'w_hh': jax.random.normal(ks[3], (3 * DIM_H, DIM_H), jnp.float32) * s, 'b_ih': jnp.zeros((3 * DIM_H,), jnp.float32), 'b_hh': jnp.zeros((3 * DIM_H,), jnp.float32), 'ln_gamma': jnp.ones((DIM_H,), jnp.float32), 'ln_beta': jnp.zeros((DIM_H,), jnp.float32), 'edge_src': jax.random.randint(ks[4], (N_EDGES,), 0, N_NODES, jnp.int32), 'edge_dst': jax.random.randint(ks[5], (N_EDGES,), 0, N_NODES, jnp.int32)}
    _L1_gnn_all = _L1_gnn_setup()
    _L1_gnn_in = {k: v for k, v in _L1_gnn_all.items() if k in ('W_msg', 'b_msg', 'w_ih', 'w_hh', 'b_ih', 'b_hh', 'ln_gamma', 'ln_beta')}
    del _L1_gnn_all

    def _L2_gnn_setup():
        import jax, jax.numpy as jnp
        import numpy as np
        IN_FEAT = 128
        OUT_FEAT = 128
        NUM_RELS = 4
        N_NODES = 50000
        N_EDGES = 12500
        key = jax.random.key(seed)
        ks = jax.random.split(key, 8)
        feat = jax.random.normal(ks[0], (N_NODES, IN_FEAT), dtype=jnp.float32)
        src = jax.random.randint(ks[1], (N_EDGES,), 0, N_NODES)
        dst = jax.random.randint(ks[2], (N_EDGES,), 0, N_NODES)
        etypes = jax.random.randint(ks[3], (N_EDGES,), 0, NUM_RELS)
        W_rel = jax.random.normal(ks[4], (NUM_RELS, IN_FEAT, OUT_FEAT), dtype=jnp.float32) / np.sqrt(IN_FEAT)
        film_rel = jax.random.normal(ks[5], (NUM_RELS, IN_FEAT, 2 * OUT_FEAT), dtype=jnp.float32) / np.sqrt(IN_FEAT)
        h_bias = jnp.zeros((OUT_FEAT,), dtype=jnp.float32)
        gain = np.sqrt(2.0)
        bound = gain * np.sqrt(6.0 / (IN_FEAT + OUT_FEAT))
        loop_w = jax.random.uniform(ks[6], (IN_FEAT, OUT_FEAT), dtype=jnp.float32, minval=-bound, maxval=bound)
        return {'feat': feat, 'src': src, 'dst': dst, 'etypes': etypes, 'W_rel': W_rel, 'film_rel': film_rel, 'h_bias': h_bias, 'loop_w': loop_w}
    _L2_gnn_all = _L2_gnn_setup()
    _L2_gnn_in = {k: v for k, v in _L2_gnn_all.items() if k in ('W_rel', 'film_rel', 'h_bias', 'loop_w')}
    del _L2_gnn_all

    def _L3_gnn_setup():
        import jax, jax.numpy as jnp
        import numpy as np
        NUM_NODES = 100000
        NUM_EDGES = 25000
        IN_DIM = 128
        OUT_DIM = 128
        key = jax.random.key(seed)
        k_x, k_e, k_wn, k_bn, k_ws, k_bs = jax.random.split(key, 6)
        x = jax.random.normal(k_x, (NUM_NODES, IN_DIM), dtype=jnp.float32)
        edge_index = jax.random.randint(k_e, (2, NUM_EDGES), 0, NUM_NODES, dtype=jnp.int64)
        s = 1.0 / np.sqrt(IN_DIM)
        W_neigh = jax.random.uniform(k_wn, (OUT_DIM, IN_DIM), dtype=jnp.float32, minval=-s, maxval=s)
        b_neigh = jax.random.uniform(k_bn, (OUT_DIM,), dtype=jnp.float32, minval=-s, maxval=s)
        W_self = jax.random.uniform(k_ws, (OUT_DIM, IN_DIM), dtype=jnp.float32, minval=-s, maxval=s)
        b_self = jax.random.uniform(k_bs, (OUT_DIM,), dtype=jnp.float32, minval=-s, maxval=s)
        return {'x': x, 'edge_index': edge_index, 'W_neigh': W_neigh, 'b_neigh': b_neigh, 'W_self': W_self, 'b_self': b_self}
    _L3_gnn_all = _L3_gnn_setup()
    _L3_gnn_in = {k: v for k, v in _L3_gnn_all.items() if k in ('W_neigh', 'b_neigh', 'W_self', 'b_self')}
    del _L3_gnn_all
    return {'x': x, 'src': src, 'dst': dst, 'edge_type_4': edge_type_4, 'L0_gnn_W1_0': _L0_gnn_in['W1_0'], 'L0_gnn_W1_1': _L0_gnn_in['W1_1'], 'L0_gnn_b1': _L0_gnn_in['b1'], 'L0_gnn_W2_0': _L0_gnn_in['W2_0'], 'L0_gnn_W2_1': _L0_gnn_in['W2_1'], 'L0_gnn_b2': _L0_gnn_in['b2'], 'L1_gnn_W_msg': _L1_gnn_in['W_msg'], 'L1_gnn_b_msg': _L1_gnn_in['b_msg'], 'L1_gnn_w_ih': _L1_gnn_in['w_ih'], 'L1_gnn_w_hh': _L1_gnn_in['w_hh'], 'L1_gnn_b_ih': _L1_gnn_in['b_ih'], 'L1_gnn_b_hh': _L1_gnn_in['b_hh'], 'L1_gnn_ln_gamma': _L1_gnn_in['ln_gamma'], 'L1_gnn_ln_beta': _L1_gnn_in['ln_beta'], 'L2_gnn_W_rel': _L2_gnn_in['W_rel'], 'L2_gnn_film_rel': _L2_gnn_in['film_rel'], 'L2_gnn_h_bias': _L2_gnn_in['h_bias'], 'L2_gnn_loop_w': _L2_gnn_in['loop_w'], 'L3_gnn_W_neigh': _L3_gnn_in['W_neigh'], 'L3_gnn_b_neigh': _L3_gnn_in['b_neigh'], 'L3_gnn_W_self': _L3_gnn_in['W_self'], 'L3_gnn_b_self': _L3_gnn_in['b_self']}

def reference(x, src, dst, edge_type_4, L0_gnn_W1_0, L0_gnn_W1_1, L0_gnn_b1, L0_gnn_W2_0, L0_gnn_W2_1, L0_gnn_b2, L1_gnn_W_msg, L1_gnn_b_msg, L1_gnn_w_ih, L1_gnn_w_hh, L1_gnn_b_ih, L1_gnn_b_hh, L1_gnn_ln_gamma, L1_gnn_ln_beta, L2_gnn_W_rel, L2_gnn_film_rel, L2_gnn_h_bias, L2_gnn_loop_w, L3_gnn_W_neigh, L3_gnn_b_neigh, L3_gnn_W_self, L3_gnn_b_self):
    import jax
    import jax.numpy as jnp

    def _L0_gnn_ref(x, edge_index, W1_0, W1_1, b1, W2_0, W2_1, b2):
        import jax, jax.numpy as jnp
        import numpy as np
        N_NODES = 100000
        N_EDGES = 10000
        D_IN = 128
        D_OUT = 128

        def _edge_norm(edge_index, n_nodes, dtype):
            src, dst = (edge_index[0], edge_index[1])
            w = (src != dst).astype(dtype)
            deg = jax.ops.segment_sum(w, src, num_segments=n_nodes)
            dis = jnp.where(deg > 0, jax.lax.rsqrt(jnp.maximum(deg, 1.0)), 0.0)
            return (src, dst, dis[src] * dis[dst] * w)

        def _cheb_conv(x, src, dst, norm, W0, W1, b):
            msg = norm[:, None] * x[src]
            Tx1 = -jax.ops.segment_sum(msg, dst, num_segments=x.shape[0])
            return x @ W0 + Tx1 @ W1 + b
        src, dst, norm = _edge_norm(edge_index, x.shape[0], x.dtype)
        h = jax.nn.relu(_cheb_conv(x, src, dst, norm, W1_0, W1_1, b1))
        return jax.nn.relu(_cheb_conv(h, src, dst, norm, W2_0, W2_1, b2))

    def _L1_gnn_ref(nodes, W_msg, b_msg, w_ih, w_hh, b_ih, b_hh, ln_gamma, ln_beta, edge_src, edge_dst):
        import jax, jax.numpy as jnp
        import numpy as np
        N_NODES = 50000
        N_EDGES = 9375
        DIM_H = 128
        LN_EPS = 1e-05

        def _layer_norm(x, gamma, beta):
            mu = jnp.mean(x, axis=-1, keepdims=True)
            var = jnp.mean(jnp.square(x - mu), axis=-1, keepdims=True)
            return gamma * (x - mu) * jax.lax.rsqrt(var + LN_EPS) + beta
        n_nodes = nodes.shape[0]
        msg_e = nodes[edge_src] @ W_msg.T + b_msg
        messages = jax.ops.segment_sum(msg_e, edge_dst, num_segments=n_nodes)
        msg = messages + jnp.mean(nodes, axis=0)
        gi = msg @ w_ih.T + b_ih
        gh = nodes @ w_hh.T + b_hh
        i_r, i_z, i_n = jnp.split(gi, 3, axis=-1)
        h_r, h_z, h_n = jnp.split(gh, 3, axis=-1)
        r = jax.nn.sigmoid(i_r + h_r)
        z = jax.nn.sigmoid(i_z + h_z)
        n = jnp.tanh(i_n + r * h_n)
        h_next = (1.0 - z) * n + z * nodes
        out = _layer_norm(h_next, ln_gamma, ln_beta)
        out = out + messages
        return out

    def _L2_gnn_ref(feat, src, dst, etypes, W_rel, film_rel, h_bias, loop_w):
        import jax, jax.numpy as jnp
        import numpy as np
        IN_FEAT = 128
        OUT_FEAT = 128
        NUM_RELS = 4
        N_NODES = 50000
        N_EDGES = 12500
        N = feat.shape[0]
        out_feat = W_rel.shape[-1]
        hW = jnp.einsum('nd,rdo->rno', feat, W_rel)
        hF = jnp.einsum('nd,rdo->rno', feat, film_rel)
        m = hW[etypes, src]
        fw = hF[etypes, dst]
        gamma = fw[:, :out_feat]
        beta = fw[:, out_feat:]
        m = jax.nn.relu(gamma * m + beta)
        h = jax.ops.segment_sum(m, dst, num_segments=N)
        h = h + h_bias
        h = h + feat @ loop_w
        return h

    def _L3_gnn_ref(x, edge_index, W_neigh, b_neigh, W_self, b_self):
        import jax, jax.numpy as jnp
        import numpy as np
        NUM_NODES = 100000
        NUM_EDGES = 25000
        IN_DIM = 128
        OUT_DIM = 128
        src, dst = (edge_index[0], edge_index[1])
        msgs = x[src]
        neigh = jax.ops.segment_sum(msgs, dst, num_segments=x.shape[0])
        neigh_proj = neigh @ W_neigh.T + b_neigh
        self_proj = x @ W_self.T + b_self
        return neigh_proj + self_proj
    edge_index = jnp.stack([src, dst])
    h = jnp.maximum(_layernorm(x, axis=-1), 0.0)
    x = x + _L0_gnn_ref(h, edge_index, L0_gnn_W1_0, L0_gnn_W1_1, L0_gnn_b1, L0_gnn_W2_0, L0_gnn_W2_1, L0_gnn_b2)
    h = jnp.maximum(_layernorm(x, axis=-1), 0.0)
    x = x + _L1_gnn_ref(h, L1_gnn_W_msg, L1_gnn_b_msg, L1_gnn_w_ih, L1_gnn_w_hh, L1_gnn_b_ih, L1_gnn_b_hh, L1_gnn_ln_gamma, L1_gnn_ln_beta, src, dst)
    h = jnp.maximum(_layernorm(x, axis=-1), 0.0)
    x = x + _L2_gnn_ref(h, src, dst, edge_type_4, L2_gnn_W_rel, L2_gnn_film_rel, L2_gnn_h_bias, L2_gnn_loop_w)
    h = jnp.maximum(_layernorm(x, axis=-1), 0.0)
    x = x + _L3_gnn_ref(h, edge_index, L3_gnn_W_neigh, L3_gnn_b_neigh, L3_gnn_W_self, L3_gnn_b_self)
    return x

_drawn_inputs = setup_inputs


def setup_inputs(seed=0):
    import zlib

    import numpy as np

    out = dict(_drawn_inputs(seed))
    spreads = {'L0_gnn_b1': (0.0, 0.1),
     'L0_gnn_b2': (0.0, 0.1),
     'L1_gnn_b_msg': (0.0, 0.1),
     'L1_gnn_b_ih': (0.0, 0.1),
     'L1_gnn_b_hh': (0.0, 0.1),
     'L1_gnn_ln_gamma': (1.0, 0.2),
     'L1_gnn_ln_beta': (0.0, 0.1),
     'L2_gnn_h_bias': (0.0, 0.1)}
    factors = {}
    for name, (base, spread) in spreads.items():
        noise = np.random.default_rng([zlib.crc32(name.encode()), seed]).standard_normal(out[name].shape)
        drawn = base * np.exp(spread * noise) if base else spread * noise
        out[name] = jnp.asarray(drawn.astype(out[name].dtype))
    for name, factor in factors.items():
        out[name] = (out[name] * factor).astype(out[name].dtype)
    return out
```

```python
from contextlib import ExitStack

import concourse.bass as bass
from concourse import mybir

F32 = mybir.dt.float32
F16 = mybir.dt.float16
BF16 = mybir.dt.bfloat16
I32 = mybir.dt.int32
ALU = mybir.AluOpType
ACT = mybir.ActivationFunctionType

P = 128
TPB = 4
BLK = P * TPB
LN_EPS = 1e-5
FAR = 1 << 22
NREL = 4


def cdiv(a, b):
    return -(-a // b)


def pipeline(eng, count, steps, depth):
    most = max(lag for lag, _ in steps)
    assert most <= depth

    def position(i):
        for lag, fn in steps:
            b = i - lag
            if 0 <= b < count:
                fn(b, b % depth, b // depth)

    peeled = 2 * depth
    end = (count - 1) // depth * depth
    if end <= peeled:
        for i in range(count + most):
            position(i)
        return
    for i in range(peeled):
        position(i)
    with eng.Fori(peeled // depth, end // depth) as n:
        for k in range(depth):
            for lag, fn in steps:
                fn(n * depth + (k - lag), (k - lag) % depth, n + (k - lag) // depth)
    for i in range(end, count + most):
        position(i)


def reused(b, slots):
    return not isinstance(b, int) or b >= slots


class Bench:

    def __init__(self, nc, name):
        self.nc, self.name, self.ctx, self.used = nc, name, ExitStack(), []

    def __enter__(self):
        self.ctx.__enter__()
        return self

    def __exit__(self, *a):
        self.ctx.__exit__(*a)
        self.nc.clear_and_free_semaphores(self.used)
        self.nc.all_engine_barrier()

    def sb(self, name, shape, dt=F32):
        return self.ctx.enter_context(self.nc.sbuf_tensor(f"{self.name}_{name}", shape, dt))

    def ps(self, name, shape=(P, BLK), dt=F32):
        return self.ctx.enter_context(self.nc.psum_tensor(f"{self.name}_{name}", list(shape), dt))

    def sem(self, name):
        self.used.append(self.nc.alloc_semaphore(f"{self.name}_{name}"))
        return self.used[-1]

    def sems(self, name, n):
        return [self.sem(f"{name}{i}") for i in range(n)]

    def settle(self, eng):
        eng.sem_inc(self.settled, 1)

    def block(self):
        self.settled = self.sem("settled")
        return self.ctx.enter_context(self.nc.Block())


def flat(ap):
    return ap.rearrange("p t d -> p (t d)")


def tiles(ap):
    return ap.rearrange("p (t d) -> p t d", t=TPB)


def over_tiles(row):
    return row.unsqueeze(1).to_broadcast([P, TPB, P])


def block_rows(table, b, slots, tail=None):
    rows = table[bass.ds(b * BLK, BLK), :] if tail is None else table[bass.ds(b * BLK, tail * TPB), :]
    return rows.rearrange("(t p) d -> p t d", t=TPB) if slots else rows.rearrange("(p t) d -> p t d", t=TPB)


class Norm:

    def __init__(self, w, name, depth):
        self.stats = w.sb(f"{name}_stats", [P, depth, TPB, 6])
        self.sums = w.sb(f"{name}_sums", [P, depth, TPB, 3])
        self.diff = w.sb(f"{name}_diff", [P, depth, TPB])
        self.diff2 = w.sb(f"{name}_diff2", [P, depth, TPB])
        self.vare = w.sb(f"{name}_vare", [P, depth, TPB])
        self.mean = w.sb(f"{name}_mean", [P, depth, TPB])
        self.var = w.sb(f"{name}_var", [P, depth, TPB])
        self.rstd = w.sb(f"{name}_rstd", [P, depth, TPB])
        self.link = w.sem(f"{name}_link")
        self.var_ready = w.sem(f"{name}_var_ready")
        self.rstd_ready = w.sem(f"{name}_rstd_ready")

    def statistics(self, nc, dve, x, b, u):
        for t in range(TPB):
            last = nc.vector.bn_stats(self.stats[:, u, t], x[:, t])
        last.then_inc(self.link, 1)
        dve.wait_ge(self.link, b * 3 + 1)
        nc.vector.tensor_tensor(self.sums[:, u], self.stats[:, u, :, 0:3], self.stats[:, u, :, 3:6], ALU.add)
        nc.vector.tensor_tensor(self.diff[:, u], self.stats[:, u, :, 1], self.stats[:, u, :, 4],
                                ALU.subtract).then_inc(self.link, 1)
        dve.wait_ge(self.link, b * 3 + 2)
        nc.vector.scalar_tensor_tensor(self.diff2[:, u], self.diff[:, u], 0.25, self.diff[:, u], ALU.mult, ALU.mult)
        nc.vector.tensor_scalar(self.mean[:, u], self.sums[:, u, :, 1], 0.5, None, ALU.mult)
        nc.vector.tensor_scalar(self.vare[:, u], self.sums[:, u, :, 2], 1.0 / P, LN_EPS, ALU.mult,
                                ALU.add).then_inc(self.link, 1)
        dve.wait_ge(self.link, b * 3 + 3)
        nc.vector.tensor_tensor(self.var[:, u], self.vare[:, u], self.diff2[:, u], ALU.add).then_inc(self.var_ready, 1)

    def inverse(self, nc, pool, minus_half, b, u):
        pool.wait_ge(self.var_ready, b + 1)
        nc.gpsimd.tensor_tensor(self.rstd[:, u], self.var[:, u], minus_half[:, :], ALU.pow).then_inc(self.rstd_ready, 1)

    def apply(self, nc, dve, out, x, b, u):
        dve.wait_ge(self.rstd_ready, b + 1)
        for t in range(TPB):
            last = nc.vector.tensor_scalar(out[:, t], x[:, t], self.mean[:, u, t:t + 1], self.rstd[:, u, t:t + 1],
                                           ALU.subtract, ALU.mult)
        return last


class Fetch:

    def __init__(self, w, name, depth, table, column, limit):
        self.index = w.sb(f"{name}_index", [P, depth, TPB], I32)
        self.copied = w.sem(f"{name}_copied")
        self.bench = w
        self.done = w.sems(f"{name}_done", depth)
        self.table, self.column, self.limit = table, column, limit

    def issue(self, nc, pool, out, b, u, r):
        w = self.bench
        if reused(b, self.index.shape[1]):
            pool.wait_ge(self.done[u], 64 * r)
            w.settle(pool)
        nc.gpsimd.tensor_copy(self.index[:, u], self.column[:, bass.ds(b * TPB, TPB)]).then_inc(self.copied, 1)
        pool.wait_ge(self.copied, b + 1)
        w.settle(pool)
        for t in range(TPB):
            nc.gpsimd.indirect_dma_start(
                out=out[:, t], out_offset=None, in_=self.table,
                in_offset=bass.IndirectOffsetOnAxis(ap=self.index[:, u, t:t + 1], axis=0),
                bounds_check=self.limit - 1, oob_is_err=False).then_inc(self.done[u], 16)

    def arrived(self, eng, u, r):
        eng.wait_ge(self.done[u], 64 * (r + 1))


def row_stage(nc, name, c, blocks, slots, source, out, *, gather=None, mend=None, keep=None, norm=True, extra=None,
              sums=None, update=None, message=None, message_scale=None, message_bias=None, message_out=None,
              bias=None, relu=False, tail_in=None, tail_out=None, scatter=None):
    D = 4
    residual = extra is not None or (norm and not relu)
    with Bench(nc, name) as w:
        x = w.sb("x", [P, D, TPB, P])
        xr = w.sb("xr", [P, D, TPB, P]) if extra is not None else x
        hn = w.sb("hn", [P, D, TPB, P]) if norm else x
        hT = w.sb("hT", [P, D, BLK])
        tmp = w.sb("tmp", [P, D, TPB, P])
        y = w.sb("y", [P, D, TPB, P])
        msg = w.sb("msg", [P, D, TPB, P])
        window = w.sb("window", [P, D, TPB + 2, P]) if sums is not None else None
        same = w.sb("same", [P, D, TPB, 3, P]) if sums is not None else None
        p_t = [w.ps(f"p_t{i}") for i in range(2)]
        p_y = [w.ps(f"p_y{i}") for i in range(2)]
        p_m = [w.ps(f"p_m{i}") for i in range(2)]
        ln = Norm(w, "ln", D) if norm else None
        fetch = None
        if gather is not None:
            fetch = Fetch(w, "gather", D, source, gather, source.shape[0])
        if mend is not None:
            fetch = Fetch(w, "mend", D, mend[0], mend[1], mend[0].shape[0])
        loads = (gather is None) + (extra is not None) + 2 * (sums is not None)
        loaded = w.sems("loaded", D)
        norm_ready = w.sem("norm_ready")
        hT_read = w.sem("hT_ready")
        turned = w.sem("turned")
        multiplied = w.sem("multiplied")
        linked = w.sem("linked")
        y_ready = w.sem("y_ready")
        msg_ready = w.sem("msg_ready")
        y_stored = w.sems("y_stored", D)
        msg_stored = w.sems("msg_stored", D)
        kept = w.sems("kept", D)
        scat = w.sem("scat")
        si = w.sb("si", [P, D, TPB], I32)
        blk = w.block()
        both = 2 if message_scale is None and message_bias is None else 1

        engines = {}

        def input_ready(eng, u, r):
            if loads:
                eng.wait_ge(loaded[u], 16 * loads * (r + 1))
                if eng is engines.get("sync"):
                    w.settle(eng)
            if fetch is not None:
                fetch.arrived(eng, u, r)

        def slot_free(eng, b, u, r):
            if reused(b, D):
                if update is not None:
                    eng.wait_ge(y_ready, b - D + 1)
                    if eng is engines.get("sync"):
                        w.settle(eng)
                if message is not None:
                    eng.wait_ge(msg_ready, b - D + 1)
                    if eng is engines.get("sync"):
                        w.settle(eng)
                if keep is not None:
                    eng.wait_ge(kept[u], 16 * r)

        @blk.sync
        def _(sp):
            engines["sync"] = sp

            def load(b, u, r):
                if loads:
                    slot_free(sp, b, u, r)
                    w.settle(sp)
                if gather is None:
                    if tail_in is not None and isinstance(b, int) and b == blocks - 1:
                        sp.dma_start(x[0:tail_in, u], block_rows(source, b, slots, tail_in)).then_inc(loaded[u], 16)
                    else:
                        sp.dma_start(x[:, u], block_rows(source, b, slots)).then_inc(loaded[u], 16)
                if extra is not None:
                    if tail_in is not None and isinstance(b, int) and b == blocks - 1:
                        sp.dma_start(xr[0:tail_in, u], block_rows(extra, b, slots, tail_in)).then_inc(loaded[u], 16)
                    else:
                        sp.dma_start(xr[:, u], block_rows(extra, b, slots)).then_inc(loaded[u], 16)
                if sums is not None:
                    sp.dma_start(window[:, u], sums[bass.ds(b * BLK, BLK + 2 * P), :].rearrange(
                        "(t p) d -> p t d", p=P)).then_inc(loaded[u], 16)
                    sp.dma_start(same[:, u].rearrange("p t w e -> p t (w e)"),
                                 c.same_dram[bass.ds(b * BLK, BLK), :].rearrange(
                                     "(t p) d -> p t d", p=P)).then_inc(loaded[u], 16)

            def store(b, u, r):
                if update is not None and scatter is None:
                    sp.wait_ge(y_ready, b + 1)
                    w.settle(sp)
                    if tail_out is not None and isinstance(b, int) and b == blocks - 1:
                        sp.dma_start(block_rows(out, b, slots, tail_out), y[0:tail_out, u]).then_inc(y_stored[u], 16)
                    else:
                        sp.dma_start(block_rows(out, b, slots), y[:, u]).then_inc(y_stored[u], 16)
                if message is not None:
                    sp.wait_ge(msg_ready, b + 1)
                    w.settle(sp)
                    sp.dma_start(block_rows(message_out[P:, :], b, True), msg[:, u]).then_inc(msg_stored[u], 16)
                if keep is not None:
                    input_ready(sp, u, r)
                    w.settle(sp)
                    sp.dma_start(block_rows(keep, b, True), x[:, u]).then_inc(kept[u], 16)

            pipeline(nc.sync, blocks, [(0, load), (3, store)], D)
            for u in range(D):
                n = cdiv(blocks - u, D)
                if update is not None and scatter is None:
                    sp.wait_ge(y_stored[u], 16 * n)
                    w.settle(sp)
                if message is not None:
                    sp.wait_ge(msg_stored[u], 16 * n)
                    w.settle(sp)
                if keep is not None:
                    sp.wait_ge(kept[u], 16 * n)
                    w.settle(sp)

        @blk.gpsimd
        def _(pool):
            def bring(b, u, r):
                if gather is not None:
                    slot_free(pool, b, u, r)
                else:
                    pool.wait_ge(loaded[u], 16 * loads * (r + 1))
                fetch.issue(nc, pool, x[:, u], b, u, r)

            def inverse(b, u, r):
                ln.inverse(nc, pool, c.minus_half, b, u)

            def spread(b, u, r):
                if reused(b, D):
                    pool.wait_ge(y_stored[u], 64 * r)
                    w.settle(pool)
                nc.gpsimd.tensor_copy(si[:, u], scatter[:, bass.ds(b * TPB, TPB)]).then_inc(scat, 1)
                pool.wait_ge(scat, b + 1)
                w.settle(pool)
                pool.wait_ge(y_ready, b + 1)
                w.settle(pool)
                for t in range(TPB):
                    nc.gpsimd.indirect_dma_start(
                        out=out, out_offset=bass.IndirectOffsetOnAxis(ap=si[:, u, t:t + 1], axis=0),
                        in_=y[:, u, t], in_offset=None, bounds_check=out.shape[0] - 1,
                        oob_is_err=False).then_inc(y_stored[u], 16)

            steps = []
            if fetch is not None:
                steps.append((0, bring))
            if norm:
                steps.append((1 if fetch is not None else 0, inverse))
            if scatter is not None:
                steps.append((3, spread))
            if steps:
                pipeline(nc.gpsimd, blocks, steps, D)
            if scatter is not None:
                for u in range(D):
                    pool.wait_ge(y_stored[u], 64 * cdiv(blocks - u, D))

        ahead = 1 if fetch is not None else 0

        @blk.vector
        def _(dve):
            def statistics(b, u, r):
                input_ready(dve, u, r)
                ln.statistics(nc, dve, x[:, u], b, u)

            def apply(b, u, r):
                ln.apply(nc, dve, hn[:, u], x[:, u], b, u).then_inc(norm_ready, 1)

            def finish(b, u, r):
                dve.wait_ge(multiplied, b + 1)
                if update is not None:
                    if reused(b, D):
                        dve.wait_ge(y_stored[u], (64 if scatter is not None else 16) * r)
                    if relu:
                        nc.vector.tensor_tensor(tmp[:, u], tiles(p_y[u % 2][:, :]), over_tiles(bias), ALU.add).then_inc(linked, 1)
                    else:
                        nc.vector.tensor_tensor(tmp[:, u], tiles(p_y[u % 2][:, :]), xr[:, u], ALU.add).then_inc(linked, 1)
                    dve.wait_ge(linked, b + 1)
                    if relu and residual:
                        op = nc.vector.scalar_tensor_tensor(flat(y[:, u]), flat(tmp[:, u]), 0.0, flat(xr[:, u]), ALU.max, ALU.add)
                    elif relu:
                        op = nc.vector.tensor_scalar(flat(y[:, u]), flat(tmp[:, u]), 0.0, None, ALU.max)
                    else:
                        op = nc.vector.tensor_tensor(y[:, u], tmp[:, u], over_tiles(bias), ALU.add)
                    op.then_inc(y_ready, 1)
                if message is not None and message_bias is not None:
                    if reused(b, D):
                        dve.wait_ge(msg_stored[u], 16 * r)
                    nc.vector.tensor_tensor(msg[:, u], tiles(p_m[u % 2][:, :]), over_tiles(message_bias), ALU.add).then_inc(msg_ready, 1)

            if norm:
                pipeline(nc.vector, blocks, [(ahead, statistics), (ahead + 2, finish), (ahead + 1, apply)], D)
            else:
                pipeline(nc.vector, blocks, [(ahead + 2, finish)], D)

        @blk.tensor
        def _(pe):
            def turn(b, u, r):
                if norm:
                    pe.wait_ge(norm_ready, b + 1)
                else:
                    input_ready(pe, u, r)
                for t in range(TPB):
                    last = nc.tensor.transpose(p_t[u % 2][:, t * P:(t + 1) * P], hn[:, u, t], c.ident[:, :])
                last.then_inc(turned, 1)

            def multiply(b, u, r):
                pe.wait_ge(hT_read, b + 1)
                if reused(b, 2):
                    if update is not None:
                        pe.wait_ge(y_ready, b - 1)
                    if message is not None:
                        pe.wait_ge(msg_ready, b - 1)
                if sums is not None:
                    pe.wait_ge(loaded[u], 16 * loads * (r + 1))
                for t in range(TPB):
                    left = hT[:, u, t * P:(t + 1) * P]
                    if update is not None:
                        to = p_y[u % 2][:, t * P:(t + 1) * P]
                        if sums is not None:
                            for v in range(3):
                                nc.tensor.matmul(to, same[:, u, t, v], window[:, u, t + v], start=(v == 0), stop=False)
                        last = nc.tensor.matmul(to, left, update, start=(sums is None), stop=True)
                    if message is not None:
                        last = nc.tensor.matmul(p_m[u % 2][:, t * P:(t + 1) * P], left, message, start=True, stop=True)
                last.then_inc(multiplied, 1)

            pipeline(nc.tensor, blocks, [(ahead + 1, turn), (ahead + 1, multiply)], D)

        @blk.scalar
        def _(act):
            def lift(b, u, r):
                act.wait_ge(turned, b + 1)
                nc.scalar.activation(hT[:, u], p_t[u % 2][:, :], ACT.Relu if norm else ACT.Copy).then_inc(hT_read, 1)

            def send(b, u, r):
                act.wait_ge(multiplied, b + 1)
                if reused(b, D):
                    act.wait_ge(msg_stored[u], 16 * r)
                if message_scale is not None:
                    for t in range(TPB):
                        last = nc.scalar.activation(msg[:, u, t], p_m[u % 2][:, t * P:(t + 1) * P], ACT.Copy,
                                                    scale=message_scale[:, bass.ds(b * TPB + t, 1)])
                else:
                    last = nc.scalar.activation(flat(msg[:, u]), p_m[u % 2][:, :], ACT.Copy)
                last.then_inc(msg_ready, 1)

            steps = [(ahead + 1, lift)]
            if message is not None and message_bias is None:
                steps.append((ahead + 2, send))
            pipeline(nc.scalar, blocks, steps, D)


def mean_stage(nc, name, c, blocks, slots, source, weight, total):
    D = 4
    with Bench(nc, name) as w:
        x = w.sb("x", [P, D, TPB, P])
        hn = w.sb("hn", [P, D, TPB, P])
        h = w.sb("h", [P, D, TPB, P])
        wt = w.sb("wt", [P, D, TPB])
        acc = w.ps("acc")
        ln = Norm(w, "ln", D)
        loaded = w.sems("loaded", D)
        norm_ready = w.sem("norm_ready")
        h_ready = w.sem("h_ready")
        w_ready = w.sem("w_ready")
        multiplied = w.sem("multiplied")
        blk = w.block()

        @blk.sync
        def _(sp):
            def load(b, u, r):
                if reused(b, D):
                    sp.wait_ge(norm_ready, b - D + 1)
                    w.settle(sp)
                sp.dma_start(x[:, u], block_rows(source, b, slots)).then_inc(loaded[u], 16)
            pipeline(nc.sync, blocks, [(0, load)], D)

        @blk.gpsimd
        def _(pool):
            def inverse(b, u, r):
                ln.inverse(nc, pool, c.minus_half, b, u)
            pipeline(nc.gpsimd, blocks, [(0, inverse)], D)

        @blk.vector
        def _(dve):
            def statistics(b, u, r):
                dve.wait_ge(loaded[u], 16 * (r + 1))
                ln.statistics(nc, dve, x[:, u], b, u)

            def apply(b, u, r):
                if reused(b, D):
                    dve.wait_ge(h_ready, b - D + 1)
                ln.apply(nc, dve, hn[:, u], x[:, u], b, u).then_inc(norm_ready, 1)
                if reused(b, D):
                    dve.wait_ge(multiplied, b - D + 1)
                nc.vector.tensor_scalar(wt[:, u], weight[:, bass.ds(b * TPB, TPB)], 1.0, None, ALU.mult).then_inc(w_ready, 1)
            pipeline(nc.vector, blocks, [(0, statistics), (1, apply)], D)

        @blk.scalar
        def _(act):
            def rectify(b, u, r):
                act.wait_ge(norm_ready, b + 1)
                if reused(b, D):
                    act.wait_ge(multiplied, b - D + 1)
                nc.scalar.activation(flat(h[:, u]), flat(hn[:, u]), ACT.Relu).then_inc(h_ready, 1)
            pipeline(nc.scalar, blocks, [(1, rectify)], D)
            act.wait_ge(multiplied, blocks)
            nc.scalar.activation(total, acc[:, 0:1], ACT.Copy)

        @blk.tensor
        def _(pe):
            def add(b, u, r):
                pe.wait_ge(h_ready, b + 1)
                pe.wait_ge(w_ready, b + 1)
                for t in range(TPB):
                    first = isinstance(b, int) and b == 0 and t == 0
                    end = isinstance(b, int) and b == blocks - 1 and t == TPB - 1
                    last = nc.tensor.matmul(acc[:, 0:1], h[:, u, t], wt[:, u, t:t + 1], start=first, stop=end)
                last.then_inc(multiplied, 1)
            pipeline(nc.tensor, blocks, [(1, add)], D)


def gru_stage(nc, name, c, blocks, slots, source, out, *, mend=None, sums=None, message=None, message_out=None):
    D, H = 6, 3
    with Bench(nc, name) as w:
        x = w.sb("x", [P, D, TPB, P])
        xb = w.sb("xb", [P, D, TPB, P])
        hn = w.sb("hn", [P, H, TPB, P])
        hT = w.sb("hT", [P, H, BLK])
        rT = w.sb("rT", [P, 2, BLK])
        zT = w.sb("zT", [P, 2, BLK])
        uT = w.sb("uT", [P, 2, BLK])
        nT = w.sb("nT", [P, 2, BLK])
        dT = w.sb("dT", [P, 2, BLK])
        eT = w.sb("eT", [P, 2, BLK])
        sT = w.sb("sT", [P, 2, BLK])
        shift = w.sb("shift", [P, D, TPB])
        yn = w.sb("yn", [P, 2, TPB, P])
        yg = w.sb("yg", [P, 2, TPB, P])
        y = w.sb("y", [P, 2, TPB, P])
        if message is not None:
            msg = w.sb("msg", [P, H, TPB, P])
            p_m = w.ps("p_m")
        if sums is not None:
            window = w.sb("window", [P, H, TPB + 2, P])
            same = w.sb("same", [P, H, TPB, 3, P])
            tT = w.sb("tT", [P, 2, BLK])
            tR = w.sb("tR", [P, H, BLK])
            vT = w.sb("vT", [P, 2, BLK])
            yt = w.sb("yt", [P, 2, TPB, P])
            p_s = w.ps("p_s")
            p_q = w.ps("p_q")
            p_i = w.ps("p_i")
        p_t = w.ps("p_t")
        p_r, p_z, p_n = w.ps("p_r"), w.ps("p_z"), w.ps("p_n")
        p_y = w.ps("p_y")
        ln, ln2 = Norm(w, "ln", D), Norm(w, "ln2", D)
        fetch = Fetch(w, "mend", D, mend[0], mend[1], mend[0].shape[0]) if mend is not None else None
        loads = 1
        loaded = w.sems("loaded", D)
        loaded_sums = w.sems("loaded_sums", H)
        names = ("norm_ready", "turned", "hT_ready", "gates", "sig", "u_ready", "n_ready", "d_ready", "e_ready", "s_ready",
                 "back", "shift_ready", "yn_ready", "yg_ready", "y_ready", "xb_ready", "summed", "tT_ready", "tR_ready",
                 "msg_mult", "msg_ready", "v_ready", "yt_ready", "stats2")
        s = {n: w.sem(n) for n in names}
        stored = w.sems("stored", 2)
        msg_stored = w.sems("msg_stored", H)
        blk = w.block()
        ahead = 1 if fetch is not None else 0

        def input_ready(eng, u, r):
            eng.wait_ge(loaded[u], 16 * (r + 1))
            if fetch is not None:
                fetch.arrived(eng, u, r)

        def uses(b, u, slots):
            return b // slots if isinstance(b, int) else None

        @blk.sync
        def _(sp):
            def load(b, u, r):
                if reused(b, D):
                    sp.wait_ge(s["xb_ready"], b - D + 1)
                    w.settle(sp)
                sp.dma_start(x[:, u], block_rows(source, b, slots)).then_inc(loaded[u], 16)

            def load_sums(b, u, r):
                if reused(b, H):
                    sp.wait_ge(s["summed"], b - H + 1)
                    w.settle(sp)
                sp.dma_start(window[:, u % H], sums[bass.ds(b * BLK, BLK + 2 * P), :].rearrange(
                    "(t p) d -> p t d", p=P)).then_inc(loaded_sums[u % H], 16)
                sp.dma_start(same[:, u % H].rearrange("p t w e -> p t (w e)"),
                             c.same_dram[bass.ds(b * BLK, BLK), :].rearrange(
                                 "(t p) d -> p t d", p=P)).then_inc(loaded_sums[u % H], 16)

            def store(b, u, r):
                sp.wait_ge(s["y_ready"], b + 1)
                w.settle(sp)
                sp.dma_start(block_rows(out, b, slots), y[:, u % 2]).then_inc(stored[u % 2], 16)

            def store_msg(b, u, r):
                sp.wait_ge(s["msg_ready"], b + 1)
                w.settle(sp)
                sp.dma_start(block_rows(message_out[P:, :], b, True), msg[:, u % H]).then_inc(msg_stored[u % H], 16)

            steps = [(0, load)]
            if sums is not None:
                steps.append((1, load_sums))
            if message is not None:
                steps.append((4, store_msg))
            steps.append((5, store))
            pipeline(nc.sync, blocks, steps, D)
            for u in range(2):
                sp.wait_ge(stored[u], 16 * cdiv(blocks - u, 2))
                w.settle(sp)
            if message is not None:
                for u in range(H):
                    sp.wait_ge(msg_stored[u], 16 * cdiv(blocks - u, H))
                    w.settle(sp)

        @blk.gpsimd
        def _(pool):
            def bring(b, u, r):
                pool.wait_ge(loaded[u], 16 * (r + 1))
                fetch.issue(nc, pool, x[:, u], b, u, r)

            def inverse(b, u, r):
                ln.inverse(nc, pool, c.minus_half, b, u)

            def with_beta(b, u, r):
                if reused(b, D):
                    pool.wait_ge(s["y_ready"], b - D + 1)
                pool.wait_ge(s["norm_ready"], b + 1)
                nc.gpsimd.tensor_tensor(xb[:, u], x[:, u], over_tiles(c.beta), ALU.add).then_inc(s["xb_ready"], 1)

            def inverse2(b, u, r):
                ln2.inverse(nc, pool, c.minus_half, b, u)

            steps = [(0, bring)] if fetch is not None else []
            steps += [(ahead, inverse), (ahead + 1, with_beta), (ahead + 3, inverse2)]
            pipeline(nc.gpsimd, blocks, steps, D)

        @blk.vector
        def _(dve):
            def statistics(b, u, r):
                input_ready(dve, u, r)
                ln.statistics(nc, dve, x[:, u], b, u)

            def apply(b, u, r):
                if reused(b, H):
                    dve.wait_ge(s["turned"], b - H + 1)
                ln.apply(nc, dve, hn[:, u % H], x[:, u], b, u).then_inc(s["norm_ready"], 1)

            def step(b, u, r):
                v, k = u % 2, u % H
                dve.wait_ge(s["sig"], b + 1)
                if reused(b, 2):
                    dve.wait_ge(s["n_ready"], b - 1)
                nc.vector.scalar_tensor_tensor(uT[:, v], p_n[:, :], c.b_hn, rT[:, v], ALU.add, ALU.mult).then_inc(s["u_ready"], 1)
                if sums is not None:
                    dve.wait_ge(s["u_ready"], b + 1)
                    nc.vector.tensor_tensor(vT[:, v], p_i[:, :], uT[:, v], ALU.add).then_inc(s["v_ready"], 1)

            def blend(b, u, r):
                v, k = u % 2, u % H
                dve.wait_ge(s["n_ready"], b + 1)
                nc.vector.tensor_tensor(dT[:, v], hT[:, k], nT[:, v], ALU.subtract).then_inc(s["d_ready"], 1)
                dve.wait_ge(s["d_ready"], b + 1)
                nc.vector.tensor_tensor(eT[:, v], dT[:, v], zT[:, v], ALU.mult).then_inc(s["e_ready"], 1)
                dve.wait_ge(s["e_ready"], b + 1)
                if reused(b, 2):
                    dve.wait_ge(s["back"], b - 1)
                nc.vector.tensor_tensor(sT[:, v], eT[:, v], nT[:, v], ALU.add).then_inc(s["s_ready"], 1)

            def send(b, u, r):
                dve.wait_ge(s["msg_mult"], b + 1)
                if reused(b, H):
                    if isinstance(b, int):
                        dve.wait_ge(msg_stored[u % H], 16 * (b // H))
                    else:
                        dve.wait_ge(msg_stored[u % H], r * (16 * (D // H)) + 16 * (u // H))
                nc.vector.tensor_tensor(msg[:, u % H], tiles(p_m[:, :]), over_tiles(c.b_msg), ALU.add).then_inc(s["msg_ready"], 1)

            def statistics2(b, u, r):
                dve.wait_ge(s["back"], b + 1)
                ln2.statistics(nc, dve, tiles(p_y[:, :]), b, u)
                dve.wait_ge(ln2.rstd_ready, b + 1)
                nc.vector.scalar_tensor_tensor(shift[:, u], ln2.mean[:, u], -1.0, ln2.rstd[:, u], ALU.mult,
                                               ALU.mult).then_inc(s["shift_ready"], 1)

            def finish(b, u, r):
                v = u % 2
                dve.wait_ge(s["yn_ready"], b + 1)
                nc.vector.tensor_tensor(yg[:, v], yn[:, v], over_tiles(c.gamma), ALU.mult).then_inc(s["yg_ready"], 1)
                dve.wait_ge(s["yg_ready"], b + 1)
                left = yg
                if sums is not None:
                    dve.wait_ge(s["tR_ready"], b + 1)
                    nc.vector.tensor_tensor(yt[:, v], yg[:, v], tiles(tR[:, u % H]), ALU.add).then_inc(s["yt_ready"], 1)
                    dve.wait_ge(s["yt_ready"], b + 1)
                    left = yt
                dve.wait_ge(s["xb_ready"], b + 1)
                if reused(b, 2):
                    if isinstance(b, int):
                        dve.wait_ge(stored[v], 16 * (b // 2))
                    else:
                        dve.wait_ge(stored[v], r * (16 * (D // 2)) + 16 * (u // 2))
                nc.vector.tensor_tensor(y[:, v], left[:, v], xb[:, u], ALU.add).then_inc(s["y_ready"], 1)

            steps = [(ahead + 4, finish), (ahead, statistics), (ahead + 2, step), (ahead + 1, apply), (ahead + 2, blend),
                     (ahead + 3, statistics2)]
            if message is not None:
                steps.append((ahead + 2, send))
            pipeline(nc.vector, blocks, steps, D)

        @blk.tensor
        def _(pe):
            def turn(b, u, r):
                pe.wait_ge(s["norm_ready"], b + 1)
                for t in range(TPB):
                    last = nc.tensor.transpose(p_t[:, t * P:(t + 1) * P], hn[:, u % H, t], c.ident[:, :])
                last.then_inc(s["turned"], 1)

            def sum_up(b, u, r):
                k = u % H
                if isinstance(b, int):
                    pe.wait_ge(loaded_sums[k], 32 * (b // H + 1))
                else:
                    pe.wait_ge(loaded_sums[k], r * (32 * (D // H)) + 32 * (u // H + 1))
                if reused(b, 1):
                    pe.wait_ge(s["tR_ready"], b)
                for t in range(TPB):
                    for v in range(3):
                        nc.tensor.matmul(p_s[:, t * P:(t + 1) * P], window[:, k, t + v], same[:, k, t, v],
                                         start=(v == 0), stop=(v == 2))
                for t in range(TPB):
                    for v in range(3):
                        last = nc.tensor.matmul(p_q[:, t * P:(t + 1) * P], same[:, k, t, v], window[:, k, t + v],
                                                start=(v == 0), stop=(v == 2))
                last.then_inc(s["summed"], 1)

            def gates(b, u, r):
                k, v = u % H, u % 2
                pe.wait_ge(s["hT_ready"], b + 1)
                if sums is not None:
                    pe.wait_ge(s["tT_ready"], b + 1)
                if reused(b, 1):
                    pe.wait_ge(s["sig"], b)
                    pe.wait_ge(s["v_ready" if sums is not None else "u_ready"], b)
                for g, to in ((0, p_r), (1, p_z)):
                    last = nc.tensor.matmul(to[:, :], c.w_hh[:, g * P:(g + 1) * P], hT[:, k], start=True, stop=(sums is None))
                    if sums is not None:
                        nc.tensor.matmul(to[:, :], c.w_ih[:, g * P:(g + 1) * P], tT[:, v], start=False, stop=True)
                last = nc.tensor.matmul(p_n[:, :], c.w_hh[:, 2 * P:3 * P], hT[:, k], start=True, stop=True)
                if sums is not None:
                    last = nc.tensor.matmul(p_i[:, :], c.w_ih[:, 2 * P:3 * P], tT[:, v], start=True, stop=True)
                last.then_inc(s["gates"], 1)

            def messages(b, u, r):
                if reused(b, 1):
                    pe.wait_ge(s["msg_ready"], b)
                for t in range(TPB):
                    last = nc.tensor.matmul(p_m[:, t * P:(t + 1) * P], hT[:, u % H, t * P:(t + 1) * P], message,
                                            start=True, stop=True)
                last.then_inc(s["msg_mult"], 1)

            def back(b, u, r):
                pe.wait_ge(s["s_ready"], b + 1)
                if reused(b, 1):
                    pe.wait_ge(s["yn_ready"], b)
                for t in range(TPB):
                    last = nc.tensor.transpose(p_y[:, t * P:(t + 1) * P], sT[:, u % 2, t * P:(t + 1) * P], c.ident[:, :])
                last.then_inc(s["back"], 1)

            steps = [(ahead + 1, turn)]
            if sums is not None:
                steps.append((ahead + 1, sum_up))
            steps.append((ahead + 1, gates))
            if message is not None:
                steps.append((ahead + 1, messages))
            steps.append((ahead + 2, back))
            pipeline(nc.tensor, blocks, steps, D)

        @blk.scalar
        def _(act):
            def lift(b, u, r):
                act.wait_ge(s["turned"], b + 1)
                if reused(b, H):
                    act.wait_ge(s["d_ready"], b - H + 1)
                nc.scalar.activation(hT[:, u % H], p_t[:, :], ACT.Relu).then_inc(s["hT_ready"], 1)

            def lift_sums(b, u, r):
                act.wait_ge(s["summed"], b + 1)
                if reused(b, 2):
                    act.wait_ge(s["gates"], b - 1)
                nc.scalar.activation(tT[:, u % 2], p_s[:, :], ACT.Copy).then_inc(s["tT_ready"], 1)
                if reused(b, H):
                    act.wait_ge(s["yt_ready"], b - H + 1)
                nc.scalar.activation(tR[:, u % H], p_q[:, :], ACT.Copy).then_inc(s["tR_ready"], 1)

            def sigmoids(b, u, r):
                v = u % 2
                act.wait_ge(s["gates"], b + 1)
                if reused(b, 2):
                    act.wait_ge(s["u_ready"], b - 1)
                nc.scalar.activation(rT[:, v], p_r[:, :], ACT.Sigmoid, bias=c.b_r)
                if reused(b, 2):
                    act.wait_ge(s["e_ready"], b - 1)
                nc.scalar.activation(zT[:, v], p_z[:, :], ACT.Sigmoid, bias=c.b_z).then_inc(s["sig"], 1)

            def candidate(b, u, r):
                v = u % 2
                act.wait_ge(s["v_ready" if sums is not None else "u_ready"], b + 1)
                if reused(b, 2):
                    act.wait_ge(s["s_ready"], b - 1)
                nc.scalar.activation(nT[:, v], (vT if sums is not None else uT)[:, v], ACT.Tanh, bias=c.b_n).then_inc(s["n_ready"], 1)

            def scale(b, u, r):
                act.wait_ge(s["shift_ready"], b + 1)
                if reused(b, 2):
                    act.wait_ge(s["yg_ready"], b - 1)
                for t in range(TPB):
                    last = nc.scalar.activation(yn[:, u % 2, t], p_y[:, t * P:(t + 1) * P], ACT.Identity,
                                                bias=shift[:, u, t:t + 1], scale=ln2.rstd[:, u, t:t + 1])
                last.then_inc(s["yn_ready"], 1)

            steps = [(ahead + 2, sigmoids), (ahead + 1, lift)]
            if sums is not None:
                steps.append((ahead + 1, lift_sums))
            steps += [(ahead + 2, candidate), (ahead + 3, scale)]
            pipeline(nc.scalar, blocks, steps, D)


def film_stage(nc, name, c, blocks, sources, dests, message_out):
    D = 4
    with Bench(nc, name) as w:
        xs = w.sb("xs", [P, D, 2, TPB, P])
        hn = w.sb("hn", [P, 2, 2, TPB, P])
        hT = w.sb("hT", [P, 2, 2, BLK])
        rel = w.sb("rel", [P, D, BLK], I32)
        hm = w.sb("hm", [P, 2, NREL, BLK])
        ms = w.sb("ms", [P, 2, TPB, P])
        gm = w.sb("gm", [P, 2, TPB, P])
        gb = w.sb("gb", [P, 2, TPB, P])
        msg = w.sb("msg", [P, D, TPB, P])
        p_t = [w.ps(f"p_t{i}") for i in range(2)]
        p_m = w.ps("p_m")
        p_f = w.ps("p_f", (P, TPB * 2 * P))
        lns = [Norm(w, f"ln{k}", D) for k in range(2)]
        loaded = w.sems("loaded", D)
        norm_ready = w.sem("norm_ready")
        turned = w.sem("turned")
        hT_ready = w.sem("hT_ready")
        masked = w.sem("masked")
        multiplied = w.sem("multiplied")
        ms_ready = w.sem("ms_ready")
        gm_ready = w.sem("gm_ready")
        gb_ready = w.sem("gb_ready")
        msg_ready = w.sem("msg_ready")
        stored = w.sems("stored", D)
        blk = w.block()

        @blk.sync
        def _(sp):
            def load(b, u, r):
                if reused(b, D):
                    sp.wait_ge(masked, b * 2 - 2 * D + 2)
                    w.settle(sp)
                sp.dma_start(xs[:, u, 0], block_rows(sources, b, True)).then_inc(loaded[u], 16)
                sp.dma_start(xs[:, u, 1], block_rows(dests, b, True)).then_inc(loaded[u], 16)
                sp.dma_start(rel[:, u], c.relation_row[:, bass.ds(b * BLK, BLK)].to_broadcast([P, BLK])).then_inc(loaded[u], 16)

            def store(b, u, r):
                sp.wait_ge(msg_ready, b + 1)
                w.settle(sp)
                sp.dma_start(block_rows(message_out[P:, :], b, True), msg[:, u]).then_inc(stored[u], 16)
            pipeline(nc.sync, blocks, [(0, load), (3, store)], D)
            for u in range(D):
                sp.wait_ge(stored[u], 16 * cdiv(blocks - u, D))
                w.settle(sp)

        @blk.gpsimd
        def _(pool):
            def inverse(b, u, r):
                for k in range(2):
                    lns[k].inverse(nc, pool, c.minus_half, b, u)
            pipeline(nc.gpsimd, blocks, [(0, inverse)], D)

        @blk.vector
        def _(dve):
            def statistics(b, u, r):
                dve.wait_ge(loaded[u], 48 * (r + 1))
                for k in range(2):
                    lns[k].statistics(nc, dve, xs[:, u, k], b, u)

            def apply(b, u, r):
                if reused(b, 2):
                    dve.wait_ge(turned, b * 2 - 2)
                for k in range(2):
                    lns[k].apply(nc, dve, hn[:, u % 2, k], xs[:, u, k], b, u).then_inc(norm_ready, 1)

            def mask(b, u, r):
                for k in range(2):
                    dve.wait_ge(hT_ready, b * 2 + k + 1)
                    if reused(b, 1):
                        dve.wait_ge(multiplied, b * 2 + k - 1)
                    for q in range(NREL):
                        last = nc.vector.scalar_tensor_tensor(hm[:, k, q], rel[:, u], float(q), hT[:, u % 2, k],
                                                              ALU.is_equal, ALU.mult)
                    last.then_inc(masked, 1)

            def finish(b, u, r):
                f = p_f[:, :].rearrange("p (t k d) -> p t k d", t=TPB, k=2)
                v = u % 2
                dve.wait_ge(multiplied, b * 2 + 2)
                dve.wait_ge(ms_ready, b + 1)
                nc.vector.tensor_tensor(gm[:, v], f[:, :, 0], ms[:, v], ALU.mult).then_inc(gm_ready, 1)
                dve.wait_ge(gm_ready, b + 1)
                if reused(b, 2):
                    dve.wait_ge(msg_ready, b - 1)
                nc.vector.tensor_tensor(gb[:, v], f[:, :, 1], gm[:, v], ALU.add).then_inc(gb_ready, 1)
            pipeline(nc.vector, blocks, [(0, statistics), (1, apply), (2, mask), (2, finish)], D)

        @blk.tensor
        def _(pe):
            def turn(b, u, r):
                for k in range(2):
                    pe.wait_ge(norm_ready, b * 2 + k + 1)
                    if reused(b, 1):
                        pe.wait_ge(hT_ready, b * 2 + k - 1)
                    for t in range(TPB):
                        last = nc.tensor.transpose(p_t[k][:, t * P:(t + 1) * P], hn[:, u % 2, k, t], c.ident[:, :])
                    last.then_inc(turned, 1)

            def multiply(b, u, r):
                for k in range(2):
                    pe.wait_ge(masked, b * 2 + k + 1)
                    if reused(b, 1):
                        pe.wait_ge(ms_ready if k == 0 else gb_ready, b)
                    for t in range(TPB):
                        for q in range(NREL):
                            left = hm[:, k, q, t * P:(t + 1) * P]
                            if k == 0:
                                last = nc.tensor.matmul(p_m[:, t * P:(t + 1) * P], left, c.w_rel[:, q * P:(q + 1) * P],
                                                        start=(q == 0), stop=(q == NREL - 1))
                            else:
                                last = nc.tensor.matmul(p_f[:, t * 2 * P:(t + 1) * 2 * P], left,
                                                        c.w_film[:, q * 2 * P:(q + 1) * 2 * P],
                                                        start=(q == 0), stop=(q == NREL - 1))
                    last.then_inc(multiplied, 1)
            pipeline(nc.tensor, blocks, [(1, turn), (2, multiply)], D)

        @blk.scalar
        def _(act):
            def lift(b, u, r):
                for k in range(2):
                    act.wait_ge(turned, b * 2 + k + 1)
                    if reused(b, 2):
                        act.wait_ge(masked, b * 2 - 4 + k + 1)
                    nc.scalar.activation(hT[:, u % 2, k], p_t[k][:, :], ACT.Relu).then_inc(hT_ready, 1)

            def copy_m(b, u, r):
                act.wait_ge(multiplied, b * 2 + 1)
                if reused(b, 2):
                    act.wait_ge(gm_ready, b - 1)
                nc.scalar.activation(flat(ms[:, u % 2]), p_m[:, :], ACT.Copy).then_inc(ms_ready, 1)

            def rectify(b, u, r):
                act.wait_ge(gb_ready, b + 1)
                if reused(b, D):
                    act.wait_ge(stored[u], 16 * r)
                nc.scalar.activation(flat(msg[:, u]), flat(gb[:, u % 2]), ACT.Relu).then_inc(msg_ready, 1)
            pipeline(nc.scalar, blocks, [(1, lift), (2, copy_m), (2, rectify)], D)


class Common:
    pass


WEIGHTS = (("W1_0", P), ("W1_1", P), ("W2_0", P), ("W2_1", P), ("W_msg", P), ("w_ih", 3 * P), ("w_hh", 3 * P),
           ("w_rel", NREL * P), ("w_film", NREL * 2 * P), ("loop_w", P), ("W_neigh", P), ("W_self", P))
ROWS = ("b1", "b2", "b_msg", "gamma", "beta", "h_bias", "b_neigh", "b_self")


def constants_phase(nc, c, args):
    with Bench(nc, "const") as w:
        loaded, made, fixed = w.sem("loaded"), w.sem("made"), w.sem("fixed")
        zero = w.sb("zero", [P, P])
        blk = w.block()
        count = [0]

        @blk.sync
        def _(sp):
            for name, cols in WEIGHTS:
                sp.dma_start(c.weights[name][:, :], args[name]).then_inc(loaded, 16)
                count[0] += 1
            for name in ROWS:
                sp.dma_start(c.rows[name][:, :], args[name].rearrange("(a n) -> a n", a=1).to_broadcast([P, P])).then_inc(loaded, 16)
                count[0] += 1
            for col, at in ((c.g_ih, args["b_ih"]), (c.g_hh, args["b_hh"])):
                for g in range(3):
                    sp.dma_start(col[:, g:g + 1], at[g * P:(g + 1) * P].rearrange("(p a) -> p a", a=1)).then_inc(loaded, 16)
                    count[0] += 1
            sp.dma_start(c.src[:, :], args["src_columns"]).then_inc(loaded, 16)
            sp.dma_start(c.dst[:, 1:c.tiles + 1], args["dst_columns"]).then_inc(loaded, 16)
            count[0] += 2
            sp.wait_ge(made, 1)
            for at in (0, (c.tiles + 1) * P):
                sp.dma_start(c.msg[at:at + P, :], zero[:, :]).then_inc(loaded, 16)
                count[0] += 1
            sp.wait_ge(loaded, 16 * count[0])

        @blk.vector
        def _(dve):
            nc.vector.memset(zero[:, :], 0.0).then_inc(made, 1)
            nc.vector.memset(c.minus_half[:, :], -0.5)
            nc.vector.memset(c.minus_half_wide[:, :], -0.5)
            nc.vector.memset(c.dst[:, 0:1], -1)
            nc.vector.memset(c.dst[:, c.tiles + 1:c.tiles + 2], -1)

        @blk.gpsimd
        def _(pool):
            nc.gpsimd.memset(c.ident[:, :], 0.0).then_inc(fixed, 1)
            nc.gpsimd.memset(c.earlier[:, :], 1.0).then_inc(fixed, 1)
            pool.wait_ge(fixed, 2)
            nc.gpsimd.affine_select(out=c.ident[:, :], in_=c.ident[:, :], compare_op=ALU.not_equal, fill=1.0, base=0,
                                    pattern=[[-1, P]], channel_multiplier=1)
            nc.gpsimd.affine_select(out=c.earlier[:, P:], in_=c.earlier[:, P:], compare_op=ALU.is_gt, fill=0.0, base=0,
                                    pattern=[[-1, P]], channel_multiplier=1)
            nc.gpsimd.iota(c.count_row[:, :], [[1, BLK]], base=0, channel_multiplier=0, allow_small_or_imprecise_dtypes=True)
            nc.gpsimd.iota(c.node_of[:, :], [[1, BLK]], base=0, channel_multiplier=BLK)
            nc.gpsimd.iota(c.slot_of[:, :], [[P, c.tiles]], base=0, channel_multiplier=1)


def degree_phase(nc, c):
    D, T = 4, c.tiles
    with Bench(nc, "deg") as w:
        part_i = w.sb("part_i", [P, 4, T], I32)
        part = w.sb("part", [P, 4, T])
        hot_hi = w.sb("hot_hi", [P, D, 2, P], BF16)
        hot_lo = w.sb("hot_lo", [P, D, 2, BLK], BF16)
        deg = w.sb("deg", [P, 2, BLK])
        least = w.sb("least", [P, 2, BLK])
        most = w.sb("most", [P, 2, BLK])
        power = w.sb("power", [P, BLK])
        valid = w.sb("valid", [P, BLK])
        weight = w.sb("weight", [P, BLK])
        row = w.sb("row", [P, BLK, 4])
        p_deg = [w.ps(f"p_deg{k}") for k in range(2)]
        split, hot, added, linked, powered, stored = (w.sem(n) for n in ("split", "hot", "added", "linked", "powered", "stored"))
        blk = w.block()

        @blk.vector
        def _(dve):
            for k, col in enumerate((c.src[:, :], c.dst[:, 1:T + 1])):
                nc.vector.tensor_scalar(part_i[:, 2 * k], col, 9, None, ALU.arith_shift_right)
                nc.vector.tensor_scalar(part_i[:, 2 * k + 1], col, BLK - 1, None, ALU.bitwise_and).then_inc(split, 1)
            nc.vector.tensor_tensor(c.apart[:, :], c.src[:, :], c.dst[:, 1:T + 1], ALU.not_equal)
            nc.vector.tensor_scalar(c.src_row[:, :], c.src[:, :], c.nodes - 1, None, ALU.min)
            nc.vector.tensor_scalar(c.dst_row[:, :], c.dst[:, 1:T + 1], c.nodes - 1, None, ALU.min)
            nc.vector.tensor_scalar(c.real[:, :], c.dst[:, 1:T + 1], c.nodes, None, ALU.is_lt)
            dve.wait_ge(split, 2)
            nc.vector.tensor_copy(part[:, :, :], part_i[:, :, :]).then_inc(split, 1)
            dve.wait_ge(split, 3)

            def one_hot(b, u, r):
                if reused(b, D):
                    dve.wait_ge(added, b - D + 1)
                at = bass.ds(b, 1)
                nc.vector.tensor_scalar(hot_hi[:, u, 0], c.count_row[:, 0:P], part[:, 0, at], c.apart[:, at], ALU.is_equal, ALU.mult)
                nc.vector.tensor_scalar(hot_lo[:, u, 0], c.count_row[:, :], part[:, 1, at], None, ALU.is_equal)
                nc.vector.tensor_scalar(hot_hi[:, u, 1], c.count_row[:, 0:P], part[:, 2, at], None, ALU.is_equal)
                nc.vector.tensor_scalar(hot_lo[:, u, 1], c.count_row[:, :], part[:, 3, at], None, ALU.is_equal).then_inc(hot, 1)
            pipeline(nc.vector, T, [(0, one_hot)], D)
            dve.wait_ge(added, T)
            for k in range(2):
                last = nc.vector.tensor_copy(deg[:, k], p_deg[k][:, :])
            last.then_inc(linked, 1)
            dve.wait_ge(linked, 1)
            nc.vector.tensor_scalar(least[:, :], deg[:, :], 1.0, None, ALU.max)
            nc.vector.tensor_scalar(most[:, :], deg[:, :], 1.0, None, ALU.min)
            nc.vector.tensor_scalar(valid[:, :], c.node_of[:, :], c.nodes, None, ALU.is_lt)
            nc.vector.memset(row[:, :, 3], 0.0)
            nc.vector.memset(row[:, :, 2].bitcast(I32), FAR).then_inc(linked, 1)
            dve.wait_ge(linked, 2)
            nc.vector.tensor_scalar(weight[:, :], most[:, 1], -1.0, 1.0, ALU.mult, ALU.add).then_inc(linked, 1)
            nc.vector.reciprocal(row[:, :, 1], least[:, 1])
            dve.wait_ge(powered, 1)
            nc.vector.tensor_tensor(row[:, :, 0], power[:, :], most[:, 0], ALU.mult).then_inc(linked, 1)
            dve.wait_ge(linked, 4)
            nc.vector.tensor_tensor(weight[:, :], weight[:, :], valid[:, :], ALU.mult).then_inc(linked, 1)

        @blk.gpsimd
        def _(pool):
            pool.wait_ge(linked, 2)
            nc.gpsimd.tensor_tensor(power[:, :], least[:, 0], c.minus_half_wide[:, :], ALU.pow).then_inc(powered, 1)

        @blk.tensor
        def _(pe):
            def add(b, u, r):
                pe.wait_ge(hot, b + 1)
                for k in range(2):
                    last = nc.tensor.matmul(p_deg[k][:, :], hot_hi[:, u, k], hot_lo[:, u, k],
                                            start=isinstance(b, int) and b == 0, stop=isinstance(b, int) and b == T - 1)
                last.then_inc(added, 1)
            pipeline(nc.tensor, T, [(0, add)], D)

        @blk.sync
        def _(sp):
            sp.wait_ge(linked, 4)
            sp.dma_start(c.table.rearrange("(p n) k -> p n k", p=P), row[:, :, :]).then_inc(stored, 16)
            sp.wait_ge(linked, 5)
            sp.dma_start(c.weight_dram.rearrange("(p n) -> p n", p=P), weight[:, :]).then_inc(stored, 16)
            sp.wait_ge(stored, 32)
            sp.dma_start(c.node_weight[:, :].rearrange("p (b t) -> p b t", t=TPB),
                         c.weight_dram[0:c.node_blocks * BLK].rearrange("(b p t) -> p b t", p=P, t=TPB)).then_inc(stored, 16)
            sp.wait_ge(stored, 48)


def same_phase(nc, c, dst_line):
    D = 4
    with Bench(nc, "same") as w:
        line = w.sb("line", [P, D, P + BLK], I32)
        same = w.sb("same", [P, D, TPB, 3, P])
        match = w.sb("match", [P, D, TPB, 2, P])
        seen = w.sb("seen", [P, D, TPB, 2, P])
        before = w.sb("before", [P, D, TPB])
        away = w.sb("away", [P, D, TPB])
        loaded = w.sems("loaded", D)
        made, linked, placed = w.sem("made"), w.sem("linked"), w.sem("placed")
        stored = w.sems("stored", D)
        col = w.sb("col", [P, c.tiles + 2])
        copied = w.sem("copied")
        blk = w.block()

        @blk.sync
        def _(sp):
            def load(b, u, r):
                if reused(b, D):
                    sp.wait_ge(made, b - D + 1)
                    w.settle(sp)
                sp.dma_start(line[:, u], dst_line[:, bass.ds(b * BLK, P + BLK)].to_broadcast([P, P + BLK])).then_inc(loaded[u], 16)

            def store(b, u, r):
                sp.wait_ge(made, b + 1)
                w.settle(sp)
                sp.dma_start(c.same_dram[bass.ds(b * BLK, BLK), :].rearrange("(t p) d -> p t d", p=P),
                             same[:, u].rearrange("p t w e -> p t (w e)")).then_inc(stored[u], 16)
            pipeline(nc.sync, c.edge_blocks, [(0, load), (2, store)], D)
            for u in range(D):
                sp.wait_ge(stored[u], 16 * cdiv(c.edge_blocks - u, D))
                w.settle(sp)

        @blk.vector
        def _(dve):
            nc.vector.tensor_copy(col[:, :], c.dst[:, :]).then_inc(copied, 1)
            dve.wait_ge(copied, 1)

            def compare(b, u, r):
                if reused(b, D):
                    dve.wait_ge(stored[u], 16 * r)
                dve.wait_ge(loaded[u], 16 * (r + 1))
                for t in range(TPB):
                    for v in range(3):
                        last = nc.vector.tensor_scalar(same[:, u, t, v], line[:, u, (t + 1) * P:(t + 2) * P],
                                                       col[:, bass.ds(b * TPB + t + v, 1)], None, ALU.is_equal)
                last.then_inc(made, 1)
                for t in range(TPB):
                    last = nc.vector.tensor_scalar(flat(match[:, u, t]), line[:, u, t * P:(t + 2) * P],
                                                   col[:, bass.ds(b * TPB + t + 1, 1)], None, ALU.is_equal)
                last.then_inc(linked, 1)
                dve.wait_ge(linked, b * 4 + 1)
                nc.vector.tensor_tensor(seen[:, u].rearrange("p t k e -> p t (k e)"),
                                        match[:, u].rearrange("p t k e -> p t (k e)"),
                                        c.earlier.unsqueeze(1).to_broadcast([P, TPB, 2 * P]), ALU.mult).then_inc(linked, 1)
                dve.wait_ge(linked, b * 4 + 2)
                nc.vector.tensor_reduce(before[:, u], seen[:, u].rearrange("p t k e -> p t (k e)"), mybir.AxisListType.X, ALU.max).then_inc(linked, 1)
                dve.wait_ge(linked, b * 4 + 3)
                nc.vector.tensor_scalar(away[:, u], before[:, u], float(FAR), None, ALU.mult).then_inc(linked, 1)
                dve.wait_ge(linked, b * 4 + 4)
                nc.vector.tensor_tensor(c.write_at[:, bass.ds(b * TPB, TPB)], away[:, u],
                                        col[:, bass.ds(b * TPB + 1, TPB)], ALU.add)
            pipeline(nc.vector, c.edge_blocks, [(0, compare)], D)


def look_up_phase(nc, name, c, column, out):
    D = 4
    with Bench(nc, name) as w:
        got = w.sb("got", [P, D, TPB, 4])
        fetch = Fetch(w, "fetch", D, c.table, column, c.table.shape[0])
        taken = w.sem("taken")
        blk = w.block()

        @blk.gpsimd
        def _(pool):
            def bring(b, u, r):
                if reused(b, D):
                    pool.wait_ge(taken, b - D + 1)
                fetch.issue(nc, pool, got[:, u], b, u, r)
            pipeline(nc.gpsimd, c.edge_blocks, [(0, bring)], D)

        @blk.vector
        def _(dve):
            def take(b, u, r):
                fetch.arrived(dve, u, r)
                dve.wait_ge(fetch.copied, b + 1)
                nc.vector.tensor_copy(out[:, bass.ds(b * TPB, TPB), :].bitcast(I32), got[:, u].bitcast(I32)).then_inc(taken, 1)
            pipeline(nc.vector, c.edge_blocks, [(1, take)], D)


def name_slots_phase(nc, c):
    D = 4
    with Bench(nc, "slots") as w:
        index = w.sb("index", [P, D, TPB], I32)
        row = w.sb("row", [P, D, TPB, 4])
        copied, filled = w.sem("copied"), w.sem("filled")
        done = w.sems("done", D)
        blk = w.block()

        @blk.vector
        def _(dve):
            nc.vector.tensor_copy(c.at_dst[:, :, 2].bitcast(I32), c.slot_of[:, :]).then_inc(filled, 1)

        @blk.gpsimd
        def _(pool):
            pool.wait_ge(filled, 1)

            def send(b, u, r):
                if reused(b, D):
                    pool.wait_ge(done[u], 64 * r)
                    w.settle(pool)
                nc.gpsimd.tensor_copy(index[:, u], c.write_at[:, bass.ds(b * TPB, TPB)]).then_inc(copied, 1)
                nc.gpsimd.tensor_copy(row[:, u].bitcast(I32), c.at_dst[:, bass.ds(b * TPB, TPB), :].bitcast(I32)).then_inc(copied, 1)
                pool.wait_ge(copied, b * 2 + 2)
                w.settle(pool)
                for t in range(TPB):
                    nc.gpsimd.indirect_dma_start(
                        out=c.table, out_offset=bass.IndirectOffsetOnAxis(ap=index[:, u, t:t + 1], axis=0),
                        in_=row[:, u, t], in_offset=None, bounds_check=c.table.shape[0] - 1,
                        oob_is_err=False).then_inc(done[u], 16)
            pipeline(nc.gpsimd, c.edge_blocks, [(0, send)], D)
            for u in range(D):
                pool.wait_ge(done[u], 64 * cdiv(c.edge_blocks - u, D))


def columns_phase(nc, c):
    with Bench(nc, "cols") as w:
        t = w.sb("t", [P, c.tiles])
        n = w.sb("n", [P, c.tiles])
        link = w.sem("link")
        blk = w.block()

        @blk.vector
        def _(dve):
            nc.vector.tensor_tensor(t[:, :], c.at_dst[:, :, 0], c.at_src[:, :, 0], ALU.mult).then_inc(link, 1)
            nc.vector.tensor_tensor(c.slot_weight[:, :], c.at_dst[:, :, 1], c.real[:, :], ALU.mult)
            nc.vector.tensor_copy(c.mend_at[:, :], c.at_src[:, :, 2].bitcast(I32))
            nc.vector.tensor_tensor(c.b_last[:, :], c.rows["b_neigh"][:, :], c.rows["b_self"][:, :], ALU.add)
            dve.wait_ge(link, 1)
            nc.vector.tensor_tensor(n[:, :], t[:, :], c.apart[:, :], ALU.mult).then_inc(link, 1)
            dve.wait_ge(link, 2)
            nc.vector.tensor_scalar(c.minus_norm[:, :], n[:, :], -1.0, None, ALU.mult)


def gate_bias_phase(nc, c):
    with Bench(nc, "gbias") as w:
        part = w.sb("part", [P, 1])
        mean = w.sb("mean", [P, 1])
        p_g = w.ps("p_g")
        link, multiplied = w.sem("link"), w.sem("multiplied")
        blk = w.block()

        @blk.vector
        def _(dve):
            nc.vector.tensor_tensor(part[:, :], c.total_nodes[:, :], c.total_slots[:, :], ALU.add).then_inc(link, 1)
            dve.wait_ge(link, 1)
            nc.vector.tensor_scalar(mean[:, :], part[:, :], 1.0 / c.nodes, None, ALU.mult).then_inc(link, 1)
            dve.wait_ge(multiplied, 1)
            nc.vector.tensor_tensor(c.g_sum[:, :], p_g[:, 0:3], c.g_ih[:, :], ALU.add).then_inc(link, 1)
            dve.wait_ge(link, 3)
            nc.vector.tensor_tensor(c.g_all[:, :], c.g_sum[:, :], c.g_hh[:, :], ALU.add)

        @blk.tensor
        def _(pe):
            pe.wait_ge(link, 2)
            for g in range(3):
                last = nc.tensor.matmul(p_g[:, g:g + 1], c.w_ih[:, g * P:(g + 1) * P], mean[:, :], start=True, stop=True)
            last.then_inc(multiplied, 1)


def build(nc, args, out):
    c = Common()
    x = args["x"]
    c.nodes = x.shape[0]
    c.tiles = args["src_columns"].shape[1]
    c.edge_blocks = c.tiles // TPB
    c.node_blocks = cdiv(c.nodes, BLK)
    slots = c.tiles * P
    tail = (c.nodes - (c.node_blocks - 1) * BLK) // TPB
    assert c.nodes % TPB == 0 and c.node_blocks <= P and c.nodes + slots <= P * BLK
    tail = None if tail == P else tail

    def dram(name, shape, dt=F32):
        return nc.dram_tensor(name, list(shape), dt, kind="Internal").ap()

    edge_rows, node_rows = [slots, P], [c.node_blocks * BLK, P]
    s_x0, s_h1, s_x1, s_x2, s_x3 = (dram(f"s_{n}", edge_rows) for n in ("x0", "h1", "x1", "x2", "x3"))
    d_x0, d_h1, d_x1, d_x2, d_x3 = (dram(f"d_{n}", edge_rows) for n in ("x0", "h1", "x1", "x2", "x3"))
    n_h1, n_x1, n_x2, n_x3 = (dram(f"n_{n}", node_rows) for n in ("h1", "x1", "x2", "x3"))
    s_x2m = dram("s_x2m", edge_rows)
    c.msg = dram("msg", [slots + 2 * P, P])
    c.same_dram = dram("same_dram", [slots, 3 * P])
    c.table = dram("table", [P * BLK, 4])
    c.weight_dram = dram("weight_dram", [P * BLK])
    c.relation_row = args["relation_line"]

    with ExitStack() as ctx:
        def sb(name, shape, dt=F32):
            return ctx.enter_context(nc.sbuf_tensor(name, shape, dt))

        T = c.tiles
        c.weights = {name: sb(f"w_{name}", [P, cols]) for name, cols in WEIGHTS}
        c.rows = {name: sb(f"r_{name}", [P, P]) for name in ROWS}
        c.w_ih, c.w_hh, c.w_rel, c.w_film = (c.weights[n] for n in ("w_ih", "w_hh", "w_rel", "w_film"))
        c.gamma, c.beta, c.b_msg = (c.rows[n][:, :] for n in ("gamma", "beta", "b_msg"))
        c.g_ih, c.g_hh, c.g_sum, c.g_all = (sb(n, [P, 3]) for n in ("g_ih", "g_hh", "g_sum", "g_all"))
        c.b_r, c.b_z, c.b_n, c.b_hn = c.g_all[:, 0:1], c.g_all[:, 1:2], c.g_sum[:, 2:3], c.g_hh[:, 2:3]
        c.b_last = sb("b_last", [P, P])
        c.ident, c.earlier_t = sb("ident", [P, P]), sb("earlier", [P, 2 * P])
        c.earlier = c.earlier_t[:, :]
        c.minus_half, c.minus_half_wide = sb("minus_half", [P, TPB]), sb("minus_half_wide", [P, BLK])
        c.count_row = sb("count_row", [P, BLK], F16)
        c.node_of = sb("node_of", [P, BLK], I32)
        c.slot_of, c.src = sb("slot_of", [P, T], I32), sb("src_t", [P, T], I32)
        c.dst = sb("dst_t", [P, T + 2], I32)
        c.src_row, c.dst_row, c.write_at, c.mend_at = (sb(n, [P, T], I32) for n in ("src_row", "dst_row", "write_at", "mend_at"))
        c.apart, c.real, c.minus_norm, c.slot_weight = (sb(n, [P, T]) for n in ("apart", "real", "minus_norm", "slot_weight"))
        c.at_dst, c.at_src = sb("at_dst", [P, T, 4]), sb("at_src", [P, T, 4])
        c.node_weight = sb("node_weight", [P, c.node_blocks * TPB])
        c.total_nodes, c.total_slots = sb("total_nodes", [P, 1]), sb("total_slots", [P, 1])
        W = {n: t[:, :] for n, t in c.weights.items()}
        R = {n: t[:, :] for n, t in c.rows.items()}
        dst_cols = c.dst[:, 1:T + 1]
        E, N = c.edge_blocks, c.node_blocks

        constants_phase(nc, c, args)
        degree_phase(nc, c)
        same_phase(nc, c, args["dst_line"])
        look_up_phase(nc, "atd", c, dst_cols, c.at_dst)
        name_slots_phase(nc, c)
        look_up_phase(nc, "ats", c, c.src, c.at_src)
        columns_phase(nc, c)

        row_stage(nc, "s0a", c, E, True, x, s_h1, gather=c.src_row, keep=s_x0, update=W["W1_0"], bias=R["b1"], relu=True,
                  message=W["W1_1"], message_scale=c.minus_norm, message_out=c.msg)
        row_stage(nc, "d0a", c, E, True, x, d_h1, gather=c.dst_row, keep=d_x0, update=W["W1_0"], bias=R["b1"], relu=True,
                  sums=c.msg)
        row_stage(nc, "n0a", c, N, False, x, n_h1, update=W["W1_0"], bias=R["b1"], relu=True, tail_in=tail)
        row_stage(nc, "s0b", c, E, True, s_h1, s_x1, mend=(d_h1, c.mend_at), norm=False, extra=s_x0, update=W["W2_0"],
                  bias=R["b2"], relu=True, message=W["W2_1"], message_scale=c.minus_norm, message_out=c.msg)
        row_stage(nc, "d0b", c, E, True, d_h1, d_x1, norm=False, extra=d_x0, update=W["W2_0"], bias=R["b2"], relu=True,
                  sums=c.msg)
        row_stage(nc, "n0b", c, N, False, n_h1, n_x1, norm=False, extra=x, update=W["W2_0"], bias=R["b2"], relu=True,
                  tail_in=tail)

        mean_stage(nc, "meann", c, N, False, n_x1, c.node_weight, c.total_nodes[:, :])
        mean_stage(nc, "meand", c, E, True, d_x1, c.slot_weight, c.total_slots[:, :])
        gate_bias_phase(nc, c)
        gru_stage(nc, "s1", c, E, True, s_x1, s_x2, mend=(d_x1, c.mend_at), message=W["W_msg"], message_out=c.msg)
        gru_stage(nc, "d1", c, E, True, d_x1, d_x2, sums=c.msg)
        gru_stage(nc, "n1", c, N, False, n_x1, n_x2)

        row_stage(nc, "s2", c, E, True, s_x2, s_x3, mend=(d_x2, c.mend_at), keep=s_x2m, update=W["loop_w"], bias=R["h_bias"])
        film_stage(nc, "f2", c, E, s_x2m, d_x2, c.msg)
        row_stage(nc, "d2", c, E, True, d_x2, d_x3, update=W["loop_w"], bias=R["h_bias"], sums=c.msg)
        row_stage(nc, "n2", c, N, False, n_x2, n_x3, update=W["loop_w"], bias=R["h_bias"])

        row_stage(nc, "s3", c, E, True, s_x3, None, mend=(d_x3, c.mend_at), message=W["W_neigh"], message_out=c.msg)
        row_stage(nc, "n3", c, N, False, n_x3, out, update=W["W_self"], bias=c.b_last[:, :], tail_out=tail)
        row_stage(nc, "d3", c, E, True, d_x3, out, update=W["W_self"], bias=c.b_last[:, :], sums=c.msg, scatter=c.write_at)


def kernel(**inputs):
    import numpy as np
    import concourse.bacc as bacc
    from concourse import mybir as mb
    from concourse.bass_utils import run_bass_kernel_spmd

    a = {k: np.ascontiguousarray(v) for k, v in inputs.items()}
    nodes, edges = a["x"].shape[0], a["src"].shape[0]
    pad = cdiv(edges, BLK) * BLK - edges
    spare = np.arange(nodes, nodes + pad, dtype=np.int32)
    src = np.concatenate([a["src"], spare])
    dst = np.concatenate([a["dst"], spare])
    rel = np.concatenate([a["edge_type_4"], np.zeros(pad, np.int32)])
    C = np.ascontiguousarray
    arrays = {
        "x": a["x"],
        "src_columns": C(src.reshape(-1, P).T), "dst_columns": C(dst.reshape(-1, P).T),
        "dst_line": C(np.concatenate([np.full(P, -1, np.int32), dst]).reshape(1, -1)), "relation_line": C(rel.reshape(1, -1)),
        "W1_0": a["L0_gnn_W1_0"], "W1_1": a["L0_gnn_W1_1"], "W2_0": a["L0_gnn_W2_0"], "W2_1": a["L0_gnn_W2_1"],
        "b1": a["L0_gnn_b1"], "b2": a["L0_gnn_b2"],
        "W_msg": C(a["L1_gnn_W_msg"].T), "w_ih": C(a["L1_gnn_w_ih"].T), "w_hh": C(a["L1_gnn_w_hh"].T),
        "b_msg": a["L1_gnn_b_msg"], "b_ih": a["L1_gnn_b_ih"], "b_hh": a["L1_gnn_b_hh"],
        "gamma": a["L1_gnn_ln_gamma"], "beta": a["L1_gnn_ln_beta"],
        "w_rel": C(a["L2_gnn_W_rel"].transpose(1, 0, 2).reshape(P, -1)),
        "w_film": C(a["L2_gnn_film_rel"].transpose(1, 0, 2).reshape(P, -1)),
        "h_bias": a["L2_gnn_h_bias"], "loop_w": a["L2_gnn_loop_w"],
        "W_neigh": C(a["L3_gnn_W_neigh"].T), "W_self": C(a["L3_gnn_W_self"].T),
        "b_neigh": a["L3_gnn_b_neigh"], "b_self": a["L3_gnn_b_self"],
    }
    nc = bacc.Bacc("TRN2", target_bir_lowering=False, num_devices=1)
    args = {k: nc.dram_tensor(f"in_{k}", v.shape, mb.dt.from_np(v.dtype), kind="ExternalInput").ap() for k, v in arrays.items()}
    out = nc.dram_tensor("out", (nodes, P), mb.dt.float32, kind="ExternalOutput").ap()
    build(nc, args, out)
    r = run_bass_kernel_spmd(nc, [{f"in_{k}": v for k, v in arrays.items()}], core_ids=[0])
    return r.results[0]["out"]
```

```python
from contextlib import ExitStack
from functools import partial

import concourse.bass as bass
from concourse import mybir

F32 = mybir.dt.float32
F16 = mybir.dt.float16
BF16 = mybir.dt.bfloat16
I32 = mybir.dt.int32
ALU = mybir.AluOpType
ACT = mybir.ActivationFunctionType

P = 128
TPB = 4
BLK = P * TPB
LN_EPS = 1e-5
FAR = 1 << 22
NREL = 4


def cdiv(a, b):
    return -(-a // b)


def pipeline(eng, count, steps, depth):
    most = max(lag for lag, _ in steps)
    assert most <= depth

    def position(i):
        for lag, fn in steps:
            b = i - lag
            if 0 <= b < count:
                fn(b, b % depth, b // depth)

    peeled = 2 * depth
    end = (count - 1) // depth * depth
    if end <= peeled:
        for i in range(count + most):
            position(i)
        return
    for i in range(peeled):
        position(i)
    with eng.Fori(peeled // depth, end // depth) as n:
        for k in range(depth):
            for lag, fn in steps:
                fn(n * depth + (k - lag), (k - lag) % depth, n + (k - lag) // depth)
    for i in range(end, count + most):
        position(i)


def reused(b, slots):
    return not isinstance(b, int) or b >= slots


class Bench:

    def __init__(self, nc, name):
        self.nc, self.name, self.ctx, self.used = nc, name, ExitStack(), []

    def __enter__(self):
        self.ctx.__enter__()
        return self

    def __exit__(self, *a):
        self.ctx.__exit__(*a)
        self.nc.clear_and_free_semaphores(self.used)
        self.nc.all_engine_barrier()

    def sb(self, name, shape, dt=F32):
        return self.ctx.enter_context(self.nc.sbuf_tensor(f"{self.name}_{name}", shape, dt))

    def ps(self, name, shape=(P, BLK), dt=F32):
        return self.ctx.enter_context(self.nc.psum_tensor(f"{self.name}_{name}", list(shape), dt))

    def sem(self, name):
        self.used.append(self.nc.alloc_semaphore(f"{self.name}_{name}"))
        return self.used[-1]

    def sems(self, name, n):
        return [self.sem(f"{name}{i}") for i in range(n)]

    def settle(self, eng):
        eng.sem_inc(self.settled, 1)

    def block(self):
        self.settled = self.sem("settled")
        return self.ctx.enter_context(self.nc.Block())


def flat(ap):
    return ap.rearrange("p t d -> p (t d)")


def tiles(ap):
    return ap.rearrange("p (t d) -> p t d", t=TPB)


def over_tiles(row):
    return row.unsqueeze(1).to_broadcast([P, TPB, P])


def block_rows(table, b, slots, tail=None):
    rows = table[bass.ds(b * BLK, BLK), :] if tail is None else table[bass.ds(b * BLK, tail * TPB), :]
    return rows.rearrange("(t p) d -> p t d", t=TPB) if slots else rows.rearrange("(p t) d -> p t d", t=TPB)


class Norm:

    def __init__(self, w, name, depth):
        self.stats = w.sb(f"{name}_stats", [P, depth, TPB, 6])
        self.sums = w.sb(f"{name}_sums", [P, depth, TPB, 3])
        self.diff = w.sb(f"{name}_diff", [P, depth, TPB])
        self.diff2 = w.sb(f"{name}_diff2", [P, depth, TPB])
        self.vare = w.sb(f"{name}_vare", [P, depth, TPB])
        self.minus_mean = w.sb(f"{name}_minus_mean", [P, depth, TPB])
        self.var = w.sb(f"{name}_var", [P, depth, TPB])
        self.rstd = w.sb(f"{name}_rstd", [P, depth, TPB])
        self.shift = w.sb(f"{name}_shift", [P, depth, TPB])
        self.link = w.sem(f"{name}_link")
        self.var_ready = w.sem(f"{name}_var_ready")
        self.powered = w.sem(f"{name}_powered")
        self.rstd_ready = w.sem(f"{name}_rstd_ready")

    def statistics(self, nc, dve, x, b, u):
        for t in range(TPB):
            last = nc.vector.bn_stats(self.stats[:, u, t], x[:, t])
        last.then_inc(self.link, 1)
        dve.wait_ge(self.link, b * 3 + 1)
        nc.vector.tensor_tensor(self.sums[:, u], self.stats[:, u, :, 0:3], self.stats[:, u, :, 3:6], ALU.add)
        nc.vector.tensor_tensor(self.diff[:, u], self.stats[:, u, :, 1], self.stats[:, u, :, 4],
                                ALU.subtract).then_inc(self.link, 1)
        dve.wait_ge(self.link, b * 3 + 2)
        nc.vector.scalar_tensor_tensor(self.diff2[:, u], self.diff[:, u], 0.25, self.diff[:, u], ALU.mult, ALU.mult)
        nc.vector.tensor_scalar(self.minus_mean[:, u], self.sums[:, u, :, 1], -0.5, None, ALU.mult)
        nc.vector.tensor_scalar(self.vare[:, u], self.sums[:, u, :, 2], 1.0 / P, LN_EPS, ALU.mult,
                                ALU.add).then_inc(self.link, 1)
        dve.wait_ge(self.link, b * 3 + 3)
        nc.vector.tensor_tensor(self.var[:, u], self.vare[:, u], self.diff2[:, u], ALU.add).then_inc(self.var_ready, 1)

    def inverse(self, nc, pool, minus_half, b, u):
        pool.wait_ge(self.var_ready, b + 1)
        nc.gpsimd.tensor_tensor(self.rstd[:, u], self.var[:, u], minus_half[:, :], ALU.pow).then_inc(self.powered, 1)
        pool.wait_ge(self.powered, b + 1)
        nc.gpsimd.tensor_tensor(self.shift[:, u], self.minus_mean[:, u], self.rstd[:, u], ALU.mult).then_inc(self.rstd_ready, 1)

    def apply(self, nc, act, out, x, b, u, function=ACT.Relu):
        act.wait_ge(self.rstd_ready, b + 1)
        for t in range(TPB):
            last = nc.scalar.activation(out[:, t], x[:, t], function, bias=self.shift[:, u, t:t + 1],
                                        scale=self.rstd[:, u, t:t + 1])
        return last


class Fetch:

    def __init__(self, w, name, depth, table, column, limit):
        self.index = w.sb(f"{name}_index", [P, depth, TPB], I32)
        self.copied = w.sem(f"{name}_copied")
        self.bench = w
        self.done = w.sems(f"{name}_done", depth)
        self.table, self.column, self.limit = table, column, limit

    def issue(self, nc, pool, out, b, u, r):
        w = self.bench
        if reused(b, self.index.shape[1]):
            pool.wait_ge(self.done[u], 64 * r)
            w.settle(pool)
        nc.gpsimd.tensor_copy(self.index[:, u], self.column[:, bass.ds(b * TPB, TPB)]).then_inc(self.copied, 1)
        pool.wait_ge(self.copied, b + 1)
        w.settle(pool)
        for t in range(TPB):
            nc.gpsimd.indirect_dma_start(
                out=out[:, t], out_offset=None, in_=self.table,
                in_offset=bass.IndirectOffsetOnAxis(ap=self.index[:, u, t:t + 1], axis=0),
                bounds_check=self.limit - 1, oob_is_err=False).then_inc(self.done[u], 16)

    def arrived(self, eng, u, r):
        eng.wait_ge(self.done[u], 64 * (r + 1))


def row_stage(nc, name, c, blocks, slots, source, out, *, gather=None, mend=None, keep=None, norm=True, extra=None,
              sums=None, update=None, message=None, message_scale=None, message_bias=None, message_out=None,
              bias=None, relu=False, tail_in=None, tail_out=None, scatter=None):
    D = 6
    residual = extra is not None or (norm and not relu)
    with Bench(nc, name) as w:
        x = w.sb("x", [P, D, TPB, P])
        xr = w.sb("xr", [P, D, TPB, P]) if extra is not None else x
        hn = w.sb("hn", [P, D, TPB, P]) if norm else x
        hT = w.sb("hT", [P, D, BLK])
        tmp = w.sb("tmp", [P, D, TPB, P])
        early_bias = not slots and not relu
        y = w.sb("y", [P, D, TPB, P])
        msg = w.sb("msg", [P, D, TPB, P])
        window = w.sb("window", [P, D, TPB + 2, P]) if sums is not None else None
        same = w.sb("same", [P, D, TPB, 3, P]) if sums is not None else None
        p_t = [w.ps(f"p_t{i}") for i in range(2)]
        p_y = [w.ps(f"p_y{i}") for i in range(2)]
        p_m = [w.ps(f"p_m{i}") for i in range(2)]
        ln = Norm(w, "ln", D) if norm else None
        fetch = None
        if gather is not None:
            fetch = Fetch(w, "gather", D, source, gather, source.shape[0])
        if mend is not None:
            fetch = Fetch(w, "mend", D, mend[0], mend[1], mend[0].shape[0])
        loads = (gather is None) + (extra is not None) + 2 * (sums is not None)
        loaded = w.sems("loaded", D)
        norm_ready = w.sem("norm_ready")
        hT_read = w.sem("hT_ready")
        turned = w.sem("turned")
        multiplied = w.sem("multiplied")
        linked = w.sem("linked")
        biased = w.sem("biased")
        y_ready = w.sem("y_ready")
        msg_ready = w.sem("msg_ready")
        y_stored = w.sems("y_stored", D)
        msg_stored = w.sems("msg_stored", D)
        kept = w.sems("kept", D)
        scat = w.sem("scat")
        si = w.sb("si", [P, D, TPB], I32)
        blk = w.block()
        both = 2 if message_scale is None and message_bias is None else 1

        engines = {}

        def input_ready(eng, u, r):
            if loads:
                eng.wait_ge(loaded[u], 16 * loads * (r + 1))
                if eng is engines.get("sync"):
                    w.settle(eng)
            if fetch is not None:
                fetch.arrived(eng, u, r)

        def slot_free(eng, b, u, r):
            if reused(b, D):
                if update is not None:
                    eng.wait_ge(y_ready, b - D + 1)
                    if eng is engines.get("sync"):
                        w.settle(eng)
                if message is not None:
                    eng.wait_ge(msg_ready, b - D + 1)
                    if eng is engines.get("sync"):
                        w.settle(eng)
                if keep is not None:
                    eng.wait_ge(kept[u], 16 * r)

        ahead = 2 if fetch is not None else 0

        @blk.sync
        def _(sp):
            engines["sync"] = sp

            def load(b, u, r):
                if loads:
                    slot_free(sp, b, u, r)
                    w.settle(sp)
                if gather is None:
                    if tail_in is not None and isinstance(b, int) and b == blocks - 1:
                        sp.dma_start(x[0:tail_in, u], block_rows(source, b, slots, tail_in)).then_inc(loaded[u], 16)
                    else:
                        sp.dma_start(x[:, u], block_rows(source, b, slots)).then_inc(loaded[u], 16)
                if extra is not None:
                    if tail_in is not None and isinstance(b, int) and b == blocks - 1:
                        sp.dma_start(xr[0:tail_in, u], block_rows(extra, b, slots, tail_in)).then_inc(loaded[u], 16)
                    else:
                        sp.dma_start(xr[:, u], block_rows(extra, b, slots)).then_inc(loaded[u], 16)
                if sums is not None:
                    sp.dma_start(window[:, u], sums[bass.ds(b * BLK, BLK + 2 * P), :].rearrange(
                        "(t p) d -> p t d", p=P)).then_inc(loaded[u], 16)
                    sp.dma_start(same[:, u].rearrange("p t w e -> p t (w e)"),
                                 c.same_dram[bass.ds(b * BLK, BLK), :].rearrange(
                                     "(t p) d -> p t d", p=P)).then_inc(loaded[u], 16)

            def store(b, u, r):
                if update is not None and scatter is None:
                    sp.wait_ge(y_ready, b + 1)
                    w.settle(sp)
                    if tail_out is not None and isinstance(b, int) and b == blocks - 1:
                        sp.dma_start(block_rows(out, b, slots, tail_out), y[0:tail_out, u]).then_inc(y_stored[u], 16)
                    else:
                        sp.dma_start(block_rows(out, b, slots), y[:, u]).then_inc(y_stored[u], 16)
                if message is not None:
                    sp.wait_ge(msg_ready, b + 1)
                    w.settle(sp)
                    sp.dma_start(block_rows(message_out[P:, :], b, True), msg[:, u]).then_inc(msg_stored[u], 16)
            def store_input(b, u, r):
                input_ready(sp, u, r)
                w.settle(sp)
                sp.dma_start(block_rows(keep, b, True), x[:, u]).then_inc(kept[u], 16)

            pipeline(nc.sync, blocks, [(0, load)] + ([(ahead + 1, store_input)] if keep is not None else []) +
                     [(ahead + 4, store)], D)
            for u in range(D):
                n = cdiv(blocks - u, D)
                if update is not None and scatter is None:
                    sp.wait_ge(y_stored[u], 16 * n)
                    w.settle(sp)
                if message is not None:
                    sp.wait_ge(msg_stored[u], 16 * n)
                    w.settle(sp)
                if keep is not None:
                    sp.wait_ge(kept[u], 16 * n)
                    w.settle(sp)

        @blk.gpsimd
        def _(pool):
            if scatter is not None:
                spread = pool.value_load(c.spread[0:1, 0:1])

            def bring(b, u, r):
                if gather is not None:
                    slot_free(pool, b, u, r)
                else:
                    pool.wait_ge(loaded[u], 16 * loads * (r + 1))
                fetch.issue(nc, pool, x[:, u], b, u, r)

            def inverse(b, u, r):
                ln.inverse(nc, pool, c.minus_half, b, u)

            def add_bias(b, u, r):
                pool.wait_ge(loaded[u], 16 * loads * (r + 1))
                nc.gpsimd.tensor_tensor(tmp[:, u], xr[:, u], over_tiles(bias), ALU.add).then_inc(biased, 1)

            def spread_out(b, u, r, in_turn):
                if reused(b, D):
                    pool.wait_ge(y_stored[u], 64 * r)
                    w.settle(pool)
                nc.gpsimd.tensor_copy(si[:, u], scatter[:, bass.ds(b * TPB, TPB)]).then_inc(scat, 1)
                pool.wait_ge(scat, b + 1)
                w.settle(pool)
                pool.wait_ge(y_ready, b + 1)
                w.settle(pool)
                for t in range(TPB):
                    nc.gpsimd.indirect_dma_start(
                        out=out, out_offset=bass.IndirectOffsetOnAxis(ap=si[:, u, t:t + 1], axis=0),
                        in_=y[:, u, t], in_offset=None, bounds_check=out.shape[0] - 1,
                        oob_is_err=False).then_inc(y_stored[u], 16)
                    if in_turn:
                        pool.wait_ge(y_stored[u], 64 * r + 16 * (t + 1))
                        w.settle(pool)

            steps = []
            if fetch is not None:
                steps.append((0, bring))
            if norm:
                steps.append((ahead, inverse))
            if early_bias:
                steps.append((ahead + 1, add_bias))
            if scatter is not None:
                with pool.If(spread == 0):
                    pipeline(nc.gpsimd, blocks, steps + [(ahead + 4, partial(spread_out, in_turn=False))], D)
                with pool.If(spread != 0):
                    pipeline(nc.gpsimd, blocks, steps + [(ahead + 4, partial(spread_out, in_turn=True))], D)
            elif steps:
                pipeline(nc.gpsimd, blocks, steps, D)
            if scatter is not None:
                for u in range(D):
                    pool.wait_ge(y_stored[u], 64 * cdiv(blocks - u, D))

        @blk.vector
        def _(dve):
            def statistics(b, u, r):
                input_ready(dve, u, r)
                ln.statistics(nc, dve, x[:, u], b, u)

            def finish(b, u, r):
                dve.wait_ge(multiplied, b + 1)
                if update is not None:
                    if reused(b, D):
                        dve.wait_ge(y_stored[u], (64 if scatter is not None else 16) * r)
                    if early_bias:
                        dve.wait_ge(biased, b + 1)
                    elif relu:
                        nc.vector.tensor_tensor(tmp[:, u], tiles(p_y[u % 2][:, :]), over_tiles(bias), ALU.add).then_inc(linked, 1)
                    else:
                        nc.vector.tensor_tensor(tmp[:, u], tiles(p_y[u % 2][:, :]), xr[:, u], ALU.add).then_inc(linked, 1)
                    if not early_bias:
                        dve.wait_ge(linked, b + 1)
                    if early_bias:
                        op = nc.vector.tensor_tensor(y[:, u], tiles(p_y[u % 2][:, :]), tmp[:, u], ALU.add)
                    elif relu and residual:
                        op = nc.vector.scalar_tensor_tensor(flat(y[:, u]), flat(tmp[:, u]), 0.0, flat(xr[:, u]), ALU.max, ALU.add)
                    elif relu:
                        op = nc.vector.tensor_scalar(flat(y[:, u]), flat(tmp[:, u]), 0.0, None, ALU.max)
                    else:
                        op = nc.vector.tensor_tensor(y[:, u], tmp[:, u], over_tiles(bias), ALU.add)
                    op.then_inc(y_ready, 1)
                if message is not None and message_bias is not None:
                    if reused(b, D):
                        dve.wait_ge(msg_stored[u], 16 * r)
                    nc.vector.tensor_tensor(msg[:, u], tiles(p_m[u % 2][:, :]), over_tiles(message_bias), ALU.add).then_inc(msg_ready, 1)

            if norm:
                pipeline(nc.vector, blocks, [(ahead + 4, finish), (ahead, statistics)], D)
            else:
                pipeline(nc.vector, blocks, [(ahead + 4, finish)], D)

        @blk.tensor
        def _(pe):
            def turn(b, u, r):
                if norm:
                    pe.wait_ge(norm_ready, b + 1)
                else:
                    input_ready(pe, u, r)
                if reused(b, 2):
                    pe.wait_ge(hT_read, b - 1)
                for t in range(TPB):
                    last = nc.tensor.transpose(p_t[u % 2][:, t * P:(t + 1) * P], hn[:, u, t], c.ident[:, :])
                last.then_inc(turned, 1)

            def multiply(b, u, r):
                pe.wait_ge(hT_read, b + 1)
                if reused(b, 2):
                    if update is not None:
                        pe.wait_ge(y_ready, b - 1)
                    if message is not None:
                        pe.wait_ge(msg_ready, b - 1)
                if sums is not None:
                    pe.wait_ge(loaded[u], 16 * loads * (r + 1))
                for t in range(TPB):
                    left = hT[:, u, t * P:(t + 1) * P]
                    if update is not None:
                        to = p_y[u % 2][:, t * P:(t + 1) * P]
                        if sums is not None:
                            for v in range(3):
                                nc.tensor.matmul(to, same[:, u, t, v], window[:, u, t + v], start=(v == 0), stop=False)
                        last = nc.tensor.matmul(to, left, update, start=(sums is None), stop=True)
                    if message is not None:
                        last = nc.tensor.matmul(p_m[u % 2][:, t * P:(t + 1) * P], left, message, start=True, stop=True)
                last.then_inc(multiplied, 1)

            pipeline(nc.tensor, blocks, [(ahead + 2, turn), (ahead + 3, multiply)], D)

        @blk.scalar
        def _(act):
            def lift(b, u, r):
                act.wait_ge(turned, b + 1)
                nc.scalar.activation(hT[:, u], p_t[u % 2][:, :], ACT.Copy).then_inc(hT_read, 1)

            def send(b, u, r):
                act.wait_ge(multiplied, b + 1)
                if reused(b, D):
                    act.wait_ge(msg_stored[u], 16 * r)
                if message_scale is not None:
                    for t in range(TPB):
                        last = nc.scalar.activation(msg[:, u, t], p_m[u % 2][:, t * P:(t + 1) * P], ACT.Copy,
                                                    scale=message_scale[:, bass.ds(b * TPB + t, 1)])
                else:
                    last = nc.scalar.activation(flat(msg[:, u]), p_m[u % 2][:, :], ACT.Copy)
                last.then_inc(msg_ready, 1)

            def apply(b, u, r):
                input_ready(act, u, r)
                ln.apply(nc, act, hn[:, u], x[:, u], b, u).then_inc(norm_ready, 1)

            steps = []
            if message is not None and message_bias is None:
                steps.append((ahead + 4, send))
            steps.append((ahead + 3, lift))
            if norm:
                steps.append((ahead + 1, apply))
            pipeline(nc.scalar, blocks, steps, D)


def mean_stage(nc, name, c, blocks, slots, source, weight, total):
    D = 4
    with Bench(nc, name) as w:
        x = w.sb("x", [P, D, TPB, P])
        h = w.sb("h", [P, D, TPB, P])
        wt = w.sb("wt", [P, D, TPB])
        acc = w.ps("acc")
        ln = Norm(w, "ln", D)
        loaded = w.sems("loaded", D)
        h_ready = w.sem("h_ready")
        w_ready = w.sem("w_ready")
        multiplied = w.sem("multiplied")
        blk = w.block()

        @blk.sync
        def _(sp):
            def load(b, u, r):
                if reused(b, D):
                    sp.wait_ge(h_ready, b - D + 1)
                    w.settle(sp)
                sp.dma_start(x[:, u], block_rows(source, b, slots)).then_inc(loaded[u], 16)
            pipeline(nc.sync, blocks, [(0, load)], D)

        @blk.gpsimd
        def _(pool):
            def inverse(b, u, r):
                ln.inverse(nc, pool, c.minus_half, b, u)
            pipeline(nc.gpsimd, blocks, [(0, inverse)], D)

        @blk.vector
        def _(dve):
            def statistics(b, u, r):
                dve.wait_ge(loaded[u], 16 * (r + 1))
                ln.statistics(nc, dve, x[:, u], b, u)

            def weigh(b, u, r):
                if reused(b, D):
                    dve.wait_ge(multiplied, b - D + 1)
                nc.vector.tensor_scalar(wt[:, u], weight[:, bass.ds(b * TPB, TPB)], 1.0, None, ALU.mult).then_inc(w_ready, 1)
            pipeline(nc.vector, blocks, [(0, statistics), (0, weigh)], D)

        @blk.scalar
        def _(act):
            def rectify(b, u, r):
                if reused(b, D):
                    act.wait_ge(multiplied, b - D + 1)
                ln.apply(nc, act, h[:, u], x[:, u], b, u).then_inc(h_ready, 1)
            pipeline(nc.scalar, blocks, [(1, rectify)], D)
            act.wait_ge(multiplied, blocks)
            nc.scalar.activation(total, acc[:, 0:1], ACT.Copy)

        @blk.tensor
        def _(pe):
            def add(b, u, r):
                pe.wait_ge(h_ready, b + 1)
                pe.wait_ge(w_ready, b + 1)
                for t in range(TPB):
                    first = isinstance(b, int) and b == 0 and t == 0
                    end = isinstance(b, int) and b == blocks - 1 and t == TPB - 1
                    last = nc.tensor.matmul(acc[:, 0:1], h[:, u, t], wt[:, u, t:t + 1], start=first, stop=end)
                last.then_inc(multiplied, 1)
            pipeline(nc.tensor, blocks, [(1, add)], D)


def gru_stage(nc, name, c, blocks, slots, source, out, *, mend=None, sums=None, message=None, message_out=None):
    D, H = 8, 4
    with Bench(nc, name) as w:
        x = w.sb("x", [P, D, TPB, P])
        xb = w.sb("xb", [P, D, TPB, P])
        hn = w.sb("hn", [P, H, TPB, P])
        hT = w.sb("hT", [P, H, BLK])
        rT = w.sb("rT", [P, 2, BLK])
        zT = w.sb("zT", [P, 2, BLK])
        uT = w.sb("uT", [P, 2, BLK])
        nT = w.sb("nT", [P, 2, BLK])
        dT = w.sb("dT", [P, 2, BLK])
        eT = w.sb("eT", [P, 2, BLK])
        sT = w.sb("sT", [P, 2, BLK])
        yn = w.sb("yn", [P, 2, TPB, P])
        yg = w.sb("yg", [P, 2, TPB, P])
        y = w.sb("y", [P, 2, TPB, P])
        if message is not None:
            msg = w.sb("msg", [P, H, TPB, P])
            p_m = w.ps("p_m")
        if sums is not None:
            window = w.sb("window", [P, H, TPB + 2, P])
            same = w.sb("same", [P, H, TPB, 3, P])
            tT = w.sb("tT", [P, 2, BLK])
            tR = w.sb("tR", [P, D, BLK])
            vT = w.sb("vT", [P, 2, BLK])
            yt = w.sb("yt", [P, 2, TPB, P])
            p_s = w.ps("p_s")
            p_q = w.ps("p_q")
            p_i = w.ps("p_i")
        G = 2 if message is None and sums is None else 1
        p_t, p_n = w.ps("p_t"), w.ps("p_n")
        p_r, p_z, p_y = ([w.ps(f"{n}{i}") for i in range(G)] for n in ("p_r", "p_z", "p_y"))
        ln, ln2 = Norm(w, "ln", D), Norm(w, "ln2", D)
        fetch = Fetch(w, "mend", D, mend[0], mend[1], mend[0].shape[0]) if mend is not None else None
        loads = 1
        loaded = w.sems("loaded", D)
        loaded_sums = w.sems("loaded_sums", H)
        names = ("norm_ready", "turned", "hT_ready", "gates", "sig", "u_ready", "n_ready", "d_ready", "e_ready", "s_ready",
                 "back", "yn_ready", "yg_ready", "y_ready", "xb_ready", "summed", "tT_ready", "tR_ready",
                 "msg_mult", "msg_ready", "v_ready", "yt_ready", "stats2")
        s = {n: w.sem(n) for n in names}
        stored = w.sems("stored", 2)
        msg_stored = w.sems("msg_stored", H)
        blk = w.block()
        ahead = 1 if fetch is not None else 0
        pool_helps = fetch is None

        def input_ready(eng, u, r):
            eng.wait_ge(loaded[u], 16 * (r + 1))
            if fetch is not None:
                fetch.arrived(eng, u, r)

        def uses(b, u, slots):
            return b // slots if isinstance(b, int) else None

        @blk.sync
        def _(sp):
            def load(b, u, r):
                if reused(b, D):
                    sp.wait_ge(s["xb_ready"], b - D + 1)
                    w.settle(sp)
                    sp.wait_ge(s["norm_ready"], b - D + 1)
                    w.settle(sp)
                sp.dma_start(x[:, u], block_rows(source, b, slots)).then_inc(loaded[u], 16)

            def load_sums(b, u, r):
                if reused(b, H):
                    sp.wait_ge(s["summed"], b - H + 1)
                    w.settle(sp)
                sp.dma_start(window[:, u % H], sums[bass.ds(b * BLK, BLK + 2 * P), :].rearrange(
                    "(t p) d -> p t d", p=P)).then_inc(loaded_sums[u % H], 16)
                sp.dma_start(same[:, u % H].rearrange("p t w e -> p t (w e)"),
                             c.same_dram[bass.ds(b * BLK, BLK), :].rearrange(
                                 "(t p) d -> p t d", p=P)).then_inc(loaded_sums[u % H], 16)

            def store(b, u, r):
                sp.wait_ge(s["y_ready"], b + 1)
                w.settle(sp)
                sp.dma_start(block_rows(out, b, slots), y[:, u % 2]).then_inc(stored[u % 2], 16)

            def store_msg(b, u, r):
                sp.wait_ge(s["msg_ready"], b + 1)
                w.settle(sp)
                sp.dma_start(block_rows(message_out[P:, :], b, True), msg[:, u % H]).then_inc(msg_stored[u % H], 16)

            steps = [(0, load)]
            if sums is not None:
                steps.append((1, load_sums))
            if message is not None:
                steps.append((ahead + 4, store_msg))
            steps.append((ahead + 7, store))
            pipeline(nc.sync, blocks, steps, D)
            for u in range(2):
                sp.wait_ge(stored[u], 16 * cdiv(blocks - u, 2))
                w.settle(sp)
            if message is not None:
                for u in range(H):
                    sp.wait_ge(msg_stored[u], 16 * cdiv(blocks - u, H))
                    w.settle(sp)

        @blk.gpsimd
        def _(pool):
            def bring(b, u, r):
                pool.wait_ge(loaded[u], 16 * (r + 1))
                fetch.issue(nc, pool, x[:, u], b, u, r)

            def inverse(b, u, r):
                ln.inverse(nc, pool, c.minus_half, b, u)

            def with_beta(b, u, r):
                if reused(b, D):
                    pool.wait_ge(s["y_ready"], b - D + 1)
                input_ready(pool, u, r)
                nc.gpsimd.tensor_tensor(xb[:, u], x[:, u], over_tiles(c.beta), ALU.add).then_inc(s["xb_ready"], 1)

            def inverse2(b, u, r):
                ln2.inverse(nc, pool, c.minus_half, b, u)

            def difference(b, u, r):
                pool.wait_ge(s["n_ready"], b + 1)
                nc.gpsimd.tensor_tensor(dT[:, u % 2], hT[:, u % H], nT[:, u % 2], ALU.subtract).then_inc(s["d_ready"], 1)

            steps = [(0, bring)] if fetch is not None else []
            if pool_helps:
                steps.append((ahead + 5, difference))
            steps += [(ahead + 6, inverse2), (ahead, inverse), (ahead + 1, with_beta)]
            pipeline(nc.gpsimd, blocks, steps, D)

        @blk.vector
        def _(dve):
            def statistics(b, u, r):
                input_ready(dve, u, r)
                ln.statistics(nc, dve, x[:, u], b, u)

            def step(b, u, r):
                v, k = u % 2, u % H
                dve.wait_ge(s["sig"], b + 1)
                if reused(b, 2):
                    dve.wait_ge(s["n_ready"], b - 1)
                nc.vector.scalar_tensor_tensor(uT[:, v], p_n[:, :], c.b_hn, rT[:, v], ALU.add, ALU.mult).then_inc(s["u_ready"], 1)
                if sums is not None:
                    dve.wait_ge(s["u_ready"], b + 1)
                    nc.vector.tensor_tensor(vT[:, v], p_i[:, :], uT[:, v], ALU.add).then_inc(s["v_ready"], 1)

            def blend(b, u, r):
                v, k = u % 2, u % H
                dve.wait_ge(s["n_ready"], b + 1)
                if not pool_helps:
                    nc.vector.tensor_tensor(dT[:, v], hT[:, k], nT[:, v], ALU.subtract).then_inc(s["d_ready"], 1)
                dve.wait_ge(s["d_ready"], b + 1)
                nc.vector.tensor_tensor(eT[:, v], dT[:, v], zT[:, v], ALU.mult).then_inc(s["e_ready"], 1)
                dve.wait_ge(s["e_ready"], b + 1)
                if reused(b, 2):
                    dve.wait_ge(s["back"], b - 1)
                nc.vector.tensor_tensor(sT[:, v], eT[:, v], nT[:, v], ALU.add).then_inc(s["s_ready"], 1)

            def send(b, u, r):
                dve.wait_ge(s["msg_mult"], b + 1)
                if reused(b, H):
                    if isinstance(b, int):
                        dve.wait_ge(msg_stored[u % H], 16 * (b // H))
                    else:
                        dve.wait_ge(msg_stored[u % H], r * (16 * (D // H)) + 16 * (u // H))
                nc.vector.tensor_tensor(msg[:, u % H], tiles(p_m[:, :]), over_tiles(c.b_msg), ALU.add).then_inc(s["msg_ready"], 1)

            def statistics2(b, u, r):
                dve.wait_ge(s["back"], b + 1)
                ln2.statistics(nc, dve, tiles(p_y[u % G][:, :]), b, u)

            def finish(b, u, r):
                v = u % 2
                dve.wait_ge(s["yn_ready"], b + 1)
                nc.vector.tensor_tensor(yg[:, v], yn[:, v], over_tiles(c.gamma), ALU.mult).then_inc(s["yg_ready"], 1)
                dve.wait_ge(s["yg_ready"], b + 1)
                left = yg
                if sums is not None:
                    dve.wait_ge(s["tR_ready"], b + 1)
                    nc.vector.tensor_tensor(yt[:, v], yg[:, v], tiles(tR[:, u]), ALU.add).then_inc(s["yt_ready"], 1)
                    dve.wait_ge(s["yt_ready"], b + 1)
                    left = yt
                dve.wait_ge(s["xb_ready"], b + 1)
                if reused(b, 2):
                    if isinstance(b, int):
                        dve.wait_ge(stored[v], 16 * (b // 2))
                    else:
                        dve.wait_ge(stored[v], r * (16 * (D // 2)) + 16 * (u // 2))
                nc.vector.tensor_tensor(y[:, v], left[:, v], xb[:, u], ALU.add).then_inc(s["y_ready"], 1)

            steps = [(ahead + 6, statistics2), (ahead + 5, blend), (ahead + 4, step), (ahead, statistics)]
            if message is not None:
                steps.append((ahead + 4, send))
            steps.append((ahead + 7, finish))
            pipeline(nc.vector, blocks, steps, D)

        @blk.tensor
        def _(pe):
            def turn(b, u, r):
                pe.wait_ge(s["norm_ready"], b + 1)
                if reused(b, 1):
                    pe.wait_ge(s["hT_ready"], b)
                for t in range(TPB):
                    last = nc.tensor.transpose(p_t[:, t * P:(t + 1) * P], hn[:, u % H, t], c.ident[:, :])
                last.then_inc(s["turned"], 1)

            def sum_up(b, u, r):
                k = u % H
                if isinstance(b, int):
                    pe.wait_ge(loaded_sums[k], 32 * (b // H + 1))
                else:
                    pe.wait_ge(loaded_sums[k], r * (32 * (D // H)) + 32 * (u // H + 1))
                if reused(b, 1):
                    pe.wait_ge(s["tR_ready"], b)
                for t in range(TPB):
                    for v in range(3):
                        nc.tensor.matmul(p_s[:, t * P:(t + 1) * P], window[:, k, t + v], same[:, k, t, v],
                                         start=(v == 0), stop=(v == 2))
                for t in range(TPB):
                    for v in range(3):
                        last = nc.tensor.matmul(p_q[:, t * P:(t + 1) * P], same[:, k, t, v], window[:, k, t + v],
                                                start=(v == 0), stop=(v == 2))
                last.then_inc(s["summed"], 1)

            def gates(b, u, r):
                k, v = u % H, u % 2
                pe.wait_ge(s["hT_ready"], b + 1)
                if sums is not None:
                    pe.wait_ge(s["tT_ready"], b + 1)
                if reused(b, G):
                    pe.wait_ge(s["sig"], b - G + 1)
                for g, to in ((0, p_r[u % G]), (1, p_z[u % G])):
                    last = nc.tensor.matmul(to[:, :], c.w_hh[:, g * P:(g + 1) * P], hT[:, k], start=True, stop=(sums is None))
                    if sums is not None:
                        nc.tensor.matmul(to[:, :], c.w_ih[:, g * P:(g + 1) * P], tT[:, v], start=False, stop=True)
                if reused(b, 1):
                    pe.wait_ge(s["v_ready" if sums is not None else "u_ready"], b)
                last = nc.tensor.matmul(p_n[:, :], c.w_hh[:, 2 * P:3 * P], hT[:, k], start=True, stop=True)
                if sums is not None:
                    last = nc.tensor.matmul(p_i[:, :], c.w_ih[:, 2 * P:3 * P], tT[:, v], start=True, stop=True)
                last.then_inc(s["gates"], 1)

            def messages(b, u, r):
                if reused(b, 1):
                    pe.wait_ge(s["msg_ready"], b)
                for t in range(TPB):
                    last = nc.tensor.matmul(p_m[:, t * P:(t + 1) * P], hT[:, u % H, t * P:(t + 1) * P], message,
                                            start=True, stop=True)
                last.then_inc(s["msg_mult"], 1)

            def back(b, u, r):
                pe.wait_ge(s["s_ready"], b + 1)
                if reused(b, G):
                    pe.wait_ge(s["yn_ready"], b - G + 1)
                for t in range(TPB):
                    last = nc.tensor.transpose(p_y[u % G][:, t * P:(t + 1) * P], sT[:, u % 2, t * P:(t + 1) * P], c.ident[:, :])
                last.then_inc(s["back"], 1)

            steps = [(ahead + 6, back), (ahead + 2, turn)]
            if sums is not None:
                steps.append((ahead + 2, sum_up))
            steps.append((ahead + 3, gates))
            if message is not None:
                steps.append((ahead + 3, messages))
            pipeline(nc.tensor, blocks, steps, D)

        @blk.scalar
        def _(act):
            def lift(b, u, r):
                act.wait_ge(s["turned"], b + 1)
                if reused(b, H):
                    act.wait_ge(s["d_ready"], b - H + 1)
                nc.scalar.activation(hT[:, u % H], p_t[:, :], ACT.Copy).then_inc(s["hT_ready"], 1)

            def lift_sums(b, u, r):
                act.wait_ge(s["summed"], b + 1)
                if reused(b, 2):
                    act.wait_ge(s["gates"], b - 1)
                nc.scalar.activation(tT[:, u % 2], p_s[:, :], ACT.Copy).then_inc(s["tT_ready"], 1)
                if reused(b, D):
                    act.wait_ge(s["yt_ready"], b - D + 1)
                nc.scalar.activation(tR[:, u], p_q[:, :], ACT.Copy).then_inc(s["tR_ready"], 1)

            def sigmoids(b, u, r):
                v = u % 2
                act.wait_ge(s["gates"], b + 1)
                if reused(b, 2):
                    act.wait_ge(s["u_ready"], b - 1)
                nc.scalar.activation(rT[:, v], p_r[u % G][:, :], ACT.Sigmoid, bias=c.b_r)
                if reused(b, 2):
                    act.wait_ge(s["e_ready"], b - 1)
                nc.scalar.activation(zT[:, v], p_z[u % G][:, :], ACT.Sigmoid, bias=c.b_z).then_inc(s["sig"], 1)

            def candidate(b, u, r):
                v = u % 2
                act.wait_ge(s["v_ready" if sums is not None else "u_ready"], b + 1)
                if reused(b, 2):
                    act.wait_ge(s["s_ready"], b - 1)
                nc.scalar.activation(nT[:, v], (vT if sums is not None else uT)[:, v], ACT.Tanh, bias=c.b_n).then_inc(s["n_ready"], 1)

            def scale(b, u, r):
                if reused(b, 2):
                    act.wait_ge(s["yg_ready"], b - 1)
                ln2.apply(nc, act, yn[:, u % 2], tiles(p_y[u % G][:, :]), b, u, ACT.Identity).then_inc(s["yn_ready"], 1)

            def apply(b, u, r):
                if reused(b, H):
                    act.wait_ge(s["turned"], b - H + 1)
                input_ready(act, u, r)
                ln.apply(nc, act, hn[:, u % H], x[:, u], b, u).then_inc(s["norm_ready"], 1)

            steps = [(ahead + 3, lift)]
            if sums is not None:
                steps.append((ahead + 3, lift_sums))
            steps += [(ahead + 5, candidate), (ahead + 4, sigmoids), (ahead + 1, apply), (ahead + 6, scale)]
            pipeline(nc.scalar, blocks, steps, D)


def film_stage(nc, name, c, blocks, sources, dests, message_out):
    D = 4
    with Bench(nc, name) as w:
        xs = w.sb("xs", [P, D, 2, TPB, P])
        hn = w.sb("hn", [P, 2, 2, TPB, P])
        hT = w.sb("hT", [P, 2, 2, BLK])
        rel = w.sb("rel", [P, D, BLK], I32)
        hm = w.sb("hm", [P, 2, 2, NREL, BLK])
        ms = w.sb("ms", [P, 2, TPB, P])
        gm = w.sb("gm", [P, 2, TPB, P])
        gb = w.sb("gb", [P, 2, TPB, P])
        msg = w.sb("msg", [P, D, TPB, P])
        p_t = [w.ps(f"p_t{i}") for i in range(2)]
        p_m = [w.ps(f"p_m{i}") for i in range(2)]
        p_f = [w.ps(f"p_f{i}", (P, TPB * 2 * P)) for i in range(2)]
        lns = [Norm(w, f"ln{k}", D) for k in range(2)]
        loaded = w.sems("loaded", D)
        norm_ready = w.sem("norm_ready")
        turned = w.sem("turned")
        hT_ready = w.sem("hT_ready")
        masked = w.sem("masked")
        multiplied = w.sem("multiplied")
        ms_ready = w.sem("ms_ready")
        gm_ready = w.sem("gm_ready")
        gb_ready = w.sem("gb_ready")
        msg_ready = w.sem("msg_ready")
        stored = w.sems("stored", D)
        blk = w.block()

        @blk.sync
        def _(sp):
            def load(b, u, r):
                if reused(b, D):
                    sp.wait_ge(masked, b * 2 - 2 * D + 2)
                    w.settle(sp)
                sp.dma_start(xs[:, u, 0], block_rows(sources, b, True)).then_inc(loaded[u], 16)
                sp.dma_start(xs[:, u, 1], block_rows(dests, b, True)).then_inc(loaded[u], 16)
                sp.dma_start(rel[:, u], c.relation_row[:, bass.ds(b * BLK, BLK)].to_broadcast([P, BLK])).then_inc(loaded[u], 16)

            def store(b, u, r):
                sp.wait_ge(msg_ready, b + 1)
                w.settle(sp)
                sp.dma_start(block_rows(message_out[P:, :], b, True), msg[:, u]).then_inc(stored[u], 16)
            pipeline(nc.sync, blocks, [(0, load), (4, store)], D)
            for u in range(D):
                sp.wait_ge(stored[u], 16 * cdiv(blocks - u, D))
                w.settle(sp)

        @blk.gpsimd
        def _(pool):
            def inverse(b, u, r):
                for k in range(2):
                    lns[k].inverse(nc, pool, c.minus_half, b, u)
            pipeline(nc.gpsimd, blocks, [(0, inverse)], D)

        @blk.vector
        def _(dve):
            def statistics(b, u, r):
                dve.wait_ge(loaded[u], 48 * (r + 1))
                for k in range(2):
                    lns[k].statistics(nc, dve, xs[:, u, k], b, u)

            def mask(b, u, r):
                for k in range(2):
                    dve.wait_ge(hT_ready, b * 2 + k + 1)
                    if reused(b, 2):
                        dve.wait_ge(multiplied, b * 2 + k - 3)
                    for q in range(NREL):
                        last = nc.vector.scalar_tensor_tensor(hm[:, u % 2, k, q], rel[:, u], float(q), hT[:, u % 2, k],
                                                              ALU.is_equal, ALU.mult)
                    last.then_inc(masked, 1)

            def finish(b, u, r):
                f = p_f[u % 2][:, :].rearrange("p (t k d) -> p t k d", t=TPB, k=2)
                v = u % 2
                dve.wait_ge(multiplied, b * 2 + 2)
                dve.wait_ge(ms_ready, b + 1)
                nc.vector.tensor_tensor(gm[:, v], f[:, :, 0], ms[:, v], ALU.mult).then_inc(gm_ready, 1)
                dve.wait_ge(gm_ready, b + 1)
                if reused(b, 2):
                    dve.wait_ge(msg_ready, b - 1)
                nc.vector.tensor_tensor(gb[:, v], f[:, :, 1], gm[:, v], ALU.add).then_inc(gb_ready, 1)
            pipeline(nc.vector, blocks, [(2, mask), (4, finish), (0, statistics)], D)

        @blk.tensor
        def _(pe):
            def turn(b, u, r):
                for k in range(2):
                    pe.wait_ge(norm_ready, b * 2 + k + 1)
                    if reused(b, 1):
                        pe.wait_ge(hT_ready, b * 2 + k - 1)
                    for t in range(TPB):
                        last = nc.tensor.transpose(p_t[k][:, t * P:(t + 1) * P], hn[:, u % 2, k, t], c.ident[:, :])
                    last.then_inc(turned, 1)

            def multiply(b, u, r):
                for k in range(2):
                    pe.wait_ge(masked, b * 2 + k + 1)
                    if reused(b, 2):
                        pe.wait_ge(ms_ready if k == 0 else gb_ready, b - 1)
                    for t in range(TPB):
                        for q in range(NREL):
                            left = hm[:, u % 2, k, q, t * P:(t + 1) * P]
                            if k == 0:
                                last = nc.tensor.matmul(p_m[u % 2][:, t * P:(t + 1) * P], left, c.w_rel[:, q * P:(q + 1) * P],
                                                        start=(q == 0), stop=(q == NREL - 1))
                            else:
                                last = nc.tensor.matmul(p_f[u % 2][:, t * 2 * P:(t + 1) * 2 * P], left,
                                                        c.w_film[:, q * 2 * P:(q + 1) * 2 * P],
                                                        start=(q == 0), stop=(q == NREL - 1))
                    last.then_inc(multiplied, 1)
            pipeline(nc.tensor, blocks, [(3, multiply), (1, turn)], D)

        @blk.scalar
        def _(act):
            def lift(b, u, r):
                for k in range(2):
                    act.wait_ge(turned, b * 2 + k + 1)
                    if reused(b, 2):
                        act.wait_ge(masked, b * 2 - 4 + k + 1)
                    nc.scalar.activation(hT[:, u % 2, k], p_t[k][:, :], ACT.Copy).then_inc(hT_ready, 1)

            def apply(b, u, r):
                if reused(b, 2):
                    act.wait_ge(turned, b * 2 - 2)
                act.wait_ge(loaded[u], 48 * (r + 1))
                for k in range(2):
                    lns[k].apply(nc, act, hn[:, u % 2, k], xs[:, u, k], b, u).then_inc(norm_ready, 1)

            def copy_m(b, u, r):
                act.wait_ge(multiplied, b * 2 + 1)
                if reused(b, 2):
                    act.wait_ge(gm_ready, b - 1)
                nc.scalar.activation(flat(ms[:, u % 2]), p_m[u % 2][:, :], ACT.Copy).then_inc(ms_ready, 1)

            def rectify(b, u, r):
                act.wait_ge(gb_ready, b + 1)
                if reused(b, D):
                    act.wait_ge(stored[u], 16 * r)
                nc.scalar.activation(flat(msg[:, u]), flat(gb[:, u % 2]), ACT.Relu).then_inc(msg_ready, 1)
            pipeline(nc.scalar, blocks, [(4, copy_m), (2, lift), (1, apply), (4, rectify)], D)


class Common:
    pass


WEIGHTS = (("W1_0", P), ("W1_1", P), ("W2_0", P), ("W2_1", P), ("W_msg", P), ("w_ih", 3 * P), ("w_hh", 3 * P),
           ("w_rel", NREL * P), ("w_film", NREL * 2 * P), ("loop_w", P), ("W_neigh", P), ("W_self", P))
ROWS = ("b1", "b2", "b_msg", "gamma", "beta", "h_bias", "b_neigh", "b_self")


def constants_phase(nc, c, args):
    with Bench(nc, "const") as w:
        loaded, made, fixed = w.sem("loaded"), w.sem("made"), w.sem("fixed")
        zero = w.sb("zero", [P, P])
        blk = w.block()
        count = [0]

        @blk.sync
        def _(sp):
            for name, cols in WEIGHTS:
                sp.dma_start(c.weights[name][:, :], args[name]).then_inc(loaded, 16)
                count[0] += 1
            for name in ROWS:
                sp.dma_start(c.rows[name][:, :], args[name].rearrange("(a n) -> a n", a=1).to_broadcast([P, P])).then_inc(loaded, 16)
                count[0] += 1
            for col, at in ((c.g_ih, args["b_ih"]), (c.g_hh, args["b_hh"])):
                for g in range(3):
                    sp.dma_start(col[:, g:g + 1], at[g * P:(g + 1) * P].rearrange("(p a) -> p a", a=1)).then_inc(loaded, 16)
                    count[0] += 1
            sp.dma_start(c.src[:, :], args["src_columns"]).then_inc(loaded, 16)
            sp.dma_start(c.dst[:, 1:c.tiles + 1], args["dst_columns"]).then_inc(loaded, 16)
            count[0] += 2
            sp.wait_ge(made, 1)
            for at in (0, (c.tiles + 1) * P):
                sp.dma_start(c.msg[at:at + P, :], zero[:, :]).then_inc(loaded, 16)
                count[0] += 1
            sp.wait_ge(loaded, 16 * count[0])

        @blk.vector
        def _(dve):
            nc.vector.memset(zero[:, :], 0.0).then_inc(made, 1)
            nc.vector.memset(c.ones[:, :], 1.0)
            nc.vector.memset(c.minus_half[:, :], -0.5)
            nc.vector.memset(c.minus_half_wide[:, :], -0.5)
            nc.vector.memset(c.dst[:, 0:1], -1)
            nc.vector.memset(c.dst[:, c.tiles + 1:c.tiles + 2], -1)

        @blk.gpsimd
        def _(pool):
            nc.gpsimd.memset(c.ident[:, :], 0.0).then_inc(fixed, 1)
            nc.gpsimd.memset(c.earlier[:, :], 1.0).then_inc(fixed, 1)
            pool.wait_ge(fixed, 2)
            nc.gpsimd.affine_select(out=c.ident[:, :], in_=c.ident[:, :], compare_op=ALU.not_equal, fill=1.0, base=0,
                                    pattern=[[-1, P]], channel_multiplier=1)
            nc.gpsimd.affine_select(out=c.earlier[:, P:], in_=c.earlier[:, P:], compare_op=ALU.is_gt, fill=0.0, base=0,
                                    pattern=[[-1, P]], channel_multiplier=1)
            nc.gpsimd.iota(c.count_row[:, :], [[1, BLK]], base=0, channel_multiplier=0, allow_small_or_imprecise_dtypes=True)
            nc.gpsimd.iota(c.node_of[:, :], [[1, BLK]], base=0, channel_multiplier=BLK)
            nc.gpsimd.iota(c.slot_of[:, :], [[P, c.tiles]], base=0, channel_multiplier=1)


def degree_phase(nc, c):
    D, T = 4, c.tiles
    with Bench(nc, "deg") as w:
        part_i = w.sb("part_i", [P, 4, T], I32)
        part = w.sb("part", [P, 4, T])
        hot_hi = w.sb("hot_hi", [P, D, 2, P], BF16)
        hot_lo = w.sb("hot_lo", [P, D, 2, BLK], BF16)
        deg = w.sb("deg", [P, 2, BLK])
        least = w.sb("least", [P, 2, BLK])
        most = w.sb("most", [P, 2, BLK])
        power = w.sb("power", [P, BLK])
        valid = w.sb("valid", [P, BLK])
        weight = w.sb("weight", [P, BLK])
        row = w.sb("row", [P, BLK, 4])
        p_deg = [w.ps(f"p_deg{k}") for k in range(2)]
        split, hot, added, linked, powered, stored = (w.sem(n) for n in ("split", "hot", "added", "linked", "powered", "stored"))
        blk = w.block()

        @blk.vector
        def _(dve):
            for k, col in enumerate((c.src[:, :], c.dst[:, 1:T + 1])):
                nc.vector.tensor_scalar(part_i[:, 2 * k], col, 9, None, ALU.arith_shift_right)
                nc.vector.tensor_scalar(part_i[:, 2 * k + 1], col, BLK - 1, None, ALU.bitwise_and).then_inc(split, 1)
            nc.vector.tensor_tensor(c.apart[:, :], c.src[:, :], c.dst[:, 1:T + 1], ALU.not_equal)
            nc.vector.tensor_scalar(c.src_row[:, :], c.src[:, :], c.nodes - 1, None, ALU.min)
            nc.vector.tensor_scalar(c.dst_row[:, :], c.dst[:, 1:T + 1], c.nodes - 1, None, ALU.min)
            nc.vector.tensor_scalar(c.real[:, :], c.dst[:, 1:T + 1], c.nodes, None, ALU.is_lt)
            dve.wait_ge(split, 2)
            nc.vector.tensor_copy(part[:, :, :], part_i[:, :, :]).then_inc(split, 1)
            dve.wait_ge(split, 3)

            def one_hot(b, u, r):
                if reused(b, D):
                    dve.wait_ge(added, b - D + 1)
                at = bass.ds(b, 1)
                nc.vector.tensor_scalar(hot_hi[:, u, 0], c.count_row[:, 0:P], part[:, 0, at], c.apart[:, at], ALU.is_equal, ALU.mult)
                nc.vector.tensor_scalar(hot_lo[:, u, 0], c.count_row[:, :], part[:, 1, at], None, ALU.is_equal)
                nc.vector.tensor_scalar(hot_hi[:, u, 1], c.count_row[:, 0:P], part[:, 2, at], None, ALU.is_equal)
                nc.vector.tensor_scalar(hot_lo[:, u, 1], c.count_row[:, :], part[:, 3, at], None, ALU.is_equal).then_inc(hot, 1)
            pipeline(nc.vector, T, [(0, one_hot)], D)
            dve.wait_ge(added, T)
            for k in range(2):
                last = nc.vector.tensor_copy(deg[:, k], p_deg[k][:, :])
            last.then_inc(linked, 1)
            dve.wait_ge(linked, 1)
            nc.vector.tensor_scalar(least[:, :], deg[:, :], 1.0, None, ALU.max)
            nc.vector.tensor_scalar(most[:, :], deg[:, :], 1.0, None, ALU.min)
            nc.vector.tensor_scalar(valid[:, :], c.node_of[:, :], c.nodes, None, ALU.is_lt)
            nc.vector.tensor_copy(row[:, :, 3], deg[:, 1])
            nc.vector.memset(row[:, :, 2].bitcast(I32), FAR).then_inc(linked, 1)
            dve.wait_ge(linked, 2)
            nc.vector.tensor_scalar(weight[:, :], most[:, 1], -1.0, 1.0, ALU.mult, ALU.add).then_inc(linked, 1)
            nc.vector.reciprocal(row[:, :, 1], least[:, 1])
            dve.wait_ge(powered, 1)
            nc.vector.tensor_tensor(row[:, :, 0], power[:, :], most[:, 0], ALU.mult).then_inc(linked, 1)
            dve.wait_ge(linked, 4)
            nc.vector.tensor_tensor(weight[:, :], weight[:, :], valid[:, :], ALU.mult).then_inc(linked, 1)

        @blk.gpsimd
        def _(pool):
            pool.wait_ge(linked, 2)
            nc.gpsimd.tensor_tensor(power[:, :], least[:, 0], c.minus_half_wide[:, :], ALU.pow).then_inc(powered, 1)

        @blk.tensor
        def _(pe):
            def add(b, u, r):
                pe.wait_ge(hot, b + 1)
                for k in range(2):
                    last = nc.tensor.matmul(p_deg[k][:, :], hot_hi[:, u, k], hot_lo[:, u, k],
                                            start=isinstance(b, int) and b == 0, stop=isinstance(b, int) and b == T - 1)
                last.then_inc(added, 1)
            pipeline(nc.tensor, T, [(0, add)], D)

        @blk.sync
        def _(sp):
            sp.wait_ge(linked, 4)
            sp.dma_start(c.table.rearrange("(p n) k -> p n k", p=P), row[:, :, :]).then_inc(stored, 16)
            sp.wait_ge(linked, 5)
            sp.dma_start(c.weight_dram.rearrange("(p n) -> p n", p=P), weight[:, :]).then_inc(stored, 16)
            sp.wait_ge(stored, 32)
            sp.dma_start(c.node_weight[:, :].rearrange("p (b t) -> p b t", t=TPB),
                         c.weight_dram[0:c.node_blocks * BLK].rearrange("(b p t) -> p b t", p=P, t=TPB)).then_inc(stored, 16)
            sp.wait_ge(stored, 48)


def same_phase(nc, c, dst_line):
    D = 4
    with Bench(nc, "same") as w:
        line = w.sb("line", [P, D, P + BLK], I32)
        same = w.sb("same", [P, D, TPB, 3, P])
        match = w.sb("match", [P, D, TPB, 2, P])
        seen = w.sb("seen", [P, D, TPB, 2, P])
        before = w.sb("before", [P, D, TPB])
        away = w.sb("away", [P, D, TPB])
        loaded = w.sems("loaded", D)
        made, linked, placed = w.sem("made"), w.sem("linked"), w.sem("placed")
        stored = w.sems("stored", D)
        p_count = w.ps("p_count", (P, c.tiles))
        col = c.dst_value
        copied, counted = w.sem("copied"), w.sem("counted")
        blk = w.block()

        @blk.tensor
        def _(pe):
            def count(b, u, r):
                pe.wait_ge(made, b + 1)
                for t in range(TPB):
                    for v in range(3):
                        last = nc.tensor.matmul(p_count[:, bass.ds(b * TPB + t, 1)], same[:, u, t, v], c.ones[:, 0:1],
                                                start=(v == 0), stop=(v == 2))
                last.then_inc(counted, 1)
            pipeline(nc.tensor, c.edge_blocks, [(0, count)], D)

        @blk.scalar
        def _(act):
            act.wait_ge(counted, c.edge_blocks)
            nc.scalar.activation(c.window_count[:, :], p_count[:, :], ACT.Copy)

        @blk.sync
        def _(sp):
            def load(b, u, r):
                if reused(b, D):
                    sp.wait_ge(made, b - D + 1)
                    w.settle(sp)
                sp.dma_start(line[:, u], dst_line[:, bass.ds(b * BLK, P + BLK)].to_broadcast([P, P + BLK])).then_inc(loaded[u], 16)

            def store(b, u, r):
                sp.wait_ge(made, b + 1)
                w.settle(sp)
                sp.dma_start(c.same_dram[bass.ds(b * BLK, BLK), :].rearrange("(t p) d -> p t d", p=P),
                             same[:, u].rearrange("p t w e -> p t (w e)")).then_inc(stored[u], 16)
            pipeline(nc.sync, c.edge_blocks, [(0, load), (2, store)], D)
            for u in range(D):
                sp.wait_ge(stored[u], 16 * cdiv(c.edge_blocks - u, D))
                w.settle(sp)

        @blk.vector
        def _(dve):
            nc.vector.tensor_copy(col[:, :], c.dst[:, :]).then_inc(copied, 1)
            dve.wait_ge(copied, 1)

            def compare(b, u, r):
                if reused(b, D):
                    dve.wait_ge(stored[u], 16 * r)
                    dve.wait_ge(counted, b - D + 1)
                dve.wait_ge(loaded[u], 16 * (r + 1))
                for t in range(TPB):
                    for v in range(3):
                        last = nc.vector.tensor_scalar(same[:, u, t, v], line[:, u, (t + 1) * P:(t + 2) * P],
                                                       col[:, bass.ds(b * TPB + t + v, 1)], None, ALU.is_equal)
                last.then_inc(made, 1)
                for t in range(TPB):
                    last = nc.vector.tensor_scalar(flat(match[:, u, t]), line[:, u, t * P:(t + 2) * P],
                                                   col[:, bass.ds(b * TPB + t + 1, 1)], None, ALU.is_equal)
                last.then_inc(linked, 1)
                dve.wait_ge(linked, b * 4 + 1)
                nc.vector.tensor_tensor(seen[:, u].rearrange("p t k e -> p t (k e)"),
                                        match[:, u].rearrange("p t k e -> p t (k e)"),
                                        c.earlier.unsqueeze(1).to_broadcast([P, TPB, 2 * P]), ALU.mult).then_inc(linked, 1)
                dve.wait_ge(linked, b * 4 + 2)
                nc.vector.tensor_reduce(before[:, u], seen[:, u].rearrange("p t k e -> p t (k e)"), mybir.AxisListType.X, ALU.max).then_inc(linked, 1)
                dve.wait_ge(linked, b * 4 + 3)
                nc.vector.tensor_scalar(away[:, u], before[:, u], float(FAR), None, ALU.mult).then_inc(linked, 1)
                dve.wait_ge(linked, b * 4 + 4)
                nc.vector.tensor_tensor(c.write_at[:, bass.ds(b * TPB, TPB)], away[:, u],
                                        col[:, bass.ds(b * TPB + 1, TPB)], ALU.add)
            pipeline(nc.vector, c.edge_blocks, [(0, compare)], D)


def look_up_phase(nc, name, c, column, out):
    D = 4
    with Bench(nc, name) as w:
        got = w.sb("got", [P, D, TPB, 4])
        fetch = Fetch(w, "fetch", D, c.table, column, c.table.shape[0])
        taken = w.sem("taken")
        blk = w.block()

        @blk.gpsimd
        def _(pool):
            def bring(b, u, r):
                if reused(b, D):
                    pool.wait_ge(taken, b - D + 1)
                fetch.issue(nc, pool, got[:, u], b, u, r)
            pipeline(nc.gpsimd, c.edge_blocks, [(0, bring)], D)

        @blk.vector
        def _(dve):
            def take(b, u, r):
                fetch.arrived(dve, u, r)
                dve.wait_ge(fetch.copied, b + 1)
                nc.vector.tensor_copy(out[:, bass.ds(b * TPB, TPB), :].bitcast(I32), got[:, u].bitcast(I32)).then_inc(taken, 1)
            pipeline(nc.vector, c.edge_blocks, [(1, take)], D)


def scatter_check_phase(nc, c):
    with Bench(nc, "check") as w:
        differs = w.sb("differs", [P, c.tiles])
        some = w.sb("some", [P, 1])
        unit = w.sb("unit", [P, 3, P])
        p_some = w.ps("p_some")
        link, summed, rewritten = w.sem("link"), w.sem("summed"), w.sem("rewritten")
        blk = w.block()

        @blk.vector
        def _(dve):
            nc.vector.memset(unit[:, :, :], 0.0).then_inc(link, 1)
            nc.vector.tensor_tensor(differs[:, :], c.window_count[:, :], c.at_dst[:, :, 3], ALU.not_equal).then_inc(link, 1)
            dve.wait_ge(link, 2)
            nc.vector.tensor_copy(unit[:, 1], c.ident[:, :])
            nc.vector.tensor_reduce(some[:, :], differs[:, :], mybir.AxisListType.X, ALU.max).then_inc(link, 1)
            dve.wait_ge(summed, 1)
            nc.vector.tensor_copy(c.spread[:, :], p_some[0:1, 0:1]).then_inc(link, 1)

        @blk.tensor
        def _(pe):
            pe.wait_ge(link, 3)
            nc.tensor.matmul(p_some[0:1, 0:1], some[:, :], c.ones[:, 0:1], start=True, stop=True).then_inc(summed, 1)

        @blk.sync
        def _(sp):
            sp.wait_ge(link, 4)
            w.settle(sp)
            spread = sp.value_load(c.spread[0:1, 0:1])
            with sp.If(spread != 0):
                with sp.Fori(0, c.tiles) as j:
                    sp.dma_start(c.same_dram[bass.ds(j * P, P), :], unit[:, :, :].rearrange("p w e -> p (w e)")).then_inc(rewritten, 16)
                sp.wait_ge(rewritten, 16 * c.tiles)
                w.settle(sp)


def spread_sums_phase(nc, name, c):
    T = c.tiles
    with Bench(nc, name) as w:
        msg = w.sb("msg", [P, T, P])
        line = w.sb("line", [P, T * P], I32)
        pair = w.sb("pair", [P, P])
        total = w.sb("total", [P, P])
        p_total = w.ps("p_total", (P, P))
        loaded, paired, pair_free, summed, lifted, total_free = (
            w.sem(n) for n in ("loaded", "paired", "pair_free", "summed", "lifted", "total_free"))
        blk = w.block()

        @blk.sync
        def _(sp):
            spread = sp.value_load(c.spread[0:1, 0:1])
            with sp.If(spread != 0):
                sp.dma_start(msg[:, :, :], c.msg[P:P + T * P, :].rearrange("(t p) d -> p t d", p=P)).then_inc(loaded, 16)
                sp.dma_start(line[:, :], c.dst_line[:, P:P + T * P].to_broadcast([P, T * P])).then_inc(loaded, 16)
                sp.wait_ge(loaded, 32)
                w.settle(sp)
                with sp.Fori(0, T) as j:
                    sp.wait_ge(lifted, j + 2)
                    w.settle(sp)
                    sp.dma_start(c.msg[bass.ds(j * P + P, P), :], total[:, :]).then_inc(total_free, 16)
                sp.wait_ge(total_free, 16 * (T + 1))
                w.settle(sp)

        @blk.vector
        def _(dve):
            spread = dve.value_load(c.spread[0:1, 0:1])
            with dve.If(spread != 0):
                dve.sem_inc(pair_free, 1)
                dve.wait_ge(loaded, 32)
                with dve.Fori(0, T) as j:
                    with dve.Fori(0, T) as i:
                        dve.wait_ge(pair_free, j * T + i + 1)
                        w.settle(dve)
                        nc.vector.tensor_scalar(pair[:, :], line[:, bass.ds(j * P, P)], c.dst_value[:, bass.ds(i + 1, 1)],
                                                None, ALU.is_equal).then_inc(paired, 1)

        @blk.tensor
        def _(pe):
            spread = pe.value_load(c.spread[0:1, 0:1])
            with pe.If(spread != 0):
                with pe.Fori(0, T) as j:
                    pe.wait_ge(lifted, j + 1)
                    w.settle(pe)

                    def add(i, start, stop):
                        pe.wait_ge(paired, j * T + i + 1)
                        w.settle(pe)
                        return nc.tensor.matmul(p_total[:, :], pair[:, :], msg[:, bass.ds(i, 1)], start=start, stop=stop)

                    add(0, True, False).then_inc(pair_free, 1)
                    with pe.Fori(1, T - 1) as i:
                        add(i, False, False).then_inc(pair_free, 1)
                    add(T - 1, False, True).then_inc(pair_free, 1)
                    pe.wait_ge(pair_free, j * T + T + 1)
                    w.settle(pe)
                    pe.sem_inc(summed, 1)

        @blk.scalar
        def _(act):
            spread = act.value_load(c.spread[0:1, 0:1])
            with act.If(spread != 0):
                act.sem_inc(lifted, 1)
                act.sem_inc(total_free, 16)
                with act.Fori(0, T) as j:
                    act.wait_ge(summed, j + 1)
                    w.settle(act)
                    act.wait_ge(total_free, j * 16 + 16)
                    w.settle(act)
                    nc.scalar.activation(total[:, :], p_total[:, :], ACT.Copy).then_inc(lifted, 1)


def name_slots_phase(nc, c):
    D = 4
    with Bench(nc, "slots") as w:
        index = w.sb("index", [P, D, TPB], I32)
        row = w.sb("row", [P, D, TPB, 4])
        copied, filled = w.sem("copied"), w.sem("filled")
        done = w.sems("done", D)
        blk = w.block()

        @blk.vector
        def _(dve):
            nc.vector.tensor_copy(c.at_dst[:, :, 2].bitcast(I32), c.slot_of[:, :]).then_inc(filled, 1)

        @blk.gpsimd
        def _(pool):
            pool.wait_ge(filled, 1)
            w.settle(pool)
            spread = pool.value_load(c.spread[0:1, 0:1])

            def send(b, u, r, in_turn):
                if reused(b, D):
                    pool.wait_ge(done[u], 64 * r)
                    w.settle(pool)
                nc.gpsimd.tensor_copy(index[:, u], c.write_at[:, bass.ds(b * TPB, TPB)]).then_inc(copied, 1)
                nc.gpsimd.tensor_copy(row[:, u].bitcast(I32), c.at_dst[:, bass.ds(b * TPB, TPB), :].bitcast(I32)).then_inc(copied, 1)
                pool.wait_ge(copied, b * 2 + 2)
                w.settle(pool)
                for t in range(TPB):
                    nc.gpsimd.indirect_dma_start(
                        out=c.table, out_offset=bass.IndirectOffsetOnAxis(ap=index[:, u, t:t + 1], axis=0),
                        in_=row[:, u, t], in_offset=None, bounds_check=c.table.shape[0] - 1,
                        oob_is_err=False).then_inc(done[u], 16)
                    if in_turn:
                        pool.wait_ge(done[u], 64 * r + 16 * (t + 1))
                        w.settle(pool)
            with pool.If(spread == 0):
                pipeline(nc.gpsimd, c.edge_blocks, [(0, partial(send, in_turn=False))], D)
            with pool.If(spread != 0):
                pipeline(nc.gpsimd, c.edge_blocks, [(0, partial(send, in_turn=True))], D)
            for u in range(D):
                pool.wait_ge(done[u], 64 * cdiv(c.edge_blocks - u, D))


def columns_phase(nc, c):
    with Bench(nc, "cols") as w:
        t = w.sb("t", [P, c.tiles])
        n = w.sb("n", [P, c.tiles])
        link = w.sem("link")
        blk = w.block()

        @blk.vector
        def _(dve):
            nc.vector.tensor_tensor(t[:, :], c.at_dst[:, :, 0], c.at_src[:, :, 0], ALU.mult).then_inc(link, 1)
            nc.vector.tensor_tensor(c.slot_weight[:, :], c.at_dst[:, :, 1], c.real[:, :], ALU.mult)
            nc.vector.tensor_copy(c.mend_at[:, :], c.at_src[:, :, 2].bitcast(I32))
            nc.vector.tensor_tensor(c.b_last[:, :], c.rows["b_neigh"][:, :], c.rows["b_self"][:, :], ALU.add)
            dve.wait_ge(link, 1)
            nc.vector.tensor_tensor(n[:, :], t[:, :], c.apart[:, :], ALU.mult).then_inc(link, 1)
            dve.wait_ge(link, 2)
            nc.vector.tensor_scalar(c.minus_norm[:, :], n[:, :], -1.0, None, ALU.mult)


def gate_bias_phase(nc, c):
    with Bench(nc, "gbias") as w:
        part = w.sb("part", [P, 1])
        mean = w.sb("mean", [P, 1])
        p_g = w.ps("p_g")
        link, multiplied = w.sem("link"), w.sem("multiplied")
        blk = w.block()

        @blk.vector
        def _(dve):
            nc.vector.tensor_tensor(part[:, :], c.total_nodes[:, :], c.total_slots[:, :], ALU.add).then_inc(link, 1)
            dve.wait_ge(link, 1)
            nc.vector.tensor_scalar(mean[:, :], part[:, :], 1.0 / c.nodes, None, ALU.mult).then_inc(link, 1)
            dve.wait_ge(multiplied, 1)
            nc.vector.tensor_tensor(c.g_sum[:, :], p_g[:, 0:3], c.g_ih[:, :], ALU.add).then_inc(link, 1)
            dve.wait_ge(link, 3)
            nc.vector.tensor_tensor(c.g_all[:, :], c.g_sum[:, :], c.g_hh[:, :], ALU.add)

        @blk.tensor
        def _(pe):
            pe.wait_ge(link, 2)
            for g in range(3):
                last = nc.tensor.matmul(p_g[:, g:g + 1], c.w_ih[:, g * P:(g + 1) * P], mean[:, :], start=True, stop=True)
            last.then_inc(multiplied, 1)


def build(nc, args, out):
    c = Common()
    x = args["x"]
    c.nodes = x.shape[0]
    c.tiles = args["src_columns"].shape[1]
    c.edge_blocks = c.tiles // TPB
    c.node_blocks = cdiv(c.nodes, BLK)
    slots = c.tiles * P
    tail = (c.nodes - (c.node_blocks - 1) * BLK) // TPB
    assert c.nodes % TPB == 0 and c.node_blocks <= P and c.nodes + slots <= P * BLK
    tail = None if tail == P else tail

    def dram(name, shape, dt=F32):
        return nc.dram_tensor(name, list(shape), dt, kind="Internal").ap()

    edge_rows, node_rows = [slots, P], [c.node_blocks * BLK, P]
    s_x0, s_h1, s_x1, s_x2, s_x3 = (dram(f"s_{n}", edge_rows) for n in ("x0", "h1", "x1", "x2", "x3"))
    d_x0, d_h1, d_x1, d_x2, d_x3 = (dram(f"d_{n}", edge_rows) for n in ("x0", "h1", "x1", "x2", "x3"))
    n_h1, n_x1, n_x2, n_x3 = (dram(f"n_{n}", node_rows) for n in ("h1", "x1", "x2", "x3"))
    s_x2m = dram("s_x2m", edge_rows)
    c.msg = dram("msg", [slots + 2 * P, P])
    c.same_dram = dram("same_dram", [slots, 3 * P])
    c.table = dram("table", [P * BLK, 4])
    c.weight_dram = dram("weight_dram", [P * BLK])
    c.relation_row = args["relation_line"]
    c.dst_line = args["dst_line"]

    with ExitStack() as ctx:
        def sb(name, shape, dt=F32):
            return ctx.enter_context(nc.sbuf_tensor(name, shape, dt))

        T = c.tiles
        c.weights = {name: sb(f"w_{name}", [P, cols]) for name, cols in WEIGHTS}
        c.rows = {name: sb(f"r_{name}", [P, P]) for name in ROWS}
        c.w_ih, c.w_hh, c.w_rel, c.w_film = (c.weights[n] for n in ("w_ih", "w_hh", "w_rel", "w_film"))
        c.gamma, c.beta, c.b_msg = (c.rows[n][:, :] for n in ("gamma", "beta", "b_msg"))
        c.g_ih, c.g_hh, c.g_sum, c.g_all = (sb(n, [P, 3]) for n in ("g_ih", "g_hh", "g_sum", "g_all"))
        c.b_r, c.b_z, c.b_n, c.b_hn = c.g_all[:, 0:1], c.g_all[:, 1:2], c.g_sum[:, 2:3], c.g_hh[:, 2:3]
        c.b_last = sb("b_last", [P, P])
        c.ident, c.earlier_t = sb("ident", [P, P]), sb("earlier", [P, 2 * P])
        c.earlier = c.earlier_t[:, :]
        c.minus_half, c.minus_half_wide = sb("minus_half", [P, TPB]), sb("minus_half_wide", [P, BLK])
        c.count_row = sb("count_row", [P, BLK], F16)
        c.dst_value, c.window_count = sb("dst_value", [P, T + 2]), sb("window_count", [P, T])
        c.ones, c.spread = sb("ones", [P, 1]), sb("spread", [1, 1], I32)
        c.node_of = sb("node_of", [P, BLK], I32)
        c.slot_of, c.src = sb("slot_of", [P, T], I32), sb("src_t", [P, T], I32)
        c.dst = sb("dst_t", [P, T + 2], I32)
        c.src_row, c.dst_row, c.write_at, c.mend_at = (sb(n, [P, T], I32) for n in ("src_row", "dst_row", "write_at", "mend_at"))
        c.apart, c.real, c.minus_norm, c.slot_weight = (sb(n, [P, T]) for n in ("apart", "real", "minus_norm", "slot_weight"))
        c.at_dst, c.at_src = sb("at_dst", [P, T, 4]), sb("at_src", [P, T, 4])
        c.node_weight = sb("node_weight", [P, c.node_blocks * TPB])
        c.total_nodes, c.total_slots = sb("total_nodes", [P, 1]), sb("total_slots", [P, 1])
        W = {n: t[:, :] for n, t in c.weights.items()}
        R = {n: t[:, :] for n, t in c.rows.items()}
        dst_cols = c.dst[:, 1:T + 1]
        E, N = c.edge_blocks, c.node_blocks

        constants_phase(nc, c, args)
        degree_phase(nc, c)
        same_phase(nc, c, args["dst_line"])
        look_up_phase(nc, "atd", c, dst_cols, c.at_dst)
        scatter_check_phase(nc, c)
        name_slots_phase(nc, c)
        look_up_phase(nc, "ats", c, c.src, c.at_src)
        columns_phase(nc, c)

        row_stage(nc, "s0a", c, E, True, x, s_h1, gather=c.src_row, keep=s_x0, update=W["W1_0"], bias=R["b1"], relu=True,
                  message=W["W1_1"], message_scale=c.minus_norm, message_out=c.msg)
        spread_sums_phase(nc, "sum1", c)
        row_stage(nc, "d0a", c, E, True, x, d_h1, gather=c.dst_row, keep=d_x0, update=W["W1_0"], bias=R["b1"], relu=True,
                  sums=c.msg)
        row_stage(nc, "n0a", c, N, False, x, n_h1, update=W["W1_0"], bias=R["b1"], relu=True, tail_in=tail)
        row_stage(nc, "s0b", c, E, True, s_h1, s_x1, mend=(d_h1, c.mend_at), norm=False, extra=s_x0, update=W["W2_0"],
                  bias=R["b2"], relu=True, message=W["W2_1"], message_scale=c.minus_norm, message_out=c.msg)
        spread_sums_phase(nc, "sum2", c)
        row_stage(nc, "d0b", c, E, True, d_h1, d_x1, norm=False, extra=d_x0, update=W["W2_0"], bias=R["b2"], relu=True,
                  sums=c.msg)
        row_stage(nc, "n0b", c, N, False, n_h1, n_x1, norm=False, extra=x, update=W["W2_0"], bias=R["b2"], relu=True,
                  tail_in=tail)

        mean_stage(nc, "meann", c, N, False, n_x1, c.node_weight, c.total_nodes[:, :])
        mean_stage(nc, "meand", c, E, True, d_x1, c.slot_weight, c.total_slots[:, :])
        gate_bias_phase(nc, c)
        gru_stage(nc, "s1", c, E, True, s_x1, s_x2, mend=(d_x1, c.mend_at), message=W["W_msg"], message_out=c.msg)
        spread_sums_phase(nc, "sum3", c)
        gru_stage(nc, "d1", c, E, True, d_x1, d_x2, sums=c.msg)
        gru_stage(nc, "n1", c, N, False, n_x1, n_x2)

        row_stage(nc, "s2", c, E, True, s_x2, s_x3, mend=(d_x2, c.mend_at), keep=s_x2m, update=W["loop_w"], bias=R["h_bias"])
        film_stage(nc, "f2", c, E, s_x2m, d_x2, c.msg)
        spread_sums_phase(nc, "sum4", c)
        row_stage(nc, "d2", c, E, True, d_x2, d_x3, update=W["loop_w"], bias=R["h_bias"], sums=c.msg)
        row_stage(nc, "n2", c, N, False, n_x2, n_x3, update=W["loop_w"], bias=R["h_bias"])

        row_stage(nc, "s3", c, E, True, s_x3, None, mend=(d_x3, c.mend_at), message=W["W_neigh"], message_out=c.msg)
        spread_sums_phase(nc, "sum5", c)
        row_stage(nc, "n3", c, N, False, n_x3, out, update=W["W_self"], bias=c.b_last[:, :], tail_out=tail)
        row_stage(nc, "d3", c, E, True, d_x3, out, update=W["W_self"], bias=c.b_last[:, :], sums=c.msg, scatter=c.write_at)


def kernel(**inputs):
    import numpy as np
    import concourse.bacc as bacc
    from concourse import mybir as mb
    from concourse.bass_utils import run_bass_kernel_spmd

    a = {k: np.ascontiguousarray(v) for k, v in inputs.items()}
    nodes, edges = a["x"].shape[0], a["src"].shape[0]
    pad = cdiv(edges, BLK) * BLK - edges
    spare = np.arange(nodes, nodes + pad, dtype=np.int32)
    src = np.concatenate([a["src"], spare])
    dst = np.concatenate([a["dst"], spare])
    rel = np.concatenate([a["edge_type_4"], np.zeros(pad, np.int32)])
    C = np.ascontiguousarray
    arrays = {
        "x": a["x"],
        "src_columns": C(src.reshape(-1, P).T), "dst_columns": C(dst.reshape(-1, P).T),
        "dst_line": C(np.concatenate([np.full(P, -1, np.int32), dst]).reshape(1, -1)), "relation_line": C(rel.reshape(1, -1)),
        "W1_0": a["L0_gnn_W1_0"], "W1_1": a["L0_gnn_W1_1"], "W2_0": a["L0_gnn_W2_0"], "W2_1": a["L0_gnn_W2_1"],
        "b1": a["L0_gnn_b1"], "b2": a["L0_gnn_b2"],
        "W_msg": C(a["L1_gnn_W_msg"].T), "w_ih": C(a["L1_gnn_w_ih"].T), "w_hh": C(a["L1_gnn_w_hh"].T),
        "b_msg": a["L1_gnn_b_msg"], "b_ih": a["L1_gnn_b_ih"], "b_hh": a["L1_gnn_b_hh"],
        "gamma": a["L1_gnn_ln_gamma"], "beta": a["L1_gnn_ln_beta"],
        "w_rel": C(a["L2_gnn_W_rel"].transpose(1, 0, 2).reshape(P, -1)),
        "w_film": C(a["L2_gnn_film_rel"].transpose(1, 0, 2).reshape(P, -1)),
        "h_bias": a["L2_gnn_h_bias"], "loop_w": a["L2_gnn_loop_w"],
        "W_neigh": C(a["L3_gnn_W_neigh"].T), "W_self": C(a["L3_gnn_W_self"].T),
        "b_neigh": a["L3_gnn_b_neigh"], "b_self": a["L3_gnn_b_self"],
    }
    nc = bacc.Bacc("TRN2", target_bir_lowering=False, num_devices=1)
    args = {k: nc.dram_tensor(f"in_{k}", v.shape, mb.dt.from_np(v.dtype), kind="ExternalInput").ap() for k, v in arrays.items()}
    out = nc.dram_tensor("out", (nodes, P), mb.dt.float32, kind="ExternalOutput").ap()
    build(nc, args, out)
    r = run_bass_kernel_spmd(nc, [{f"in_{k}": v for k, v in arrays.items()}], core_ids=[0])
    return r.results[0]["out"]
```

```python
from contextlib import ExitStack
from functools import partial

import concourse.bass as bass
from concourse import mybir

F32 = mybir.dt.float32
F16 = mybir.dt.float16
BF16 = mybir.dt.bfloat16
I32 = mybir.dt.int32
ALU = mybir.AluOpType
ACT = mybir.ActivationFunctionType

P = 128
TPB = 4
BLK = P * TPB
LN_EPS = 1e-5
FAR = 1 << 22
NREL = 4


def cdiv(a, b):
    return -(-a // b)


def pipeline(eng, count, steps, depth):
    most = max(lag for lag, _ in steps)

    def position(i):
        for lag, fn in steps:
            b = i - lag
            if 0 <= b < count:
                fn(b, b % depth, b // depth)

    peeled = (1 + cdiv(max(most, 1), depth)) * depth
    end = (count - 1) // depth * depth
    if end <= peeled:
        for i in range(count + most):
            position(i)
        return
    for i in range(peeled):
        position(i)
    with eng.Fori(peeled // depth, end // depth) as n:
        for k in range(depth):
            for lag, fn in steps:
                fn(n * depth + (k - lag), (k - lag) % depth, n + (k - lag) // depth)
    for i in range(end, count + most):
        position(i)


def in_turns(first, second):
    return [step for pair in zip(first, second) for step in pair]


def reused(b, slots):
    return not isinstance(b, int) or b >= slots


class Bench:

    def __init__(self, nc, name):
        self.nc, self.name, self.ctx, self.used = nc, name, ExitStack(), []

    def __enter__(self):
        self.ctx.__enter__()
        return self

    def __exit__(self, *a):
        self.ctx.__exit__(*a)
        self.nc.clear_and_free_semaphores(self.used)
        self.nc.all_engine_barrier()

    def sb(self, name, shape, dt=F32):
        return self.ctx.enter_context(self.nc.sbuf_tensor(f"{self.name}_{name}", shape, dt))

    def ps(self, name, shape=(P, BLK), dt=F32):
        return self.ctx.enter_context(self.nc.psum_tensor(f"{self.name}_{name}", list(shape), dt))

    def sem(self, name):
        self.used.append(self.nc.alloc_semaphore(f"{self.name}_{name}"))
        return self.used[-1]

    def sems(self, name, n):
        return [self.sem(f"{name}{i}") for i in range(n)]

    def settle(self, eng):
        eng.sem_inc(self.settled, 1)

    def block(self):
        self.settled = self.sem("settled")
        return self.ctx.enter_context(self.nc.Block())


def flat(ap):
    return ap.rearrange("p t d -> p (t d)")


def tiles(ap):
    return ap.rearrange("p (t d) -> p t d", t=TPB)


def over_tiles(row):
    return row.unsqueeze(1).to_broadcast([P, TPB, P])


def block_rows(table, b, slots, tail=None):
    rows = table[bass.ds(b * BLK, BLK), :] if tail is None else table[bass.ds(b * BLK, tail * TPB), :]
    return rows.rearrange("(t p) d -> p t d", t=TPB) if slots else rows.rearrange("(p t) d -> p t d", t=TPB)


class Norm:

    def __init__(self, w, name, depth):
        self.stats = w.sb(f"{name}_stats", [P, depth, TPB, 6])
        self.sums = w.sb(f"{name}_sums", [P, depth, TPB, 3])
        self.diff = w.sb(f"{name}_diff", [P, depth, TPB])
        self.diff2 = w.sb(f"{name}_diff2", [P, depth, TPB])
        self.vare = w.sb(f"{name}_vare", [P, depth, TPB])
        self.minus_mean = w.sb(f"{name}_minus_mean", [P, depth, TPB])
        self.var = w.sb(f"{name}_var", [P, depth, TPB])
        self.rstd = w.sb(f"{name}_rstd", [P, depth, TPB])
        self.shift = w.sb(f"{name}_shift", [P, depth, TPB])
        self.link = w.sem(f"{name}_link")
        self.var_ready = w.sem(f"{name}_var_ready")
        self.powered = w.sem(f"{name}_powered")
        self.rstd_ready = w.sem(f"{name}_rstd_ready")

    def statistics(self, nc, dve, x, b, u):
        for step in range(4):
            self.statistics_step(step, nc, dve, x, b, u)

    def statistics_step(self, step, nc, dve, x, b, u):
        if step == 0:
            for t in range(TPB):
                last = nc.vector.bn_stats(self.stats[:, u, t], x[:, t])
            last.then_inc(self.link, 1)
        elif step == 1:
            dve.wait_ge(self.link, b * 3 + 1)
            nc.vector.tensor_tensor(self.sums[:, u], self.stats[:, u, :, 0:3], self.stats[:, u, :, 3:6], ALU.add)
            nc.vector.tensor_tensor(self.diff[:, u], self.stats[:, u, :, 1], self.stats[:, u, :, 4],
                                    ALU.subtract).then_inc(self.link, 1)
        elif step == 2:
            dve.wait_ge(self.link, b * 3 + 2)
            nc.vector.scalar_tensor_tensor(self.diff2[:, u], self.diff[:, u], 0.25, self.diff[:, u], ALU.mult, ALU.mult)
            nc.vector.tensor_scalar(self.minus_mean[:, u], self.sums[:, u, :, 1], -0.5, None, ALU.mult)
            nc.vector.tensor_scalar(self.vare[:, u], self.sums[:, u, :, 2], 1.0 / P, LN_EPS, ALU.mult,
                                    ALU.add).then_inc(self.link, 1)
        else:
            dve.wait_ge(self.link, b * 3 + 3)
            nc.vector.tensor_tensor(self.var[:, u], self.vare[:, u], self.diff2[:, u], ALU.add).then_inc(self.var_ready, 1)

    def power(self, nc, pool, minus_half, b, u):
        pool.wait_ge(self.var_ready, b + 1)
        nc.gpsimd.tensor_tensor(self.rstd[:, u], self.var[:, u], minus_half[:, :], ALU.pow).then_inc(self.powered, 1)

    def shifts(self, nc, pool, b, u):
        pool.wait_ge(self.powered, b + 1)
        nc.gpsimd.tensor_tensor(self.shift[:, u], self.minus_mean[:, u], self.rstd[:, u], ALU.mult).then_inc(self.rstd_ready, 1)

    def inverse(self, nc, pool, minus_half, b, u):
        self.power(nc, pool, minus_half, b, u)
        self.shifts(nc, pool, b, u)

    def apply(self, nc, act, out, x, b, u, function=ACT.Relu):
        act.wait_ge(self.rstd_ready, b + 1)
        for t in range(TPB):
            last = nc.scalar.activation(out[:, t], x[:, t], function, bias=self.shift[:, u, t:t + 1],
                                        scale=self.rstd[:, u, t:t + 1])
        return last


class Fetch:

    def __init__(self, w, name, depth, table, column, limit):
        self.index = w.sb(f"{name}_index", [P, depth, TPB], I32)
        self.copied = w.sem(f"{name}_copied")
        self.bench = w
        self.done = w.sems(f"{name}_done", depth)
        self.table, self.column, self.limit = table, column, limit

    def issue(self, nc, pool, out, b, u, r, half=None):
        if half != 1:
            self.name_rows(nc, pool, b, u, r)
        for t in halves(half):
            nc.gpsimd.indirect_dma_start(
                out=out[:, t], out_offset=None, in_=self.table,
                in_offset=bass.IndirectOffsetOnAxis(ap=self.index[:, u, t:t + 1], axis=0),
                bounds_check=self.limit - 1, oob_is_err=False).then_inc(self.done[u], 16)

    def name_rows(self, nc, pool, b, u, r):
        w = self.bench
        if reused(b, self.index.shape[1]):
            pool.wait_ge(self.done[u], 64 * r)
            w.settle(pool)
        nc.gpsimd.tensor_copy(self.index[:, u], self.column[:, bass.ds(b * TPB, TPB)]).then_inc(self.copied, 1)
        pool.wait_ge(self.copied, b + 1)
        w.settle(pool)

    def arrived(self, eng, u, r):
        eng.wait_ge(self.done[u], 64 * (r + 1))


def row_stage(nc, name, c, blocks, slots, source, out, *, gather=None, mend=None, keep=None, norm=True, extra=None,
              sums=None, update=None, message=None, message_scale=None, message_out=None,
              bias=None, relu=False, scatter=None, mean=None):
    D = 6 if slots else 8
    with Bench(nc, name) as w:
        x = w.sb("x", [P, D, TPB, P])
        xr = w.sb("xr", [P, D, TPB, P]) if extra is not None else x
        hn = w.sb("hn", [P, D, TPB, P]) if norm else x
        hT = w.sb("hT", [P, D, BLK])
        y = w.sb("y", [P, D, TPB, P])
        msg = w.sb("msg", [P, D, TPB, P]) if message is not None else None
        window = w.sb("window", [P, D, TPB + 2, P]) if sums is not None else None
        same = w.sb("same", [P, D, TPB, 3, P]) if sums is not None else None
        p_t = [w.ps(f"p_t{i}") for i in range(2)]
        p_y = [w.ps(f"p_y{i}") for i in range(2)]
        p_m = [w.ps(f"p_m{i}") for i in range(2)]
        ln = Norm(w, "ln", D) if norm else None
        if mean is not None:
            h2 = w.sb("h2", [P, D, TPB, P])
            acc = w.ps("acc")
            ln2 = Norm(w, "ln2", D)
            h2_ready, summed = w.sem("h2_ready"), w.sem("summed")
        fetch = None
        if gather is not None:
            fetch = Fetch(w, "gather", D, source, gather, source.shape[0])
        if mend is not None:
            fetch = Fetch(w, "mend", D, mend[0], mend[1], mend[0].shape[0])
        loads = (gather is None) + (extra is not None) + 2 * (sums is not None)
        loaded = w.sems("loaded", D)
        norm_ready = w.sem("norm_ready")
        hT_ready = w.sem("hT_ready")
        turned = w.sem("turned")
        multiplied = w.sem("multiplied")
        y_ready = w.sem("y_ready")
        msg_ready = w.sem("msg_ready")
        y_stored = w.sems("y_stored", D)
        msg_stored = w.sems("msg_stored", D)
        kept = w.sems("kept", D)
        named = w.sem("named")
        to_rows = w.sb("to_rows", [P, D, TPB], I32)
        blk = w.block()

        engines = {}

        def input_ready(eng, u, r):
            if loads:
                eng.wait_ge(loaded[u], 16 * loads * (r + 1))
                if eng is engines.get("sync"):
                    w.settle(eng)
            if fetch is not None:
                fetch.arrived(eng, u, r)

        def slot_free(eng, b, u, r):
            if reused(b, D):
                if update is not None:
                    eng.wait_ge(y_ready, b - D + 1)
                    if eng is engines.get("sync"):
                        w.settle(eng)
                if message is not None:
                    eng.wait_ge(msg_ready, b - D + 1)
                    if eng is engines.get("sync"):
                        w.settle(eng)
                if keep is not None:
                    eng.wait_ge(kept[u], 16 * r)

        ahead = 2 if fetch is not None else 0

        @blk.sync
        def _(sp):
            engines["sync"] = sp

            def load(b, u, r):
                if loads:
                    slot_free(sp, b, u, r)
                    w.settle(sp)
                if gather is None:
                    sp.dma_start(x[:, u], block_rows(source, b, slots)).then_inc(loaded[u], 16)
                if extra is not None:
                    sp.dma_start(xr[:, u], block_rows(extra, b, slots)).then_inc(loaded[u], 16)
                if sums is not None:
                    sp.dma_start(window[:, u], sums[bass.ds(b * BLK, BLK + 2 * P), :].rearrange(
                        "(t p) d -> p t d", p=P)).then_inc(loaded[u], 16)
                    sp.dma_start(same[:, u].rearrange("p t w e -> p t (w e)"),
                                 c.same_dram[bass.ds(b * BLK, BLK), :].rearrange(
                                     "(t p) d -> p t d", p=P)).then_inc(loaded[u], 16)

            def store(b, u, r):
                if update is not None and scatter is None:
                    sp.wait_ge(y_ready, b + 1)
                    w.settle(sp)
                    sp.dma_start(block_rows(out, b, slots), y[:, u]).then_inc(y_stored[u], 16)
                if message is not None:
                    sp.wait_ge(msg_ready, b + 1)
                    w.settle(sp)
                    sp.dma_start(block_rows(message_out[P:, :], b, True), msg[:, u]).then_inc(msg_stored[u], 16)
            def store_input(b, u, r):
                input_ready(sp, u, r)
                w.settle(sp)
                sp.dma_start(block_rows(keep, b, True), x[:, u]).then_inc(kept[u], 16)

            pipeline(nc.sync, blocks, [(0, load)] + ([(ahead + 1, store_input)] if keep is not None else []) +
                     [(ahead + 6, store)], D)
            for u in range(D):
                n = cdiv(blocks - u, D)
                if update is not None and scatter is None:
                    sp.wait_ge(y_stored[u], 16 * n)
                    w.settle(sp)
                if message is not None:
                    sp.wait_ge(msg_stored[u], 16 * n)
                    w.settle(sp)
                if keep is not None:
                    sp.wait_ge(kept[u], 16 * n)
                    w.settle(sp)

        @blk.gpsimd
        def _(pool):
            if scatter is not None:
                spread = pool.value_load(c.spread[0:1, 0:1])

            def bring(b, u, r):
                if gather is not None:
                    slot_free(pool, b, u, r)
                else:
                    pool.wait_ge(loaded[u], 16 * loads * (r + 1))
                fetch.issue(nc, pool, x[:, u], b, u, r)

            def inverse(b, u, r):
                ln.inverse(nc, pool, c.minus_half, b, u)

            def inverse2(b, u, r):
                ln2.inverse(nc, pool, c.minus_half, b, u)

            def spread_out(b, u, r, in_turn):
                if reused(b, D):
                    pool.wait_ge(y_stored[u], 64 * r)
                    w.settle(pool)
                nc.gpsimd.tensor_copy(to_rows[:, u], scatter[:, bass.ds(b * TPB, TPB)]).then_inc(named, 1)
                pool.wait_ge(named, b + 1)
                w.settle(pool)
                pool.wait_ge(y_ready, b + 1)
                w.settle(pool)
                for t in range(TPB):
                    nc.gpsimd.indirect_dma_start(
                        out=out, out_offset=bass.IndirectOffsetOnAxis(ap=to_rows[:, u, t:t + 1], axis=0),
                        in_=y[:, u, t], in_offset=None, bounds_check=out.shape[0] - 1,
                        oob_is_err=False).then_inc(y_stored[u], 16)
                    if in_turn:
                        pool.wait_ge(y_stored[u], 64 * r + 16 * (t + 1))
                        w.settle(pool)

            steps = []
            if fetch is not None:
                steps.append((0, bring))
            if norm:
                steps.append((ahead, inverse))
            if scatter is not None:
                with pool.If(spread == 0):
                    pipeline(nc.gpsimd, blocks, steps + [(ahead + 4, partial(spread_out, in_turn=False))], D)
                with pool.If(spread != 0):
                    pipeline(nc.gpsimd, blocks, steps + [(ahead + 4, partial(spread_out, in_turn=True))], D)
            else:
                if mean is not None:
                    steps.append((ahead + 4, inverse2))
                if steps:
                    pipeline(nc.gpsimd, blocks, steps, D)
            if scatter is not None:
                for u in range(D):
                    pool.wait_ge(y_stored[u], 64 * cdiv(blocks - u, D))

        @blk.vector
        def _(dve):
            def statistics(b, u, r):
                input_ready(dve, u, r)
                ln.statistics(nc, dve, x[:, u], b, u)

            def finish(b, u, r):
                dve.wait_ge(multiplied, b + 1)
                if update is not None:
                    if reused(b, D):
                        dve.wait_ge(y_stored[u], (64 if scatter is not None else 16) * r)
                        if mean is not None:
                            dve.wait_ge(h2_ready, b - D + 1)
                    if relu and extra is not None:
                        op = nc.vector.scalar_tensor_tensor(flat(y[:, u]), p_y[u % 2][:, :], 0.0, flat(xr[:, u]), ALU.max, ALU.add)
                    elif relu:
                        op = nc.vector.tensor_scalar(flat(y[:, u]), p_y[u % 2][:, :], 0.0, None, ALU.max)
                    else:
                        op = nc.vector.tensor_tensor(y[:, u], tiles(p_y[u % 2][:, :]), xr[:, u], ALU.add)
                    op.then_inc(y_ready, 1)

            def statistics2(b, u, r):
                dve.wait_ge(y_ready, b + 1)
                ln2.statistics(nc, dve, y[:, u], b, u)

            steps = [(ahead + 4, finish)]
            if norm:
                steps.append((ahead, statistics))
            if mean is not None:
                steps.append((ahead + 4, statistics2))
            pipeline(nc.vector, blocks, steps, D)

        @blk.tensor
        def _(pe):
            def turn(b, u, r):
                if norm:
                    pe.wait_ge(norm_ready, b + 1)
                else:
                    input_ready(pe, u, r)
                if reused(b, 2):
                    pe.wait_ge(hT_ready, b - 1)
                for t in range(TPB):
                    last = nc.tensor.transpose(p_t[u % 2][:, t * P:(t + 1) * P], hn[:, u, t], c.ident[:, :])
                last.then_inc(turned, 1)

            def multiply(b, u, r):
                pe.wait_ge(hT_ready, b + 1)
                if reused(b, 2):
                    if update is not None:
                        pe.wait_ge(y_ready, b - 1)
                    if message is not None:
                        pe.wait_ge(msg_ready, b - 1)
                if sums is not None:
                    pe.wait_ge(loaded[u], 16 * loads * (r + 1))
                for t in range(TPB):
                    left = hT[:, u, t * P:(t + 1) * P]
                    if update is not None:
                        to = p_y[u % 2][:, t * P:(t + 1) * P]
                        nc.tensor.matmul(to, c.first_row[:, :], bias, start=True, stop=False)
                        if sums is not None:
                            for v in range(3):
                                nc.tensor.matmul(to, same[:, u, t, v], window[:, u, t + v], start=False, stop=False)
                        last = nc.tensor.matmul(to, left, update, start=False, stop=True)
                    if message is not None:
                        last = nc.tensor.matmul(p_m[u % 2][:, t * P:(t + 1) * P], left, message, start=True, stop=True)
                last.then_inc(multiplied, 1)

            def sum_up(b, u, r):
                pe.wait_ge(h2_ready, b + 1)
                for t in range(TPB):
                    last = nc.tensor.matmul(acc[:, 0:1], h2[:, u, t], mean[0][:, bass.ds(b * TPB + t, 1)],
                                            start=isinstance(b, int) and b == 0 and t == 0,
                                            stop=isinstance(b, int) and b == blocks - 1 and t == TPB - 1)
                last.then_inc(summed, 1)

            pipeline(nc.tensor, blocks, [(ahead + 2, turn), (ahead + 3, multiply)] +
                     ([(ahead + 6, sum_up)] if mean is not None else []), D)

        @blk.scalar
        def _(act):
            def lift(b, u, r):
                act.wait_ge(turned, b + 1)
                nc.scalar.activation(hT[:, u], p_t[u % 2][:, :], ACT.Copy).then_inc(hT_ready, 1)

            def send(b, u, r):
                act.wait_ge(multiplied, b + 1)
                if reused(b, D):
                    act.wait_ge(msg_stored[u], 16 * r)
                if message_scale is not None:
                    for t in range(TPB):
                        last = nc.scalar.activation(msg[:, u, t], p_m[u % 2][:, t * P:(t + 1) * P], ACT.Copy,
                                                    scale=message_scale[:, bass.ds(b * TPB + t, 1)])
                else:
                    last = nc.scalar.activation(flat(msg[:, u]), p_m[u % 2][:, :], ACT.Copy)
                last.then_inc(msg_ready, 1)

            def apply(b, u, r):
                input_ready(act, u, r)
                ln.apply(nc, act, hn[:, u], x[:, u], b, u).then_inc(norm_ready, 1)

            def apply2(b, u, r):
                if reused(b, D):
                    act.wait_ge(summed, b - D + 1)
                ln2.apply(nc, act, h2[:, u], y[:, u], b, u).then_inc(h2_ready, 1)

            steps = [(ahead + 3, lift)]
            if message is not None:
                steps.append((ahead + 4, send))
            if norm:
                steps.append((ahead + 1, apply))
            if mean is not None:
                steps.append((ahead + 5, apply2))
            pipeline(nc.scalar, blocks, steps, D)
            if mean is not None:
                act.wait_ge(summed, blocks)
                nc.scalar.activation(mean[1], acc[:, 0:1], ACT.Copy)


def gru_stage(nc, name, c, blocks, slots, source, out, *, mend=None, sums=None, message=None, message_out=None):
    D, H = 8, 4
    with Bench(nc, name) as w:
        x = w.sb("x", [P, D, TPB, P])
        xb = w.sb("xb", [P, D, TPB, P])
        hn = w.sb("hn", [P, H, TPB, P])
        hT = w.sb("hT", [P, H, BLK])
        rT = w.sb("rT", [P, 2, BLK])
        zT = w.sb("zT", [P, H, BLK])
        uT = w.sb("uT", [P, 2, BLK])
        nT = w.sb("nT", [P, H, BLK])
        sT = w.sb("sT", [P, 2, BLK]) if sums is not None or message is not None else None
        dT = w.sb("dT", [P, 2, BLK])
        eT = w.sb("eT", [P, 2, BLK])
        yn = w.sb("yn", [P, 2, TPB, P])
        yg = w.sb("yg", [P, 2, TPB, P])
        y = w.sb("y", [P, 2, TPB, P])
        if message is not None:
            msg = w.sb("msg", [P, H, TPB, P])
            p_m = w.ps("p_m")
        if sums is not None:
            window = w.sb("window", [P, H, TPB + 2, P])
            same = w.sb("same", [P, H, TPB, 3, P])
            tT = w.sb("tT", [P, D, BLK])
            vT = w.sb("vT", [P, 2, BLK])
            yt = w.sb("yt", [P, 2, TPB, P])
            p_s = w.ps("p_s")
            p_q = w.ps("p_q")
            p_i = w.ps("p_i")
        G = 2 if message is None and sums is None else 1
        p_t, p_n = w.ps("p_t"), w.ps("p_n")
        p_r, p_z, p_y = ([w.ps(f"{n}{i}") for i in range(G)] for n in ("p_r", "p_z", "p_y"))
        ln, ln2 = Norm(w, "ln", D), Norm(w, "ln2", D)
        fetch = Fetch(w, "mend", D, mend[0], mend[1], mend[0].shape[0]) if mend is not None else None
        loaded = w.sems("loaded", D)
        loaded_sums = w.sems("loaded_sums", H)
        names = ("norm_ready", "turned", "hT_ready", "gates", "sig", "u_ready", "n_ready", "d_ready", "e_ready", "s_ready",
                 "back", "yn_ready", "yg_ready", "y_ready", "xb_ready", "summed", "tT_ready", "tR_ready",
                 "msg_mult", "msg_ready", "v_ready", "yt_ready")
        s = {n: w.sem(n) for n in names}
        stored = w.sems("stored", 2)
        msg_stored = w.sems("msg_stored", H)
        blk = w.block()
        ahead = 2 if fetch is not None else 0
        pool_helps = fetch is None
        more = 1 if pool_helps else 0
        add_turned = sums is None and message is None

        def input_ready(eng, u, r):
            eng.wait_ge(loaded[u], 16 * (r + 1))
            if fetch is not None:
                fetch.arrived(eng, u, r)

        @blk.sync
        def _(sp):
            def load(b, u, r):
                if reused(b, D):
                    sp.wait_ge(s["xb_ready"], b - D + 1)
                    w.settle(sp)
                    sp.wait_ge(s["norm_ready"], b - D + 1)
                    w.settle(sp)
                sp.dma_start(x[:, u], block_rows(source, b, slots)).then_inc(loaded[u], 16)

            def load_sums(b, u, r):
                if reused(b, H):
                    sp.wait_ge(s["summed"], b - H + 1)
                    w.settle(sp)
                sp.dma_start(window[:, u % H], sums[bass.ds(b * BLK, BLK + 2 * P), :].rearrange(
                    "(t p) d -> p t d", p=P)).then_inc(loaded_sums[u % H], 16)
                sp.dma_start(same[:, u % H].rearrange("p t w e -> p t (w e)"),
                             c.same_dram[bass.ds(b * BLK, BLK), :].rearrange(
                                 "(t p) d -> p t d", p=P)).then_inc(loaded_sums[u % H], 16)

            def store(b, u, r):
                sp.wait_ge(s["y_ready"], b + 1)
                w.settle(sp)
                sp.dma_start(block_rows(out, b, slots), y[:, u % 2]).then_inc(stored[u % 2], 16)

            def store_msg(b, u, r):
                sp.wait_ge(s["msg_ready"], b + 1)
                w.settle(sp)
                sp.dma_start(block_rows(message_out[P:, :], b, True), msg[:, u % H]).then_inc(msg_stored[u % H], 16)

            steps = [(0, load)]
            if sums is not None:
                steps.append((1, load_sums))
            if message is not None:
                steps.append((ahead + 4, store_msg))
            steps.append((ahead + more + 9, store))
            pipeline(nc.sync, blocks, steps, D)
            for u in range(2):
                sp.wait_ge(stored[u], 16 * cdiv(blocks - u, 2))
                w.settle(sp)
            if message is not None:
                for u in range(H):
                    sp.wait_ge(msg_stored[u], 16 * cdiv(blocks - u, H))
                    w.settle(sp)

        @blk.gpsimd
        def _(pool):
            def bring(b, u, r):
                pool.wait_ge(loaded[u], 16 * (r + 1))
                fetch.issue(nc, pool, x[:, u], b, u, r)

            def power(b, u, r):
                ln.power(nc, pool, c.minus_half, b, u)

            def with_beta(b, u, r):
                if reused(b, D):
                    pool.wait_ge(s["y_ready"], b - D + 1)
                input_ready(pool, u, r)
                nc.gpsimd.tensor_tensor(xb[:, u], x[:, u], over_tiles(c.beta), ALU.add).then_inc(s["xb_ready"], 1)

            def power2(b, u, r):
                ln2.power(nc, pool, c.minus_half, b, u)

            def shifts2(b, u, r):
                ln2.shifts(nc, pool, b, u)

            def shifts(b, u, r):
                ln.shifts(nc, pool, b, u)

            def difference(b, u, r):
                pool.wait_ge(s["n_ready"], b + 1)
                nc.gpsimd.tensor_tensor(dT[:, u % 2], hT[:, u % H], nT[:, u % H], ALU.subtract).then_inc(s["d_ready"], 1)

            steps = [(ahead + more + 6, power2), (ahead + more + 6, shifts2), (ahead + 1, with_beta)]
            if fetch is not None:
                steps.append((0, bring))
            steps.append((ahead, power))
            if pool_helps:
                steps.append((ahead + 5, difference))
            steps.append((ahead, shifts))
            pipeline(nc.gpsimd, blocks, steps, D)

        @blk.vector
        def _(dve):
            def statistics(b, u, r):
                input_ready(dve, u, r)
                ln.statistics(nc, dve, x[:, u], b, u)

            def step(b, u, r):
                v, k = u % 2, u % H
                dve.wait_ge(s["sig"], b + 1)
                if reused(b, 2):
                    dve.wait_ge(s["n_ready"], b - 1)
                nc.vector.scalar_tensor_tensor(uT[:, v], p_n[:, :], c.b_hn, rT[:, v], ALU.add, ALU.mult).then_inc(s["u_ready"], 1)
                if sums is not None:
                    dve.wait_ge(s["u_ready"], b + 1)
                    nc.vector.tensor_tensor(vT[:, v], p_i[:, :], uT[:, v], ALU.add).then_inc(s["v_ready"], 1)

            def blend(b, u, r):
                v, k = u % 2, u % H
                dve.wait_ge(s["n_ready"], b + 1)
                if not pool_helps:
                    nc.vector.tensor_tensor(dT[:, v], hT[:, k], nT[:, u % H], ALU.subtract).then_inc(s["d_ready"], 1)
                dve.wait_ge(s["d_ready"], b + 1)
                if reused(b, 2):
                    dve.wait_ge(s["back"], b - 1)
                nc.vector.tensor_tensor(eT[:, v], dT[:, v], zT[:, k], ALU.mult).then_inc(s["e_ready"], 1)
                if not add_turned:
                    dve.wait_ge(s["e_ready"], b + 1)
                    nc.vector.tensor_tensor(sT[:, v], eT[:, v], nT[:, k], ALU.add).then_inc(s["s_ready"], 1)

            def send(b, u, r):
                dve.wait_ge(s["msg_mult"], b + 1)
                if reused(b, H):
                    if isinstance(b, int):
                        dve.wait_ge(msg_stored[u % H], 16 * (b // H))
                    else:
                        dve.wait_ge(msg_stored[u % H], r * (16 * (D // H)) + 16 * (u // H))
                nc.vector.tensor_tensor(msg[:, u % H], tiles(p_m[:, :]), over_tiles(c.b_msg), ALU.add).then_inc(s["msg_ready"], 1)

            def statistics2(b, u, r):
                dve.wait_ge(s["back"], b + 1)
                ln2.statistics(nc, dve, tiles(p_y[u % G][:, :]), b, u)

            def finish(b, u, r):
                v = u % 2
                dve.wait_ge(s["yn_ready"], b + 1)
                nc.vector.tensor_tensor(yg[:, v], yn[:, v], over_tiles(c.gamma), ALU.mult).then_inc(s["yg_ready"], 1)
                dve.wait_ge(s["yg_ready"], b + 1)
                left = yg
                if sums is not None:
                    dve.wait_ge(s["tR_ready"], b + 1)
                    nc.vector.tensor_tensor(yt[:, v], yg[:, v], tiles(p_q[:, :]), ALU.add).then_inc(s["yt_ready"], 1)
                    dve.wait_ge(s["yt_ready"], b + 1)
                    left = yt
                dve.wait_ge(s["xb_ready"], b + 1)
                if reused(b, 2):
                    if isinstance(b, int):
                        dve.wait_ge(stored[v], 16 * (b // 2))
                    else:
                        dve.wait_ge(stored[v], r * (16 * (D // 2)) + 16 * (u // 2))
                nc.vector.tensor_tensor(y[:, v], left[:, v], xb[:, u], ALU.add).then_inc(s["y_ready"], 1)

            steps = [(ahead + more + 6, statistics2), (ahead + more + 5, blend), (ahead + 4, step)]
            if message is not None:
                steps.append((ahead + 4, send))
            steps.append((ahead, statistics))
            steps.insert(0 if sums is not None else len(steps), (ahead + more + 7, finish))
            pipeline(nc.vector, blocks, steps, D)

        @blk.tensor
        def _(pe):
            def turn(b, u, r):
                pe.wait_ge(s["norm_ready"], b + 1)
                if reused(b, 1):
                    pe.wait_ge(s["hT_ready"], b)
                for t in range(TPB):
                    last = nc.tensor.transpose(p_t[:, t * P:(t + 1) * P], hn[:, u % H, t], c.ident[:, :])
                last.then_inc(s["turned"], 1)

            def sum_up(b, u, r):
                k = u % H
                if isinstance(b, int):
                    pe.wait_ge(loaded_sums[k], 32 * (b // H + 1))
                else:
                    pe.wait_ge(loaded_sums[k], r * (32 * (D // H)) + 32 * (u // H + 1))
                if reused(b, 1):
                    pe.wait_ge(s["tT_ready"], b)
                for t in range(TPB):
                    for v in range(3):
                        last = nc.tensor.matmul(p_s[:, t * P:(t + 1) * P], window[:, k, t + v], same[:, k, t, v],
                                                start=(v == 0), stop=(v == 2))
                last.then_inc(s["summed"], 1)

            def gates(b, u, r):
                k, v = u % H, u % 2
                pe.wait_ge(s["hT_ready"], b + 1)
                if sums is not None:
                    pe.wait_ge(s["tT_ready"], b + 1)
                if reused(b, G):
                    pe.wait_ge(s["sig"], b - G + 1)
                for g, to in ((0, p_r[u % G]), (1, p_z[u % G])):
                    last = nc.tensor.matmul(to[:, :], c.w_hh[:, g * P:(g + 1) * P], hT[:, k], start=True, stop=(sums is None))
                    if sums is not None:
                        nc.tensor.matmul(to[:, :], c.w_ih[:, g * P:(g + 1) * P], tT[:, u], start=False, stop=True)
                if reused(b, 1):
                    pe.wait_ge(s["v_ready" if sums is not None else "u_ready"], b)
                last = nc.tensor.matmul(p_n[:, :], c.w_hh[:, 2 * P:3 * P], hT[:, k], start=True, stop=True)
                if sums is not None:
                    last = nc.tensor.matmul(p_i[:, :], c.w_ih[:, 2 * P:3 * P], tT[:, u], start=True, stop=True)
                last.then_inc(s["gates"], 1)

            def messages(b, u, r):
                if reused(b, 1):
                    pe.wait_ge(s["msg_ready"], b)
                for t in range(TPB):
                    last = nc.tensor.matmul(p_m[:, t * P:(t + 1) * P], hT[:, u % H, t * P:(t + 1) * P], message,
                                            start=True, stop=True)
                last.then_inc(s["msg_mult"], 1)

            def sums_back(b, u, r):
                if reused(b, 1):
                    pe.wait_ge(s["yt_ready"], b)
                for t in range(TPB):
                    last = nc.tensor.transpose(p_q[:, t * P:(t + 1) * P], tT[:, u, t * P:(t + 1) * P], c.ident[:, :])
                last.then_inc(s["tR_ready"], 1)

            def back(b, u, r):
                pe.wait_ge(s["e_ready" if add_turned else "s_ready"], b + 1)
                if reused(b, G):
                    pe.wait_ge(s["yn_ready"], b - G + 1)
                for t in range(TPB):
                    to, part = p_y[u % G][:, t * P:(t + 1) * P], slice(t * P, (t + 1) * P)
                    if add_turned:
                        nc.tensor.matmul(to, eT[:, u % 2, part], c.ident[:, :], start=True, stop=False)
                        last = nc.tensor.matmul(to, nT[:, u % H, part], c.ident[:, :], start=False, stop=True)
                    else:
                        last = nc.tensor.transpose(to, sT[:, u % 2, part], c.ident[:, :])
                last.then_inc(s["back"], 1)

            steps = [(ahead + more + 6, back), (ahead + 2, turn)]
            if sums is not None:
                steps.append((ahead + 2, sum_up))
            steps.append((ahead + 3, gates))
            if sums is not None:
                steps.append((ahead + more + 6, sums_back))
            if message is not None:
                steps.append((ahead + 3, messages))
            pipeline(nc.tensor, blocks, steps, D)

        @blk.scalar
        def _(act):
            def lift(b, u, r):
                act.wait_ge(s["turned"], b + 1)
                if reused(b, H):
                    act.wait_ge(s["d_ready"], b - H + 1)
                nc.scalar.activation(hT[:, u % H], p_t[:, :], ACT.Copy).then_inc(s["hT_ready"], 1)

            def lift_sums(b, u, r):
                act.wait_ge(s["summed"], b + 1)
                if reused(b, D):
                    act.wait_ge(s["tR_ready"], b - D + 1)
                nc.scalar.activation(tT[:, u], p_s[:, :], ACT.Copy).then_inc(s["tT_ready"], 1)

            def sigmoids(b, u, r):
                v = u % 2
                act.wait_ge(s["gates"], b + 1)
                if reused(b, 2):
                    act.wait_ge(s["u_ready"], b - 1)
                nc.scalar.activation(rT[:, v], p_r[u % G][:, :], ACT.Sigmoid, bias=c.b_r)
                if reused(b, H):
                    act.wait_ge(s["e_ready"], b - H + 1)
                nc.scalar.activation(zT[:, u % H], p_z[u % G][:, :], ACT.Sigmoid, bias=c.b_z).then_inc(s["sig"], 1)

            def candidate(b, u, r):
                v = u % 2
                act.wait_ge(s["v_ready" if sums is not None else "u_ready"], b + 1)
                if reused(b, H):
                    act.wait_ge(s["back"], b - H + 1)
                nc.scalar.activation(nT[:, u % H], (vT if sums is not None else uT)[:, v], ACT.Tanh, bias=c.b_n).then_inc(s["n_ready"], 1)

            def scale(b, u, r):
                if reused(b, 2):
                    act.wait_ge(s["yg_ready"], b - 1)
                ln2.apply(nc, act, yn[:, u % 2], tiles(p_y[u % G][:, :]), b, u, ACT.Identity).then_inc(s["yn_ready"], 1)

            def apply(b, u, r):
                if reused(b, H):
                    act.wait_ge(s["turned"], b - H + 1)
                input_ready(act, u, r)
                ln.apply(nc, act, hn[:, u % H], x[:, u], b, u).then_inc(s["norm_ready"], 1)

            steps = [(ahead + 3, lift)]
            if sums is not None:
                steps.append((ahead + 3, lift_sums))
            steps += [(ahead + 5, candidate), (ahead + 4, sigmoids), (ahead + 1, apply), (ahead + more + 6, scale)]
            pipeline(nc.scalar, blocks, steps, D)


def film_stage(nc, name, c, blocks, sources, mend, dests, message_out, out):
    D = 6
    with Bench(nc, name) as w:
        xs = w.sb("xs", [P, D, 2, TPB, P])
        hn = w.sb("hn", [P, 2, 2, TPB, P])
        hT = w.sb("hT", [P, 2, 2, BLK])
        rel = w.sb("rel", [P, D, BLK], I32)
        hm = w.sb("hm", [P, 2, 2, NREL, BLK])
        ms = w.sb("ms", [P, 2, TPB, P])
        gm = w.sb("gm", [P, 2, TPB, P])
        gb = w.sb("gb", [P, 2, TPB, P])
        msg = w.sb("msg", [P, D, TPB, P])
        p_t = [w.ps(f"p_t{i}") for i in range(2)]
        y = w.sb("y", [P, D, TPB, P])
        part = w.sb("part", [P, 2, TPB, P])
        added = w.sem("added")
        p_m, p_u = w.ps("p_m"), w.ps("p_u")
        p_f = [w.ps(f"p_f{i}", (P, TPB * 2 * P)) for i in range(2)]
        lns = [Norm(w, f"ln{k}", D) for k in range(2)]
        loaded = w.sems("loaded", D)
        norm_ready = w.sem("norm_ready")
        turned = w.sem("turned")
        hT_ready = w.sem("hT_ready")
        masked = w.sem("masked")
        multiplied = w.sem("multiplied")
        ms_ready = w.sem("ms_ready")
        gm_ready = w.sem("gm_ready")
        gb_ready = w.sem("gb_ready")
        msg_ready = w.sem("msg_ready")
        y_ready = w.sem("y_ready")
        stored = w.sems("stored", D)
        y_stored = w.sems("y_stored", D)
        fetch = Fetch(w, "mend", D, mend[0], mend[1], mend[0].shape[0])
        ahead = 2
        blk = w.block()

        @blk.sync
        def _(sp):
            def load(b, u, r):
                if reused(b, D):
                    sp.wait_ge(masked, b * 2 - 2 * D + 2)
                    w.settle(sp)
                    sp.wait_ge(y_ready, b - D + 1)
                    w.settle(sp)
                sp.dma_start(xs[:, u, 0], block_rows(sources, b, True)).then_inc(loaded[u], 16)
                sp.dma_start(xs[:, u, 1], block_rows(dests, b, True)).then_inc(loaded[u], 16)
                sp.dma_start(rel[:, u], c.relation_row[:, bass.ds(b * BLK, BLK)].to_broadcast([P, BLK])).then_inc(loaded[u], 16)

            def store(b, u, r):
                sp.wait_ge(msg_ready, b + 1)
                w.settle(sp)
                sp.dma_start(block_rows(message_out[P:, :], b, True), msg[:, u]).then_inc(stored[u], 16)
                sp.wait_ge(y_ready, b + 1)
                w.settle(sp)
                sp.dma_start(block_rows(out, b, True), y[:, u]).then_inc(y_stored[u], 16)
            pipeline(nc.sync, blocks, [(0, load), (ahead + 5, store)], D)
            for u in range(D):
                sp.wait_ge(stored[u], 16 * cdiv(blocks - u, D))
                w.settle(sp)
                sp.wait_ge(y_stored[u], 16 * cdiv(blocks - u, D))
                w.settle(sp)

        @blk.gpsimd
        def _(pool):
            def bring(b, u, r):
                pool.wait_ge(loaded[u], 48 * (r + 1))
                fetch.issue(nc, pool, xs[:, u, 0], b, u, r)

            def inverse(b, u, r):
                for k in range(2):
                    lns[k].inverse(nc, pool, c.minus_half, b, u)
            pipeline(nc.gpsimd, blocks, [(0, bring), (ahead, inverse)], D)

        @blk.vector
        def _(dve):
            def statistics(b, u, r):
                dve.wait_ge(loaded[u], 48 * (r + 1))
                fetch.arrived(dve, u, r)
                for k in range(2):
                    lns[k].statistics(nc, dve, xs[:, u, k], b, u)

            def mask(b, u, r):
                for k in range(2):
                    dve.wait_ge(hT_ready, b * 2 + k + 1)
                    if reused(b, 2):
                        dve.wait_ge(multiplied, b * 2 + k - 3)
                    for q in range(NREL):
                        last = nc.vector.scalar_tensor_tensor(hm[:, u % 2, k, q], rel[:, u], float(q), hT[:, u % 2, k],
                                                              ALU.is_equal, ALU.mult)
                    last.then_inc(masked, 1)

            def add(b, u, r):
                dve.wait_ge(multiplied, b * 2 + 1)
                if reused(b, D):
                    dve.wait_ge(y_stored[u], 16 * r)
                nc.vector.tensor_tensor(flat(part[:, u % 2]), p_u[:, :], flat(xs[:, u, 0]), ALU.add).then_inc(added, 1)
                dve.wait_ge(added, b + 1)
                nc.vector.tensor_tensor(y[:, u], part[:, u % 2], over_tiles(c.rows["h_bias"][:, :]), ALU.add).then_inc(y_ready, 1)

            def finish(b, u, r):
                f = p_f[u % 2][:, :].rearrange("p (t k d) -> p t k d", t=TPB, k=2)
                v = u % 2
                dve.wait_ge(multiplied, b * 2 + 2)
                dve.wait_ge(ms_ready, b + 1)
                nc.vector.tensor_tensor(gm[:, v], f[:, :, 0], ms[:, v], ALU.mult).then_inc(gm_ready, 1)
                dve.wait_ge(gm_ready, b + 1)
                if reused(b, 2):
                    dve.wait_ge(msg_ready, b - 1)
                nc.vector.tensor_tensor(gb[:, v], f[:, :, 1], gm[:, v], ALU.add).then_inc(gb_ready, 1)
            pipeline(nc.vector, blocks, [(ahead + 4, add), (ahead + 2, mask), (ahead + 4, finish), (ahead, statistics)], D)

        @blk.tensor
        def _(pe):
            def turn(b, u, r):
                for k in range(2):
                    pe.wait_ge(norm_ready, b * 2 + k + 1)
                    if reused(b, 1):
                        pe.wait_ge(hT_ready, b * 2 + k - 1)
                    for t in range(TPB):
                        last = nc.tensor.transpose(p_t[k][:, t * P:(t + 1) * P], hn[:, u % 2, k, t], c.ident[:, :])
                    last.then_inc(turned, 1)

            def multiply(b, u, r):
                for k in range(2):
                    pe.wait_ge(masked, b * 2 + k + 1)
                    if k == 0:
                        if reused(b, 1):
                            pe.wait_ge(ms_ready, b)
                            pe.wait_ge(added, b)
                        for t in range(TPB):
                            to = p_u[:, t * P:(t + 1) * P]
                            nc.tensor.matmul(to, hT[:, u % 2, 0, t * P:(t + 1) * P], c.weights["loop_w"][:, :], start=True, stop=True)
                    elif reused(b, 2):
                        pe.wait_ge(gb_ready, b - 1)
                    for t in range(TPB):
                        for q in range(NREL):
                            left = hm[:, u % 2, k, q, t * P:(t + 1) * P]
                            if k == 0:
                                last = nc.tensor.matmul(p_m[:, t * P:(t + 1) * P], left, c.w_rel[:, q * P:(q + 1) * P],
                                                        start=(q == 0), stop=(q == NREL - 1))
                            else:
                                last = nc.tensor.matmul(p_f[u % 2][:, t * 2 * P:(t + 1) * 2 * P], left,
                                                        c.w_film[:, q * 2 * P:(q + 1) * 2 * P],
                                                        start=(q == 0), stop=(q == NREL - 1))
                    last.then_inc(multiplied, 1)
            pipeline(nc.tensor, blocks, [(ahead + 3, multiply), (ahead + 1, turn)], D)

        @blk.scalar
        def _(act):
            def lift(b, u, r):
                for k in range(2):
                    act.wait_ge(turned, b * 2 + k + 1)
                    if reused(b, 2):
                        act.wait_ge(masked, b * 2 - 4 + k + 1)
                        act.wait_ge(multiplied, b * 2 - 4 + k + 1)
                    nc.scalar.activation(hT[:, u % 2, k], p_t[k][:, :], ACT.Copy).then_inc(hT_ready, 1)

            def apply(b, u, r):
                if reused(b, 2):
                    act.wait_ge(turned, b * 2 - 2)
                act.wait_ge(loaded[u], 48 * (r + 1))
                fetch.arrived(act, u, r)
                for k in range(2):
                    lns[k].apply(nc, act, hn[:, u % 2, k], xs[:, u, k], b, u).then_inc(norm_ready, 1)

            def copy_m(b, u, r):
                act.wait_ge(multiplied, b * 2 + 1)
                if reused(b, 2):
                    act.wait_ge(gm_ready, b - 1)
                nc.scalar.activation(flat(ms[:, u % 2]), p_m[:, :], ACT.Copy).then_inc(ms_ready, 1)

            def rectify(b, u, r):
                act.wait_ge(gb_ready, b + 1)
                if reused(b, D):
                    act.wait_ge(stored[u], 16 * r)
                nc.scalar.activation(flat(msg[:, u]), flat(gb[:, u % 2]), ACT.Relu).then_inc(msg_ready, 1)
            pipeline(nc.scalar, blocks, [(ahead + 4, copy_m), (ahead + 2, lift), (ahead + 1, apply), (ahead + 4, rectify)], D)


def first_nodes_stage(nc, name, c, start, blocks, source, out, total, tail, job):
    D, H = 8, 4
    source, out = source[start * BLK:, :], out[start * BLK:, :]
    with Bench(nc, name) as w:
        x = w.sb("x", [P, D, TPB, P])
        y = w.sb("y", [P, D, TPB, P])
        hn = w.sb("hn", [P, H, TPB, P])
        hT = w.sb("hT", [P, H, BLK])
        aT = w.sb("aT", [P, H, BLK])
        h2 = w.sb("h2", [P, H, TPB, P])
        p_t, p_a, p_y = ([w.ps(f"{n}{i}") for i in range(2)] for n in ("p_t", "p_a", "p_y"))
        acc = w.ps("acc")
        ln, ln2 = Norm(w, "ln", D), Norm(w, "ln2", D)
        side = job(w, c)
        assert side.D == D // 2
        loaded, stored = w.sems("loaded", D), w.sems("stored", D)
        norm_ready, turned, hT_ready, a_done, aT_ready, y_done, y_ready, h2_ready, summed = (
            w.sem(n) for n in ("norm_ready", "turned", "hT_ready", "a_done", "aT_ready", "y_done", "y_ready", "h2_ready",
                               "summed"))
        blk = w.block()

        @blk.sync
        def _(sp):
            def load(b, u, r):
                if reused(b, D):
                    sp.wait_ge(y_ready, b - D + 1)
                    w.settle(sp)
                if tail is not None and isinstance(b, int) and b == blocks - 1:
                    sp.dma_start(x[0:tail, u], block_rows(source, b, False, tail)).then_inc(loaded[u], 16)
                else:
                    sp.dma_start(x[:, u], block_rows(source, b, False)).then_inc(loaded[u], 16)

            def store(b, u, r):
                sp.wait_ge(y_ready, b + 1)
                w.settle(sp)
                sp.dma_start(block_rows(out, b, False), y[:, u]).then_inc(stored[u], 16)
            pipeline(nc.sync, blocks, [(0, load), (7, store)], D)
            for u in range(D):
                sp.wait_ge(stored[u], 16 * cdiv(blocks - u, D))
                w.settle(sp)

        @blk.gpsimd
        def _(pool):
            def power(b, u, r):
                ln.power(nc, pool, c.minus_half, b, u)

            def power2(b, u, r):
                ln2.power(nc, pool, c.minus_half, b, u)

            def shifts(b, u, r):
                ln.shifts(nc, pool, b, u)

            def shifts2(b, u, r):
                ln2.shifts(nc, pool, b, u)

            def beside(b, u, r, in_turn):
                every = 2
                e = b // every if isinstance(b, int) else r * (D // every) + u // every
                if not isinstance(e, int) or e < c.edge_blocks:
                    side.block(nc, pool, e, u // every, r, u % every, in_turn)

            def program(in_turn):
                pipeline(nc.gpsimd, blocks, [(0, power), (5, power2), (0, shifts), (5, shifts2),
                                             (0, partial(beside, in_turn=in_turn))], D)
                for e in range(blocks // 2, c.edge_blocks):
                    for half in range(2):
                        if e * 2 + half >= blocks:
                            side.block(nc, pool, e, e % side.D, e // side.D, half, in_turn)
                side.end(nc, pool, c.edge_blocks)

            spread = side.start(nc, pool)
            if spread is None:
                program(False)
            else:
                with pool.If(spread == 0):
                    program(False)
                with pool.If(spread != 0):
                    program(True)

        @blk.vector
        def _(dve):
            def lift(b, u, r):
                dve.wait_ge(turned, b + 1)
                if reused(b, H):
                    dve.wait_ge(a_done, b - H + 1)
                nc.vector.tensor_copy(hT[:, u % H], p_t[u % 2][:, :]).then_inc(hT_ready, 1)

            def finish(b, u, r):
                dve.wait_ge(y_done, b + 1)
                if reused(b, D):
                    dve.wait_ge(stored[u], 16 * r)
                    dve.wait_ge(h2_ready, b - D + 1)
                nc.vector.scalar_tensor_tensor(flat(y[:, u]), p_y[u % 2][:, :], 0.0, flat(x[:, u]), ALU.max,
                                               ALU.add).then_inc(y_ready, 1)

            def statistics(step, b, u, r):
                if step == 0:
                    dve.wait_ge(loaded[u], 16 * (r + 1))
                ln.statistics_step(step, nc, dve, x[:, u], b, u)

            def statistics2(step, b, u, r):
                if step == 0:
                    dve.wait_ge(y_ready, b + 1)
                ln2.statistics_step(step, nc, dve, y[:, u], b, u)
            pipeline(nc.vector, blocks, [(3, lift), (5, finish), *in_turns([(0, partial(statistics, step)) for step in range(4)],
                    [(5, partial(statistics2, step)) for step in range(4)])], D)

        @blk.scalar
        def _(act):
            def rectify(b, u, r):
                act.wait_ge(a_done, b + 1)
                if reused(b, H):
                    act.wait_ge(y_done, b - H + 1)
                nc.scalar.activation(aT[:, u % H], p_a[u % 2][:, :], ACT.Relu, bias=c.b1_col[:, :]).then_inc(aT_ready, 1)

            def apply2(b, u, r):
                if reused(b, H):
                    act.wait_ge(summed, b - H + 1)
                ln2.apply(nc, act, h2[:, u % H], y[:, u], b, u).then_inc(h2_ready, 1)

            def apply(b, u, r):
                act.wait_ge(loaded[u], 16 * (r + 1))
                if reused(b, H):
                    act.wait_ge(turned, b - H + 1)
                ln.apply(nc, act, hn[:, u % H], x[:, u], b, u).then_inc(norm_ready, 1)
            pipeline(nc.scalar, blocks, [(4, rectify), (6, apply2), (1, apply)], D)
            act.wait_ge(summed, blocks)
            nc.scalar.activation(total, acc[:, 0:1], ACT.Copy)

        @blk.tensor
        def _(pe):
            def sum_up(b, u, r):
                pe.wait_ge(h2_ready, b + 1)
                for t in range(TPB):
                    last = nc.tensor.matmul(acc[:, 0:1], h2[:, u % H, t], c.node_weight[:, bass.ds(b * TPB + (start * TPB + t), 1)],
                                            start=isinstance(b, int) and b == 0 and t == 0,
                                            stop=isinstance(b, int) and b == blocks - 1 and t == TPB - 1)
                last.then_inc(summed, 1)

            def turn(b, u, r):
                pe.wait_ge(norm_ready, b + 1)
                if reused(b, 2):
                    pe.wait_ge(hT_ready, b - 1)
                for t in range(TPB):
                    last = nc.tensor.transpose(p_t[u % 2][:, t * P:(t + 1) * P], hn[:, u % H, t], c.ident[:, :])
                last.then_inc(turned, 1)

            def second(b, u, r):
                pe.wait_ge(aT_ready, b + 1)
                if reused(b, 2):
                    pe.wait_ge(y_ready, b - 1)
                for t in range(TPB):
                    to = p_y[u % 2][:, t * P:(t + 1) * P]
                    nc.tensor.matmul(to, c.first_row[:, :], c.rows["b2"][:, :], start=True, stop=False)
                    last = nc.tensor.matmul(to, aT[:, u % H, t * P:(t + 1) * P], c.weights["W2_0"][:, :], start=False, stop=True)
                last.then_inc(y_done, 1)

            def first(b, u, r):
                pe.wait_ge(hT_ready, b + 1)
                if reused(b, 2):
                    pe.wait_ge(aT_ready, b - 1)
                nc.tensor.matmul(p_a[u % 2][:, :], c.weights["W1_0"][:, :], hT[:, u % H], start=True, stop=True).then_inc(a_done, 1)
            pipeline(nc.tensor, blocks, [(7, sum_up), (2, turn), (4, second), (3, first)], D)


def last_nodes_stage(nc, name, c, blocks, source, out, layers, tail):
    D, H = 8, 4
    with Bench(nc, name) as w:
        xs = [w.sb(f"x{k}", [P, D, TPB, P]) for k in range(3)]
        xb = w.sb("xb", [P, D, TPB, P])
        hn = [w.sb(f"hn{k}", [P, H, TPB, P]) for k in range(2)]
        hT = [w.sb(f"hT{k}", [P, H, BLK]) for k in range(2)]
        p_t = [[w.ps(f"p_t{k}{i}") for i in range(2)] for k in range(2)]
        p_y = [[w.ps(f"p_y{k}{i}") for i in range(2)] for k in range(2)]
        lns = [Norm(w, f"ln{k}", D) for k in range(2)]
        loaded, stored = w.sems("loaded", D), w.sems("stored", D)
        norm_ready, turned, hT_ready, multiplied, x_ready = (
            w.sems(n, 2) for n in ("norm_ready", "turned", "hT_ready", "multiplied", "x_ready"))
        xb_ready = w.sem("xb_ready")
        blk = w.block()

        def input_ready(eng, k, b, u, r):
            if k == 0:
                eng.wait_ge(loaded[u], 16 * (r + 1))
            else:
                eng.wait_ge(x_ready[0], b + 1)

        @blk.sync
        def _(sp):
            def load(b, u, r):
                if reused(b, D):
                    sp.wait_ge(x_ready[0], b - D + 1)
                    w.settle(sp)
                sp.dma_start(xs[0][:, u], block_rows(source, b, False)).then_inc(loaded[u], 16)

            def store(b, u, r):
                sp.wait_ge(x_ready[1], b + 1)
                w.settle(sp)
                if tail is not None and isinstance(b, int) and b == blocks - 1:
                    sp.dma_start(block_rows(out, b, False, tail), xs[2][0:tail, u]).then_inc(stored[u], 16)
                else:
                    sp.dma_start(block_rows(out, b, False), xs[2][:, u]).then_inc(stored[u], 16)
            pipeline(nc.sync, blocks, [(0, load), (10, store)], D)
            for u in range(D):
                sp.wait_ge(stored[u], 16 * cdiv(blocks - u, D))
                w.settle(sp)

        @blk.gpsimd
        def _(pool):
            def power(k, b, u, r):
                lns[k].power(nc, pool, c.minus_half, b, u)

            def add_bias(b, u, r):
                if reused(b, D):
                    pool.wait_ge(x_ready[0], b - D + 1)
                input_ready(pool, 0, b, u, r)
                nc.gpsimd.tensor_tensor(xb[:, u], xs[0][:, u], over_tiles(layers[0][1]), ALU.add).then_inc(xb_ready, 1)

            def shifts(k, b, u, r):
                lns[k].shifts(nc, pool, b, u)
            pipeline(nc.gpsimd, blocks, [(0, partial(power, 0)), (0, partial(shifts, 0)), (4, partial(power, 1)),
                                         (4, partial(shifts, 1)), (1, add_bias)], D)

        @blk.vector
        def _(dve):
            def add(k, b, u, r):
                dve.wait_ge(multiplied[k], b + 1)
                if k == 0:
                    dve.wait_ge(xb_ready, b + 1)
                if reused(b, D):
                    if k == 0:
                        dve.wait_ge(x_ready[1], b - D + 1)
                    else:
                        dve.wait_ge(stored[u], 16 * r)
                nc.vector.tensor_tensor(flat(xs[k + 1][:, u]), p_y[k][u % 2][:, :], flat((xb, xs[1])[k][:, u]), ALU.add).then_inc(x_ready[k], 1)

            def statistics(k, step, b, u, r):
                if step == 0:
                    input_ready(dve, k, b, u, r)
                lns[k].statistics_step(step, nc, dve, xs[k][:, u], b, u)
            pipeline(nc.vector, blocks, [(4, partial(add, 0)), (8, partial(add, 1)), *in_turns(
                [(0, partial(statistics, 0, step)) for step in range(4)],
                [(4, partial(statistics, 1, step)) for step in range(4)])], D)

        @blk.scalar
        def _(act):
            def lift(k, b, u, r):
                act.wait_ge(turned[k], b + 1)
                if reused(b, H):
                    act.wait_ge(multiplied[k], b - H + 1)
                nc.scalar.activation(hT[k][:, u % H], p_t[k][u % 2][:, :], ACT.Copy).then_inc(hT_ready[k], 1)

            def apply(k, b, u, r):
                input_ready(act, k, b, u, r)
                if reused(b, H):
                    act.wait_ge(turned[k], b - H + 1)
                lns[k].apply(nc, act, hn[k][:, u % H], xs[k][:, u], b, u).then_inc(norm_ready[k], 1)
            pipeline(nc.scalar, blocks, [(3, partial(lift, 0)), (7, partial(lift, 1)), (1, partial(apply, 0)),
                                         (5, partial(apply, 1))], D)

        @blk.tensor
        def _(pe):
            def turn(k, b, u, r):
                pe.wait_ge(norm_ready[k], b + 1)
                if reused(b, 2):
                    pe.wait_ge(hT_ready[k], b - 1)
                for t in range(TPB):
                    last = nc.tensor.transpose(p_t[k][u % 2][:, t * P:(t + 1) * P], hn[k][:, u % H, t], c.ident[:, :])
                last.then_inc(turned[k], 1)

            def multiply(k, b, u, r):
                update, bias = layers[k]
                pe.wait_ge(hT_ready[k], b + 1)
                if reused(b, 2):
                    pe.wait_ge(x_ready[k], b - 1)
                for t in range(TPB):
                    to = p_y[k][u % 2][:, t * P:(t + 1) * P]
                    if k == 1:
                        nc.tensor.matmul(to, c.first_row[:, :], bias, start=True, stop=False)
                    last = nc.tensor.matmul(to, hT[k][:, u % H, t * P:(t + 1) * P], update, start=(k == 0), stop=True)
                last.then_inc(multiplied[k], 1)
            pipeline(nc.tensor, blocks, [(2, partial(turn, 0)), (6, partial(turn, 1)), (7, partial(multiply, 1)),
                                         (3, partial(multiply, 0))], D)


class Common:
    pass


WEIGHTS = (("W1_0", P), ("W1_1", P), ("W2_0", P), ("W2_1", P), ("W_msg", P), ("w_ih", 3 * P), ("w_hh", 3 * P),
           ("w_rel", NREL * P), ("w_film", NREL * 2 * P), ("loop_w", P), ("W_neigh", P), ("W_self", P))
ROWS = ("b1", "b2", "b_msg", "gamma", "beta", "h_bias", "b_neigh", "b_self")


def constants_phase(nc, c, args):
    with Bench(nc, "const") as w:
        loaded, made, fixed = w.sem("loaded"), w.sem("made"), w.sem("fixed")
        zero = w.sb("zero", [P, P])
        blk = w.block()
        count = [0]

        @blk.sync
        def _(sp):
            for name, cols in WEIGHTS:
                sp.dma_start(c.weights[name][:, :], args[name]).then_inc(loaded, 16)
                count[0] += 1
            for name in ROWS:
                sp.dma_start(c.rows[name][:, :], args[name].rearrange("(a n) -> a n", a=1).to_broadcast([P, P])).then_inc(loaded, 16)
                count[0] += 1
            for col, at in ((c.g_ih, args["b_ih"]), (c.g_hh, args["b_hh"])):
                for g in range(3):
                    sp.dma_start(col[:, g:g + 1], at[g * P:(g + 1) * P].rearrange("(p a) -> p a", a=1)).then_inc(loaded, 16)
                    count[0] += 1
            sp.dma_start(c.b1_col[:, :], args["b1"].rearrange("(p a) -> p a", a=1)).then_inc(loaded, 16)
            count[0] += 1
            sp.dma_start(c.src[:, :], args["src_columns"]).then_inc(loaded, 16)
            sp.dma_start(c.dst[:, 1:c.tiles + 1], args["dst_columns"]).then_inc(loaded, 16)
            count[0] += 2
            sp.wait_ge(made, 1)
            for at in (0, (c.tiles + 1) * P):
                sp.dma_start(c.msg[at:at + P, :], zero[:, :]).then_inc(loaded, 16)
                count[0] += 1
            sp.wait_ge(loaded, 16 * count[0])

        @blk.vector
        def _(dve):
            nc.vector.memset(zero[:, :], 0.0).then_inc(made, 1)
            nc.vector.memset(c.ones[:, :], 1.0)
            nc.vector.memset(c.minus_half[:, :], -0.5)
            nc.vector.memset(c.minus_half_wide[:, :], -0.5)
            nc.vector.memset(c.dst[:, 0:1], -1)
            nc.vector.memset(c.dst[:, c.tiles + 1:c.tiles + 2], -1)

        @blk.gpsimd
        def _(pool):
            nc.gpsimd.memset(c.ident[:, :], 0.0).then_inc(fixed, 1)
            nc.gpsimd.memset(c.earlier[:, :], 1.0).then_inc(fixed, 1)
            pool.wait_ge(fixed, 2)
            nc.gpsimd.affine_select(out=c.ident[:, :], in_=c.ident[:, :], compare_op=ALU.not_equal, fill=1.0, base=0,
                                    pattern=[[-1, P]], channel_multiplier=1)
            nc.gpsimd.memset(c.first_row[:, :], 1.0).then_inc(fixed, 1)
            pool.wait_ge(fixed, 3)
            nc.gpsimd.affine_select(out=c.first_row[:, :], in_=c.first_row[:, :], compare_op=ALU.is_equal, fill=0.0, base=0,
                                    pattern=[[0, P]], channel_multiplier=1)
            nc.gpsimd.affine_select(out=c.earlier[:, :], in_=c.earlier[:, :], compare_op=ALU.is_gt, fill=0.0, base=0,
                                    pattern=[[-1, P]], channel_multiplier=1)
            nc.gpsimd.iota(c.count_row[:, :], [[1, BLK]], base=0, channel_multiplier=0, allow_small_or_imprecise_dtypes=True)
            nc.gpsimd.iota(c.node_of[:, :], [[1, BLK]], base=0, channel_multiplier=BLK)
            nc.gpsimd.iota(c.slot_of[:, :], [[P, c.tiles]], base=0, channel_multiplier=1)


def degree_phase(nc, c, x, s_x0):
    D, T = 4, c.tiles
    with Bench(nc, "deg") as w:
        part_i = w.sb("part_i", [P, 4, T], I32)
        part = w.sb("part", [P, 4, T])
        hot_hi = w.sb("hot_hi", [P, D, 2, P], BF16)
        hot_lo = w.sb("hot_lo", [P, D, 2, BLK], BF16)
        deg = w.sb("deg", [P, 2, BLK])
        least = w.sb("least", [P, 2, BLK])
        most = w.sb("most", [P, 2, BLK])
        valid = w.sb("valid", [P, BLK])
        weight = w.sb("weight", [P, BLK])
        row = w.sb("row", [P, BLK, 4])
        p_deg = [w.ps(f"p_deg{k}") for k in range(2)]
        split, hot, added, linked, stored = (w.sem(n) for n in ("split", "hot", "added", "linked", "stored"))
        rows = w.sb("rows", [P, D, TPB, P])
        fetch = Fetch(w, "fetch", D, x, c.src_row, x.shape[0])
        named, kept = w.sem("named"), w.sems("kept", D)
        blk = w.block()

        @blk.gpsimd
        def _(pool):
            pool.wait_ge(named, 1)

            def bring(b, u, r):
                if reused(b, D):
                    pool.wait_ge(kept[u], 16 * r)
                fetch.issue(nc, pool, rows[:, u], b, u, r)
            pipeline(nc.gpsimd, c.edge_blocks, [(0, bring)], D)

        @blk.vector
        def _(dve):
            for k, col in enumerate((c.src[:, :], c.dst[:, 1:T + 1])):
                nc.vector.tensor_scalar(part_i[:, 2 * k], col, 9, None, ALU.arith_shift_right)
                nc.vector.tensor_scalar(part_i[:, 2 * k + 1], col, BLK - 1, None, ALU.bitwise_and).then_inc(split, 1)
            nc.vector.tensor_tensor(c.apart[:, :], c.src[:, :], c.dst[:, 1:T + 1], ALU.not_equal)
            nc.vector.tensor_scalar(c.src_row[:, :], c.src[:, :], c.nodes - 1, None, ALU.min).then_inc(named, 1)
            nc.vector.tensor_scalar(c.dst_row[:, :], c.dst[:, 1:T + 1], c.nodes - 1, None, ALU.min)
            nc.vector.tensor_scalar(c.real[:, :], c.dst[:, 1:T + 1], c.nodes, None, ALU.is_lt)
            dve.wait_ge(split, 2)
            nc.vector.tensor_copy(part[:, :, :], part_i[:, :, :]).then_inc(split, 1)
            dve.wait_ge(split, 3)

            def one_hot(b, u, r):
                if reused(b, D):
                    dve.wait_ge(added, b - D + 1)
                at = bass.ds(b, 1)
                nc.vector.tensor_scalar(hot_hi[:, u, 0], c.count_row[:, 0:P], part[:, 0, at], c.apart[:, at], ALU.is_equal, ALU.mult)
                nc.vector.tensor_scalar(hot_lo[:, u, 0], c.count_row[:, :], part[:, 1, at], None, ALU.is_equal)
                nc.vector.tensor_scalar(hot_hi[:, u, 1], c.count_row[:, 0:P], part[:, 2, at], None, ALU.is_equal)
                nc.vector.tensor_scalar(hot_lo[:, u, 1], c.count_row[:, :], part[:, 3, at], None, ALU.is_equal).then_inc(hot, 1)
            pipeline(nc.vector, T, [(0, one_hot)], D)
            dve.wait_ge(added, T)
            for k in range(2):
                last = nc.vector.tensor_copy(deg[:, k], p_deg[k][:, :])
            last.then_inc(linked, 1)
            dve.wait_ge(linked, 1)
            nc.vector.tensor_scalar(least[:, 1], deg[:, 1], 1.0, None, ALU.max)
            nc.vector.tensor_copy(row[:, :, 0], deg[:, 0])
            nc.vector.tensor_scalar(most[:, 1], deg[:, 1], 1.0, None, ALU.min)
            nc.vector.tensor_scalar(valid[:, :], c.node_of[:, :], c.nodes, None, ALU.is_lt)
            nc.vector.tensor_copy(row[:, :, 3], deg[:, 1])
            nc.vector.memset(row[:, :, 2].bitcast(I32), FAR).then_inc(linked, 1)
            dve.wait_ge(linked, 2)
            nc.vector.tensor_scalar(weight[:, :], most[:, 1], -1.0, 1.0, ALU.mult, ALU.add).then_inc(linked, 1)
            nc.vector.reciprocal(row[:, :, 1], least[:, 1]).then_inc(linked, 1)
            dve.wait_ge(linked, 4)
            nc.vector.tensor_tensor(weight[:, :], weight[:, :], valid[:, :], ALU.mult).then_inc(linked, 1)

        @blk.tensor
        def _(pe):
            def add(b, u, r):
                pe.wait_ge(hot, b + 1)
                for k in range(2):
                    last = nc.tensor.matmul(p_deg[k][:, :], hot_hi[:, u, k], hot_lo[:, u, k],
                                            start=isinstance(b, int) and b == 0, stop=isinstance(b, int) and b == T - 1)
                last.then_inc(added, 1)
            pipeline(nc.tensor, T, [(0, add)], D)

        @blk.sync
        def _(sp):
            def keep(b, u, r):
                fetch.arrived(sp, u, r)
                w.settle(sp)
                sp.dma_start(block_rows(s_x0, b, True), rows[:, u]).then_inc(kept[u], 16)
            pipeline(nc.sync, c.edge_blocks, [(0, keep)], D)
            for u in range(D):
                sp.wait_ge(kept[u], 16 * cdiv(c.edge_blocks - u, D))
                w.settle(sp)
            sp.wait_ge(linked, 4)
            sp.dma_start(c.table.rearrange("(p n) k -> p n k", p=P), row[:, :, :]).then_inc(stored, 16)
            sp.wait_ge(linked, 5)
            sp.dma_start(c.weight_dram.rearrange("(p n) -> p n", p=P), weight[:, :]).then_inc(stored, 16)
            sp.wait_ge(stored, 32)
            sp.dma_start(c.node_weight[:, :].rearrange("p (b t) -> p b t", t=TPB),
                         c.weight_dram[0:c.node_blocks * BLK].rearrange("(b p t) -> p b t", p=P, t=TPB)).then_inc(stored, 16)
            sp.wait_ge(stored, 48)


def same_phase(nc, c, dst_line, dst_columns):
    D = 4
    with Bench(nc, "same") as w:
        line = w.sb("line", [P, D, P + BLK], I32)
        same = w.sb("same", [P, D, TPB, 3, P])
        seen = w.sb("seen", [P, D, TPB, 2, P])
        before = w.sb("before", [P, D, TPB])
        away = w.sb("away", [P, D, TPB])
        loaded = w.sems("loaded", D)
        made, linked = w.sem("made"), w.sem("linked")
        stored = w.sems("stored", D)
        p_count = w.ps("p_count", (P, c.tiles))
        got = w.sb("got", [P, D, TPB, 4])
        fetch = Fetch(w, "fetch", D, c.table, dst_columns, c.table.shape[0])
        taken = w.sem("taken")
        col = c.dst_value
        copied, counted = w.sem("copied"), w.sem("counted")
        blk = w.block()

        @blk.gpsimd
        def _(pool):
            def bring(b, u, r):
                if reused(b, D):
                    pool.wait_ge(taken, b - D + 1)
                fetch.issue(nc, pool, got[:, u], b, u, r)
            pipeline(nc.gpsimd, c.edge_blocks, [(0, bring)], D)

        @blk.tensor
        def _(pe):
            def count(b, u, r):
                pe.wait_ge(made, b + 1)
                for t in range(TPB):
                    for v in range(3):
                        last = nc.tensor.matmul(p_count[:, bass.ds(b * TPB + t, 1)], same[:, u, t, v], c.ones[:, 0:1],
                                                start=(v == 0), stop=(v == 2))
                last.then_inc(counted, 1)
            pipeline(nc.tensor, c.edge_blocks, [(0, count)], D)

        @blk.scalar
        def _(act):
            act.wait_ge(counted, c.edge_blocks)
            nc.scalar.activation(c.window_count[:, :], p_count[:, :], ACT.Copy)

        @blk.sync
        def _(sp):
            def load(b, u, r):
                if reused(b, D):
                    sp.wait_ge(made, b - D + 1)
                    w.settle(sp)
                sp.dma_start(line[:, u], dst_line[:, bass.ds(b * BLK, P + BLK)].to_broadcast([P, P + BLK])).then_inc(loaded[u], 16)

            def store(b, u, r):
                sp.wait_ge(made, b + 1)
                w.settle(sp)
                sp.dma_start(c.same_dram[bass.ds(b * BLK, BLK), :].rearrange("(t p) d -> p t d", p=P),
                             same[:, u].rearrange("p t w e -> p t (w e)")).then_inc(stored[u], 16)
            pipeline(nc.sync, c.edge_blocks, [(0, load), (2, store)], D)
            for u in range(D):
                sp.wait_ge(stored[u], 16 * cdiv(c.edge_blocks - u, D))
                w.settle(sp)

        @blk.vector
        def _(dve):
            nc.vector.tensor_copy(col[:, :], c.dst[:, :]).then_inc(copied, 1)
            dve.wait_ge(copied, 1)

            def compare(b, u, r):
                if reused(b, D):
                    dve.wait_ge(stored[u], 16 * r)
                    dve.wait_ge(counted, b - D + 1)
                dve.wait_ge(loaded[u], 16 * (r + 1))
                for t in range(TPB):
                    for v in range(3):
                        last = nc.vector.tensor_scalar(same[:, u, t, v], line[:, u, (t + 1) * P:(t + 2) * P],
                                                       col[:, bass.ds(b * TPB + t + v, 1)], None, ALU.is_equal)
                last.then_inc(made, 1)
                for t in range(TPB):
                    last = nc.vector.tensor_scalar(seen[:, u, t, 0], line[:, u, t * P:(t + 1) * P],
                                                   col[:, bass.ds(b * TPB + t + 1, 1)], None, ALU.is_equal)
                last.then_inc(linked, 1)
                dve.wait_ge(made, b + 1)
                nc.vector.tensor_tensor(seen[:, u, :, 1], same[:, u, :, 1], c.earlier.unsqueeze(1).to_broadcast([P, TPB, P]),
                                        ALU.mult).then_inc(linked, 1)
                dve.wait_ge(linked, b * 4 + 2)
                nc.vector.tensor_reduce(before[:, u], seen[:, u].rearrange("p t k e -> p t (k e)"), mybir.AxisListType.X, ALU.max).then_inc(linked, 1)
                dve.wait_ge(linked, b * 4 + 3)
                nc.vector.tensor_scalar(away[:, u], before[:, u], float(FAR), None, ALU.mult).then_inc(linked, 1)
                dve.wait_ge(linked, b * 4 + 4)
                nc.vector.tensor_tensor(c.write_at[:, bass.ds(b * TPB, TPB)], away[:, u],
                                        col[:, bass.ds(b * TPB + 1, TPB)], ALU.add)

            def take(b, u, r):
                fetch.arrived(dve, u, r)
                nc.vector.tensor_copy(c.at_dst[:, bass.ds(b * TPB, TPB), :].bitcast(I32), got[:, u].bitcast(I32)).then_inc(taken, 1)
            pipeline(nc.vector, c.edge_blocks, [(0, compare), (1, take)], D)


def scatter_check_phase(nc, c):
    with Bench(nc, "check") as w:
        differs = w.sb("differs", [P, c.tiles])
        some = w.sb("some", [P, 1])
        unit = w.sb("unit", [P, 3, P])
        p_some = w.ps("p_some")
        link, summed, rewritten = w.sem("link"), w.sem("summed"), w.sem("rewritten")
        blk = w.block()

        @blk.vector
        def _(dve):
            nc.vector.memset(unit[:, :, :], 0.0).then_inc(link, 1)
            nc.vector.tensor_tensor(differs[:, :], c.window_count[:, :], c.at_dst[:, :, 3], ALU.not_equal).then_inc(link, 1)
            dve.wait_ge(link, 2)
            nc.vector.tensor_copy(unit[:, 1], c.ident[:, :])
            nc.vector.tensor_reduce(some[:, :], differs[:, :], mybir.AxisListType.X, ALU.max).then_inc(link, 1)
            nc.vector.tensor_copy(c.at_dst[:, :, 2].bitcast(I32), c.slot_of[:, :])
            dve.wait_ge(summed, 1)
            nc.vector.tensor_copy(c.spread[:, :], p_some[0:1, 0:1]).then_inc(link, 1)

        @blk.tensor
        def _(pe):
            pe.wait_ge(link, 3)
            nc.tensor.matmul(p_some[0:1, 0:1], some[:, :], c.ones[:, 0:1], start=True, stop=True).then_inc(summed, 1)

        @blk.sync
        def _(sp):
            sp.wait_ge(link, 4)
            w.settle(sp)
            spread = sp.value_load(c.spread[0:1, 0:1])
            with sp.If(spread != 0):
                with sp.Fori(0, c.tiles) as j:
                    sp.dma_start(c.same_dram[bass.ds(j * P, P), :], unit[:, :, :].rearrange("p w e -> p (w e)")).then_inc(rewritten, 16)
                sp.wait_ge(rewritten, 16 * c.tiles)
                w.settle(sp)


def spread_sums_phase(nc, name, c):
    T = c.tiles
    with Bench(nc, name) as w:
        msg = w.sb("msg", [P, T, P])
        line = w.sb("line", [P, T * P], I32)
        pair = w.sb("pair", [P, P])
        total = w.sb("total", [P, P])
        p_total = w.ps("p_total", (P, P))
        loaded, paired, pair_free, summed, lifted, total_free = (
            w.sem(n) for n in ("loaded", "paired", "pair_free", "summed", "lifted", "total_free"))
        blk = w.block()

        @blk.sync
        def _(sp):
            spread = sp.value_load(c.spread[0:1, 0:1])
            with sp.If(spread != 0):
                sp.dma_start(msg[:, :, :], c.msg[P:P + T * P, :].rearrange("(t p) d -> p t d", p=P)).then_inc(loaded, 16)
                sp.dma_start(line[:, :], c.dst_line[:, P:P + T * P].to_broadcast([P, T * P])).then_inc(loaded, 16)
                sp.wait_ge(loaded, 32)
                w.settle(sp)
                with sp.Fori(0, T) as j:
                    sp.wait_ge(lifted, j + 2)
                    w.settle(sp)
                    sp.dma_start(c.msg[bass.ds(j * P + P, P), :], total[:, :]).then_inc(total_free, 16)
                sp.wait_ge(total_free, 16 * (T + 1))
                w.settle(sp)

        @blk.vector
        def _(dve):
            spread = dve.value_load(c.spread[0:1, 0:1])
            with dve.If(spread != 0):
                dve.sem_inc(pair_free, 1)
                dve.wait_ge(loaded, 32)
                with dve.Fori(0, T) as j:
                    with dve.Fori(0, T) as i:
                        dve.wait_ge(pair_free, j * T + i + 1)
                        w.settle(dve)
                        nc.vector.tensor_scalar(pair[:, :], line[:, bass.ds(j * P, P)], c.dst_value[:, bass.ds(i + 1, 1)],
                                                None, ALU.is_equal).then_inc(paired, 1)

        @blk.tensor
        def _(pe):
            spread = pe.value_load(c.spread[0:1, 0:1])
            with pe.If(spread != 0):
                with pe.Fori(0, T) as j:
                    pe.wait_ge(lifted, j + 1)
                    w.settle(pe)

                    def add(i, start, stop):
                        pe.wait_ge(paired, j * T + i + 1)
                        w.settle(pe)
                        return nc.tensor.matmul(p_total[:, :], pair[:, :], msg[:, bass.ds(i, 1)], start=start, stop=stop)

                    add(0, True, False).then_inc(pair_free, 1)
                    with pe.Fori(1, T - 1) as i:
                        add(i, False, False).then_inc(pair_free, 1)
                    add(T - 1, False, True).then_inc(pair_free, 1)
                    pe.wait_ge(pair_free, j * T + T + 1)
                    w.settle(pe)
                    pe.sem_inc(summed, 1)

        @blk.scalar
        def _(act):
            spread = act.value_load(c.spread[0:1, 0:1])
            with act.If(spread != 0):
                act.sem_inc(lifted, 1)
                act.sem_inc(total_free, 16)
                with act.Fori(0, T) as j:
                    act.wait_ge(summed, j + 1)
                    w.settle(act)
                    act.wait_ge(total_free, j * 16 + 16)
                    w.settle(act)
                    nc.scalar.activation(total[:, :], p_total[:, :], ACT.Copy).then_inc(lifted, 1)


def halves(half):
    return range(TPB) if half is None else range(half * TPB // 2, (half + 1) * TPB // 2)


class NameSlots:
    D = 4

    def __init__(self, w, c):
        self.w, self.c = w, c
        self.index = w.sb("slot_index", [P, self.D, TPB], I32)
        self.row = w.sb("slot_row", [P, self.D, TPB, 4])
        self.copied = w.sem("slot_copied")
        self.done = w.sems("slot_done", self.D)

    def start(self, nc, pool):
        return pool.value_load(self.c.spread[0:1, 0:1])

    def block(self, nc, pool, e, u, r, half, in_turn):
        w, c = self.w, self.c
        if half == 0:
            self.fill(nc, pool, e, u, r)
        for t in halves(half):
            nc.gpsimd.indirect_dma_start(
                out=c.table, out_offset=bass.IndirectOffsetOnAxis(ap=self.index[:, u, t:t + 1], axis=0),
                in_=self.row[:, u, t], in_offset=None, bounds_check=c.table.shape[0] - 1,
                oob_is_err=False).then_inc(self.done[u], 16)
            if in_turn:
                pool.wait_ge(self.done[u], 64 * r + 16 * (t + 1))
                w.settle(pool)

    def fill(self, nc, pool, e, u, r):
        w, c = self.w, self.c
        if reused(e, self.D):
            pool.wait_ge(self.done[u], 64 * r)
            w.settle(pool)
        nc.gpsimd.tensor_copy(self.index[:, u], c.write_at[:, bass.ds(e * TPB, TPB)]).then_inc(self.copied, 1)
        nc.gpsimd.tensor_copy(self.row[:, u].bitcast(I32), c.at_dst[:, bass.ds(e * TPB, TPB), :].bitcast(I32)).then_inc(self.copied, 1)
        pool.wait_ge(self.copied, e * 2 + 2)
        w.settle(pool)

    def end(self, nc, pool, blocks):
        for u in range(self.D):
            pool.wait_ge(self.done[u], 64 * cdiv(blocks - u, self.D))


class LookUpSources:
    D = 4

    def __init__(self, w, c):
        self.w, self.c = w, c
        self.got = w.sb("got", [P, self.D, TPB, 4])
        self.fetch = Fetch(w, "fetch", self.D, c.table, c.src, c.table.shape[0])
        self.taken = w.sem("taken")

    def take(self, nc, pool, e, u, r):
        self.fetch.arrived(pool, u, r)
        self.w.settle(pool)
        nc.gpsimd.tensor_copy(self.c.at_src[:, bass.ds(e * TPB, TPB), :].bitcast(I32), self.got[:, u].bitcast(I32)).then_inc(
            self.taken, 1)

    def start(self, nc, pool):
        return None

    def block(self, nc, pool, e, u, r, half, in_turn):
        if half == 0 and reused(e, self.D):
            self.take(nc, pool, e - self.D, u, r - 1)
            pool.wait_ge(self.taken, e - self.D + 1)
            self.w.settle(pool)
        self.fetch.issue(nc, pool, self.got[:, u], e, u, r, half)

    def end(self, nc, pool, blocks):
        for e in range(max(blocks - self.D, 0), blocks):
            self.take(nc, pool, e, e % self.D, e // self.D)


def columns_phase(nc, c):
    with Bench(nc, "cols") as w:
        t = w.sb("t", [P, c.tiles])
        n = w.sb("n", [P, c.tiles])
        least, some, power, dis = (w.sb(name, [P, 2, c.tiles]) for name in ("least", "some", "power", "dis"))
        link, powered = w.sem("link"), w.sem("powered")
        blk = w.block()

        @blk.gpsimd
        def _(pool):
            pool.wait_ge(link, 1)
            nc.gpsimd.tensor_tensor(power[:, :, :], least[:, :, :], c.minus_half_wide[:, :].unsqueeze(1).to_broadcast(
                [P, 2, c.tiles]), ALU.pow).then_inc(powered, 1)

        @blk.vector
        def _(dve):
            for k, at in enumerate((c.at_dst, c.at_src)):
                nc.vector.tensor_scalar(some[:, k], at[:, :, 0], 1.0, None, ALU.min)
                last = nc.vector.tensor_scalar(least[:, k], at[:, :, 0], 1.0, None, ALU.max)
            last.then_inc(link, 1)
            nc.vector.tensor_tensor(c.slot_weight[:, :], c.at_dst[:, :, 1], c.real[:, :], ALU.mult)
            nc.vector.tensor_tensor(c.b_last[:, :], c.rows["b_neigh"][:, :], c.rows["b_self"][:, :], ALU.add)
            nc.vector.tensor_copy(c.mend_at[:, :], c.at_src[:, :, 2].bitcast(I32))
            dve.wait_ge(powered, 1)
            nc.vector.tensor_tensor(dis[:, :, :], power[:, :, :], some[:, :, :], ALU.mult).then_inc(link, 1)
            dve.wait_ge(link, 2)
            nc.vector.tensor_tensor(t[:, :], dis[:, 0], dis[:, 1], ALU.mult).then_inc(link, 1)
            dve.wait_ge(link, 3)
            nc.vector.tensor_tensor(n[:, :], t[:, :], c.apart[:, :], ALU.mult).then_inc(link, 1)
            dve.wait_ge(link, 4)
            nc.vector.tensor_scalar(c.minus_norm[:, :], n[:, :], -1.0, None, ALU.mult)


def gate_bias_phase(nc, c):
    with Bench(nc, "gbias") as w:
        nodes = w.sb("nodes", [P, 1])
        part = w.sb("part", [P, 1])
        mean = w.sb("mean", [P, 1])
        p_g = w.ps("p_g")
        link, multiplied = w.sem("link"), w.sem("multiplied")
        blk = w.block()

        @blk.vector
        def _(dve):
            nc.vector.tensor_tensor(nodes[:, :], c.total_nodes[:, 0:1], c.total_nodes[:, 1:2], ALU.add).then_inc(link, 1)
            dve.wait_ge(link, 1)
            nc.vector.tensor_tensor(part[:, :], nodes[:, :], c.total_slots[:, :], ALU.add).then_inc(link, 1)
            dve.wait_ge(link, 2)
            nc.vector.tensor_scalar(mean[:, :], part[:, :], 1.0 / c.nodes, None, ALU.mult).then_inc(link, 1)
            dve.wait_ge(multiplied, 1)
            nc.vector.tensor_tensor(c.g_sum[:, :], p_g[:, 0:3], c.g_ih[:, :], ALU.add).then_inc(link, 1)
            dve.wait_ge(link, 4)
            nc.vector.tensor_tensor(c.g_all[:, :], c.g_sum[:, :], c.g_hh[:, :], ALU.add)

        @blk.tensor
        def _(pe):
            pe.wait_ge(link, 3)
            for g in range(3):
                last = nc.tensor.matmul(p_g[:, g:g + 1], c.w_ih[:, g * P:(g + 1) * P], mean[:, :], start=True, stop=True)
            last.then_inc(multiplied, 1)


def build(nc, args, out):
    c = Common()
    x = args["x"]
    c.nodes = x.shape[0]
    c.tiles = args["src_columns"].shape[1]
    c.edge_blocks = c.tiles // TPB
    c.node_blocks = cdiv(c.nodes, BLK)
    slots = c.tiles * P
    tail = (c.nodes - (c.node_blocks - 1) * BLK) // TPB
    assert c.nodes % TPB == 0 and c.node_blocks <= P and c.nodes + slots <= P * BLK
    tail = None if tail == P else tail

    def dram(name, shape, dt=F32):
        return nc.dram_tensor(name, list(shape), dt, kind="Internal").ap()

    edge_rows, node_rows = [slots, P], [c.node_blocks * BLK, P]
    s_x0, s_h1, s_x1, s_x2, s_x3 = (dram(f"s_{n}", edge_rows) for n in ("x0", "h1", "x1", "x2", "x3"))
    d_x0, d_h1, d_x1, d_x2, d_x3 = (dram(f"d_{n}", edge_rows) for n in ("x0", "h1", "x1", "x2", "x3"))
    n_x1, n_x2 = (dram(f"n_{n}", node_rows) for n in ("x1", "x2"))
    c.msg = dram("msg", [slots + 2 * P, P])
    c.same_dram = dram("same_dram", [slots, 3 * P])
    c.table = dram("table", [P * BLK, 4])
    c.weight_dram = dram("weight_dram", [P * BLK])
    c.relation_row = args["relation_line"]
    c.dst_line = args["dst_line"]

    with ExitStack() as ctx:
        def sb(name, shape, dt=F32):
            return ctx.enter_context(nc.sbuf_tensor(name, shape, dt))

        T = c.tiles
        c.weights = {name: sb(f"w_{name}", [P, cols]) for name, cols in WEIGHTS}
        c.rows = {name: sb(f"r_{name}", [P, P]) for name in ROWS}
        c.w_ih, c.w_hh, c.w_rel, c.w_film = (c.weights[n] for n in ("w_ih", "w_hh", "w_rel", "w_film"))
        c.gamma, c.beta, c.b_msg = (c.rows[n][:, :] for n in ("gamma", "beta", "b_msg"))
        c.g_ih, c.g_hh, c.g_sum, c.g_all = (sb(n, [P, 3]) for n in ("g_ih", "g_hh", "g_sum", "g_all"))
        c.b_r, c.b_z, c.b_n, c.b_hn = c.g_all[:, 0:1], c.g_all[:, 1:2], c.g_sum[:, 2:3], c.g_hh[:, 2:3]
        c.b_last = sb("b_last", [P, P])
        c.first_row, c.b1_col = sb("first_row", [P, P]), sb("b1_col", [P, 1])
        c.ident, c.earlier_t = sb("ident", [P, P]), sb("earlier", [P, P])
        c.earlier = c.earlier_t[:, :]
        c.minus_half, c.minus_half_wide = sb("minus_half", [P, TPB]), sb("minus_half_wide", [P, T])
        c.count_row = sb("count_row", [P, BLK], F16)
        c.dst_value, c.window_count = sb("dst_value", [P, T + 2]), sb("window_count", [P, T])
        c.ones, c.spread = sb("ones", [P, 1]), sb("spread", [1, 1], I32)
        c.node_of = sb("node_of", [P, BLK], I32)
        c.slot_of, c.src = sb("slot_of", [P, T], I32), sb("src_t", [P, T], I32)
        c.dst = sb("dst_t", [P, T + 2], I32)
        c.src_row, c.dst_row, c.write_at, c.mend_at = (sb(n, [P, T], I32) for n in ("src_row", "dst_row", "write_at", "mend_at"))
        c.apart, c.real, c.minus_norm, c.slot_weight = (sb(n, [P, T]) for n in ("apart", "real", "minus_norm", "slot_weight"))
        c.at_dst, c.at_src = sb("at_dst", [P, T, 4]), sb("at_src", [P, T, 4])
        c.node_weight = sb("node_weight", [P, c.node_blocks * TPB])
        c.total_nodes, c.total_slots = sb("total_nodes", [P, 2]), sb("total_slots", [P, 1])
        W = {n: t[:, :] for n, t in c.weights.items()}
        L = {n: t[:, :] for n, t in c.rows.items()}
        dst_cols = c.dst[:, 1:T + 1]
        E, N = c.edge_blocks, c.node_blocks

        constants_phase(nc, c, args)
        degree_phase(nc, c, x, s_x0)
        same_phase(nc, c, args["dst_line"], dst_cols)
        scatter_check_phase(nc, c)
        half = cdiv(N, 2)
        first_nodes_stage(nc, "n0", c, 0, half, x, n_x1, c.total_nodes[:, 0:1], None, NameSlots)
        first_nodes_stage(nc, "m0", c, half, N - half, x, n_x1, c.total_nodes[:, 1:2], tail, LookUpSources)
        columns_phase(nc, c)

        row_stage(nc, "s0a", c, E, True, s_x0, s_h1, update=W["W1_0"], bias=L["b1"], relu=True,
                  message=W["W1_1"], message_scale=c.minus_norm, message_out=c.msg)
        spread_sums_phase(nc, "sum1", c)
        row_stage(nc, "d0a", c, E, True, x, d_h1, gather=c.dst_row, keep=d_x0, update=W["W1_0"], bias=L["b1"], relu=True,
                  sums=c.msg)
        row_stage(nc, "s0b", c, E, True, s_h1, s_x1, mend=(d_h1, c.mend_at), norm=False, extra=s_x0, update=W["W2_0"],
                  bias=L["b2"], relu=True, message=W["W2_1"], message_scale=c.minus_norm, message_out=c.msg)
        spread_sums_phase(nc, "sum2", c)
        row_stage(nc, "d0b", c, E, True, d_h1, d_x1, norm=False, extra=d_x0, update=W["W2_0"], bias=L["b2"], relu=True,
                  sums=c.msg, mean=(c.slot_weight, c.total_slots[:, :]))
        gate_bias_phase(nc, c)
        gru_stage(nc, "s1", c, E, True, s_x1, s_x2, mend=(d_x1, c.mend_at), message=W["W_msg"], message_out=c.msg)
        spread_sums_phase(nc, "sum3", c)
        gru_stage(nc, "d1", c, E, True, d_x1, d_x2, sums=c.msg)
        gru_stage(nc, "n1", c, N, False, n_x1, n_x2)

        film_stage(nc, "f2", c, E, s_x2, (d_x2, c.mend_at), d_x2, c.msg, s_x3)
        spread_sums_phase(nc, "sum4", c)
        row_stage(nc, "d2", c, E, True, d_x2, d_x3, update=W["loop_w"], bias=L["h_bias"], sums=c.msg)

        row_stage(nc, "s3", c, E, True, s_x3, None, mend=(d_x3, c.mend_at), message=W["W_neigh"], message_out=c.msg)
        spread_sums_phase(nc, "sum5", c)
        last_nodes_stage(nc, "n2", c, N, n_x2, out, ((W["loop_w"], L["h_bias"]), (W["W_self"], c.b_last[:, :])), tail)
        row_stage(nc, "d3", c, E, True, d_x3, out, update=W["W_self"], bias=c.b_last[:, :], sums=c.msg, scatter=c.write_at)


def kernel(**inputs):
    import numpy as np
    import concourse.bacc as bacc
    from concourse import mybir as mb
    from concourse.bass_utils import run_bass_kernel_spmd

    a = {k: np.ascontiguousarray(v) for k, v in inputs.items()}
    nodes, edges = a["x"].shape[0], a["src"].shape[0]
    pad = cdiv(edges, BLK) * BLK - edges
    spare = np.arange(nodes, nodes + pad, dtype=np.int32)
    src = np.concatenate([a["src"], spare])
    dst = np.concatenate([a["dst"], spare])
    rel = np.concatenate([a["edge_type_4"], np.zeros(pad, np.int32)])
    C = np.ascontiguousarray
    arrays = {
        "x": a["x"],
        "src_columns": C(src.reshape(-1, P).T), "dst_columns": C(dst.reshape(-1, P).T),
        "dst_line": C(np.concatenate([np.full(P, -1, np.int32), dst]).reshape(1, -1)), "relation_line": C(rel.reshape(1, -1)),
        "W1_0": a["L0_gnn_W1_0"], "W1_1": a["L0_gnn_W1_1"], "W2_0": a["L0_gnn_W2_0"], "W2_1": a["L0_gnn_W2_1"],
        "b1": a["L0_gnn_b1"], "b2": a["L0_gnn_b2"],
        "W_msg": C(a["L1_gnn_W_msg"].T), "w_ih": C(a["L1_gnn_w_ih"].T), "w_hh": C(a["L1_gnn_w_hh"].T),
        "b_msg": a["L1_gnn_b_msg"], "b_ih": a["L1_gnn_b_ih"], "b_hh": a["L1_gnn_b_hh"],
        "gamma": a["L1_gnn_ln_gamma"], "beta": a["L1_gnn_ln_beta"],
        "w_rel": C(a["L2_gnn_W_rel"].transpose(1, 0, 2).reshape(P, -1)),
        "w_film": C(a["L2_gnn_film_rel"].transpose(1, 0, 2).reshape(P, -1)),
        "h_bias": a["L2_gnn_h_bias"], "loop_w": a["L2_gnn_loop_w"],
        "W_neigh": C(a["L3_gnn_W_neigh"].T), "W_self": C(a["L3_gnn_W_self"].T),
        "b_neigh": a["L3_gnn_b_neigh"], "b_self": a["L3_gnn_b_self"],
    }
    nc = bacc.Bacc("TRN2", target_bir_lowering=False, num_devices=1)
    args = {k: nc.dram_tensor(f"in_{k}", v.shape, mb.dt.from_np(v.dtype), kind="ExternalInput").ap() for k, v in arrays.items()}
    out = nc.dram_tensor("out", (nodes, P), mb.dt.float32, kind="ExternalOutput").ap()
    build(nc, args, out)
    r = run_bass_kernel_spmd(nc, [{f"in_{k}": v for k, v in arrays.items()}], core_ids=[0])
    return r.results[0]["out"]
```
